# Optimizing a Trainium2 kernel written in Bass

```python
import numpy as np
import jax
import jax.numpy as jnp

def _softmax(x, axis=-1):
    return jax.nn.softmax(x, axis=axis)

def _gelu(x):
    return jax.nn.gelu(x, approximate=True)

def _silu(x):
    return jax.nn.silu(x)

def _sigmoid(x):
    return jax.nn.sigmoid(x)

def _layernorm(x, axis=-1, eps=1e-05):
    m = jnp.mean(x, axis=axis, keepdims=True)
    v = jnp.var(x, axis=axis, keepdims=True)
    return (x - m) / jnp.sqrt(v + eps)

def _scatter_add(tgt, idx, src, axis=0):
    return tgt.at[idx].add(src)

def _segment_sum(src, seg, n):
    return jax.ops.segment_sum(src, seg, n)
kernel_name = 'mk_adaln_d2_jaxref_r8_474e20'

def setup_inputs(seed: int=0):
    np.random.seed(seed)
    _w = jnp.asarray

    def _L0_attn_setup():
        import math
        import jax, jax.numpy as jnp
        import numpy as np
        B, S, HID = (2, 128, 256)
        H, D, R = (16, 128, 64)
        KVC, QC = (64, 192)
        MAX_POS = 512

        def _lin(x, w, b):
            return x @ w.T + b

        def _rotate_half(x):
            x1, x2 = (x[..., :x.shape[-1] // 2], x[..., x.shape[-1] // 2:])
            return jnp.concatenate([-x2, x1], axis=-1)

        def _rope_tables(dim, end, theta=10000.0):
            freqs = 1.0 / theta ** (jnp.arange(0, dim, 2)[:dim // 2].astype(jnp.float32) / dim)
            f = jnp.outer(jnp.arange(end, dtype=jnp.float32), freqs)
            cos, sin = (jnp.cos(f), jnp.sin(f))
            return (jnp.concatenate([cos, cos], -1), jnp.concatenate([sin, sin], -1))

        def _reference_tuple_inner(hidden_states, W_DKV_w, W_DKV_b, W_UK_w, W_UK_b, W_UV_w, W_UV_b, W_KR_w, W_KR_b, W_DQ_w, W_DQ_b, W_UQ_w, W_UQ_b, W_QR_w, W_QR_b, W_O_w, W_O_b):
            b, s = hidden_states.shape[:2]
            c_kv = _lin(hidden_states, W_DKV_w, W_DKV_b)
            k = _lin(c_kv, W_UK_w, W_UK_b).reshape(b, s, H, D)
            v = _lin(c_kv, W_UV_w, W_UV_b).reshape(b, s, H, D)
            c_q = _lin(hidden_states, W_DQ_w, W_DQ_b)
            q = _lin(c_q, W_UQ_w, W_UQ_b).reshape(b, s, H, D)
            k_r = _lin(k, W_KR_w, W_KR_b)
            q_r = _lin(q, W_QR_w, W_QR_b)
            cos, sin = _rope_tables(R, MAX_POS)
            cos_p = cos[:s][:, None, :]
            sin_p = sin[:s][:, None, :]
            q_r = q_r * cos_p + _rotate_half(q_r) * sin_p
            k_r = k_r * cos_p + _rotate_half(k_r) * sin_p
            scale = 1.0 / math.sqrt(D)
            scores = jnp.einsum('bqhd,bkhd->bhqk', q, k) * scale
            probs = jax.nn.softmax(scores, axis=-1)
            attn = jnp.einsum('bhqk,bkhd->bqhd', probs, v).reshape(b, s, H * D)
            output = _lin(attn, W_O_w, W_O_b)
            return (output, c_kv, k_r)
        key = jax.random.key(seed)
        ks = jax.random.split(key, 17)
        w = lambda k, shape: jax.random.normal(k, shape, jnp.float32) * 0.02
        return {'hidden_states': jax.random.normal(ks[0], (B, S, HID), jnp.float32), 'W_DKV_w': w(ks[1], (KVC, HID)), 'W_DKV_b': w(ks[2], (KVC,)), 'W_UK_w': w(ks[3], (H * D, KVC)), 'W_UK_b': w(ks[4], (H * D,)), 'W_UV_w': w(ks[5], (H * D, KVC)), 'W_UV_b': w(ks[6], (H * D,)), 'W_KR_w': w(ks[7], (R, D)), 'W_KR_b': w(ks[8], (R,)), 'W_DQ_w': w(ks[9], (QC, HID)), 'W_DQ_b': w(ks[10], (QC,)), 'W_UQ_w': w(ks[11], (H * D, QC)), 'W_UQ_b': w(ks[12], (H * D,)), 'W_QR_w': w(ks[13], (R, D)), 'W_QR_b': w(ks[14], (R,)), 'W_O_w': w(ks[15], (HID, H * D)), 'W_O_b': w(ks[16], (HID,))}
    _L0_attn_in = _L0_attn_setup()

    def _L0_ffn_setup():
        import jax, jax.numpy as jnp
        import numpy as np
        B, S, H, F, E, K = (2, 128, 256, 688, 8, 2)
        key = jax.random.key(seed)
        k0, k1, k2, k3, k4 = jax.random.split(key, 5)
        x = jax.random.normal(k0, (B, S, H), dtype=jnp.float32)
        router_w = jax.random.normal(k1, (E, H), dtype=jnp.float32) * 0.02
        gate_w = jax.random.normal(k2, (E, F, H), dtype=jnp.float32) * 0.02
        up_w = jax.random.normal(k3, (E, F, H), dtype=jnp.float32) * 0.02
        down_w = jax.random.normal(k4, (E, H, F), dtype=jnp.float32) * 0.02
        return {'x': x, 'router_w': router_w, 'gate_w': gate_w, 'up_w': up_w, 'down_w': down_w}
    _L0_ffn_in = _L0_ffn_setup()
    _L0_c = _w((lambda *s: np.random.randn(*s).astype(np.float32) * 0.05)(8, 256))
    _L0_wmod = _w((lambda *s: np.random.randn(*s).astype(np.float32) * 0.05)(256, 6 * 256) * 256 ** (-0.5))

    def _L1_attn_setup():
        import jax, jax.numpy as jnp
        import numpy as np
        B, S, D = (2, 512, 256)
        H = 16
        DC = 64
        DKQV = 256
        DR = 128
        DCKV = 64
        DOUT = 256
        DH = DKQV // H
        DRH = DR // H
        SCALER = 1.0 / float(np.sqrt(DH + DRH))

        def _rope(x):
            dr = x.shape[-1]
            inv_freq = 1.0 / 10000.0 ** (jnp.arange(0, dr, 2, dtype=jnp.float32) / dr)
            t = jnp.arange(x.shape[1], dtype=jnp.float32)
            freqs = t[:, None] * inv_freq[None, :]
            emb = jnp.concatenate([freqs, freqs], axis=-1)[None, :, None, :]
            x1, x2 = jnp.split(x, 2, axis=-1)
            rot = jnp.concatenate([-x2, x1], axis=-1)
            return x * jnp.cos(emb) + rot * jnp.sin(emb)
        key = jax.random.key(seed)
        ks = jax.random.split(key, 20)

        def lin(k, din, dout):
            s = 1.0 / np.sqrt(din)
            kw, kb = jax.random.split(k)
            W = jax.random.uniform(kw, (din, dout), jnp.float32, -s, s)
            b = jax.random.uniform(kb, (dout,), jnp.float32, -s, s)
            return (W, b)
        h_t = jax.random.normal(ks[0], (B, S, D), jnp.float32)
        Wc, bc = lin(ks[1], D, DC)
        Wcq, bcq = lin(ks[2], DC, DKQV)
        Wqr, bqr = lin(ks[3], DC, DR)
        Wckv, bckv = lin(ks[4], D, DCKV)
        Wck, bck = lin(ks[5], DCKV, DKQV)
        Wkr, bkr = lin(ks[6], D, DR)
        Wv, bv = lin(ks[7], DCKV, DKQV)
        Wo, bo = lin(ks[8], DKQV, DOUT)
        return dict(h_t=h_t, Wc=Wc, bc=bc, Wcq=Wcq, bcq=bcq, Wqr=Wqr, bqr=bqr, Wckv=Wckv, bckv=bckv, Wck=Wck, bck=bck, Wkr=Wkr, bkr=bkr, Wv=Wv, bv=bv, Wo=Wo, bo=bo)
    _L1_attn_in = _L1_attn_setup()

    def _L1_ffn_setup():
        import jax, jax.numpy as jnp
        import numpy as np
        from jax import lax
        E = 8
        K = 2
        H = 256
        I = 512
        B, S = (2, 256)
        SCALE = 0.02

        def _silu_and_mul(gu):
            g, u = jnp.split(gu, 2, axis=-1)
            return jax.nn.silu(g) * u
        key = jax.random.key(seed)
        ks = jax.random.split(key, 6)
        return {'hidden_states': jax.random.normal(ks[0], (B, S, H), dtype=jnp.float32), 'gate_w': jax.random.normal(ks[1], (H, E), dtype=jnp.float32) * SCALE, 'w_gate_up': jax.random.normal(ks[2], (E, H, 2 * I), dtype=jnp.float32) * SCALE, 'w_down': jax.random.normal(ks[3], (E, I, H), dtype=jnp.float32) * SCALE, 'shared_gate_up': jax.random.normal(ks[4], (H, 2 * I), dtype=jnp.float32) * SCALE, 'shared_down': jax.random.normal(ks[5], (I, H), dtype=jnp.float32) * SCALE}
    _L1_ffn_in = _L1_ffn_setup()
    _L1_c = _w((lambda *s: np.random.randn(*s).astype(np.float32) * 0.05)(8, 256))
    _L1_wmod = _w((lambda *s: np.random.randn(*s).astype(np.float32) * 0.05)(256, 6 * 256) * 256 ** (-0.5))
    _d = {'L0_attn_hidden_states': _L0_attn_in['hidden_states'], 'L0_attn_W_DKV_w': _L0_attn_in['W_DKV_w'], 'L0_attn_W_DKV_b': _L0_attn_in['W_DKV_b'], 'L0_attn_W_UK_w': _L0_attn_in['W_UK_w'], 'L0_attn_W_UK_b': _L0_attn_in['W_UK_b'], 'L0_attn_W_UV_w': _L0_attn_in['W_UV_w'], 'L0_attn_W_UV_b': _L0_attn_in['W_UV_b'], 'L0_attn_W_KR_w': _L0_attn_in['W_KR_w'], 'L0_attn_W_KR_b': _L0_attn_in['W_KR_b'], 'L0_attn_W_DQ_w': _L0_attn_in['W_DQ_w'], 'L0_attn_W_DQ_b': _L0_attn_in['W_DQ_b'], 'L0_attn_W_UQ_w': _L0_attn_in['W_UQ_w'], 'L0_attn_W_UQ_b': _L0_attn_in['W_UQ_b'], 'L0_attn_W_QR_w': _L0_attn_in['W_QR_w'], 'L0_attn_W_QR_b': _L0_attn_in['W_QR_b'], 'L0_attn_W_O_w': _L0_attn_in['W_O_w'], 'L0_attn_W_O_b': _L0_attn_in['W_O_b'], 'L0_ffn_router_w': _L0_ffn_in['router_w'], 'L0_ffn_gate_w': _L0_ffn_in['gate_w'], 'L0_ffn_up_w': _L0_ffn_in['up_w'], 'L0_ffn_down_w': _L0_ffn_in['down_w'], 'L0_c': _L0_c, 'L0_wmod': _L0_wmod, 'L1_attn_Wc': _L1_attn_in['Wc'], 'L1_attn_bc': _L1_attn_in['bc'], 'L1_attn_Wcq': _L1_attn_in['Wcq'], 'L1_attn_bcq': _L1_attn_in['bcq'], 'L1_attn_Wqr': _L1_attn_in['Wqr'], 'L1_attn_bqr': _L1_attn_in['bqr'], 'L1_attn_Wckv': _L1_attn_in['Wckv'], 'L1_attn_bckv': _L1_attn_in['bckv'], 'L1_attn_Wck': _L1_attn_in['Wck'], 'L1_attn_bck': _L1_attn_in['bck'], 'L1_attn_Wkr': _L1_attn_in['Wkr'], 'L1_attn_bkr': _L1_attn_in['bkr'], 'L1_attn_Wv': _L1_attn_in['Wv'], 'L1_attn_bv': _L1_attn_in['bv'], 'L1_attn_Wo': _L1_attn_in['Wo'], 'L1_attn_bo': _L1_attn_in['bo'], 'L1_ffn_gate_w': _L1_ffn_in['gate_w'], 'L1_ffn_w_gate_up': _L1_ffn_in['w_gate_up'], 'L1_ffn_w_down': _L1_ffn_in['w_down'], 'L1_ffn_shared_gate_up': _L1_ffn_in['shared_gate_up'], 'L1_ffn_shared_down': _L1_ffn_in['shared_down'], 'L1_c': _L1_c, 'L1_wmod': _L1_wmod}
    _x0 = _d['L0_attn_hidden_states']
    _d['L0_attn_hidden_states'] = jax.random.normal(jax.random.fold_in(jax.random.key(seed), 1), (8, 256, 256), dtype=_x0.dtype)
    del _x0
    return _d

def reference(L0_attn_hidden_states, L0_attn_W_DKV_w, L0_attn_W_DKV_b, L0_attn_W_UK_w, L0_attn_W_UK_b, L0_attn_W_UV_w, L0_attn_W_UV_b, L0_attn_W_KR_w, L0_attn_W_KR_b, L0_attn_W_DQ_w, L0_attn_W_DQ_b, L0_attn_W_UQ_w, L0_attn_W_UQ_b, L0_attn_W_QR_w, L0_attn_W_QR_b, L0_attn_W_O_w, L0_attn_W_O_b, L0_ffn_router_w, L0_ffn_gate_w, L0_ffn_up_w, L0_ffn_down_w, L0_c, L0_wmod, L1_attn_Wc, L1_attn_bc, L1_attn_Wcq, L1_attn_bcq, L1_attn_Wqr, L1_attn_bqr, L1_attn_Wckv, L1_attn_bckv, L1_attn_Wck, L1_attn_bck, L1_attn_Wkr, L1_attn_bkr, L1_attn_Wv, L1_attn_bv, L1_attn_Wo, L1_attn_bo, L1_ffn_gate_w, L1_ffn_w_gate_up, L1_ffn_w_down, L1_ffn_shared_gate_up, L1_ffn_shared_down, L1_c, L1_wmod):

    def _L0_attn_ref(hidden_states, W_DKV_w, W_DKV_b, W_UK_w, W_UK_b, W_UV_w, W_UV_b, W_KR_w, W_KR_b, W_DQ_w, W_DQ_b, W_UQ_w, W_UQ_b, W_QR_w, W_QR_b, W_O_w, W_O_b):
        import math
        import jax, jax.numpy as jnp
        import numpy as np
        B, S, HID = (2, 128, 256)
        H, D, R = (16, 128, 64)
        KVC, QC = (64, 192)
        MAX_POS = 512

        def _lin(x, w, b):
            return x @ w.T + b

        def _rotate_half(x):
            x1, x2 = (x[..., :x.shape[-1] // 2], x[..., x.shape[-1] // 2:])
            return jnp.concatenate([-x2, x1], axis=-1)

        def _rope_tables(dim, end, theta=10000.0):
            freqs = 1.0 / theta ** (jnp.arange(0, dim, 2)[:dim // 2].astype(jnp.float32) / dim)
            f = jnp.outer(jnp.arange(end, dtype=jnp.float32), freqs)
            cos, sin = (jnp.cos(f), jnp.sin(f))
            return (jnp.concatenate([cos, cos], -1), jnp.concatenate([sin, sin], -1))

        def _reference_tuple_inner(hidden_states, W_DKV_w, W_DKV_b, W_UK_w, W_UK_b, W_UV_w, W_UV_b, W_KR_w, W_KR_b, W_DQ_w, W_DQ_b, W_UQ_w, W_UQ_b, W_QR_w, W_QR_b, W_O_w, W_O_b):
            b, s = hidden_states.shape[:2]
            c_kv = _lin(hidden_states, W_DKV_w, W_DKV_b)
            k = _lin(c_kv, W_UK_w, W_UK_b).reshape(b, s, H, D)
            v = _lin(c_kv, W_UV_w, W_UV_b).reshape(b, s, H, D)
            c_q = _lin(hidden_states, W_DQ_w, W_DQ_b)
            q = _lin(c_q, W_UQ_w, W_UQ_b).reshape(b, s, H, D)
            k_r = _lin(k, W_KR_w, W_KR_b)
            q_r = _lin(q, W_QR_w, W_QR_b)
            cos, sin = _rope_tables(R, MAX_POS)
            cos_p = cos[:s][:, None, :]
            sin_p = sin[:s][:, None, :]
            q_r = q_r * cos_p + _rotate_half(q_r) * sin_p
            k_r = k_r * cos_p + _rotate_half(k_r) * sin_p
            scale = 1.0 / math.sqrt(D)
            scores = jnp.einsum('bqhd,bkhd->bhqk', q, k) * scale
            probs = jax.nn.softmax(scores, axis=-1)
            attn = jnp.einsum('bhqk,bkhd->bqhd', probs, v).reshape(b, s, H * D)
            output = _lin(attn, W_O_w, W_O_b)
            return (output, c_kv, k_r)
        return _reference_tuple_inner(hidden_states, W_DKV_w, W_DKV_b, W_UK_w, W_UK_b, W_UV_w, W_UV_b, W_KR_w, W_KR_b, W_DQ_w, W_DQ_b, W_UQ_w, W_UQ_b, W_QR_w, W_QR_b, W_O_w, W_O_b)[0]

    def _L0_ffn_ref(x, router_w, gate_w, up_w, down_w):
        import jax, jax.numpy as jnp
        import numpy as np
        B, S, H, F, E, K = (2, 128, 256, 688, 8, 2)
        b, s, h = x.shape
        xf = x.reshape(-1, h)
        logits = xf @ router_w.T
        top_v, top_i = jax.lax.top_k(logits, K)
        probs = jax.nn.softmax(top_v.astype(jnp.float32), axis=-1).astype(logits.dtype)
        combine = jnp.sum(jax.nn.one_hot(top_i, E, dtype=x.dtype) * probs[..., None], axis=1)
        g = jnp.einsum('th,efh->etf', xf, gate_w)
        u = jnp.einsum('th,efh->etf', xf, up_w)
        y = jnp.einsum('etf,ehf->eth', jax.nn.silu(g) * u, down_w)
        out = jnp.einsum('te,eth->th', combine, y)
        return out.reshape(b, s, h)

    def _L1_attn_ref(h_t, Wc, bc, Wcq, bcq, Wqr, bqr, Wckv, bckv, Wck, bck, Wkr, bkr, Wv, bv, Wo, bo):
        import jax, jax.numpy as jnp
        import numpy as np
        B, S, D = (2, 512, 256)
        H = 16
        DC = 64
        DKQV = 256
        DR = 128
        DCKV = 64
        DOUT = 256
        DH = DKQV // H
        DRH = DR // H
        SCALER = 1.0 / float(np.sqrt(DH + DRH))

        def _rope(x):
            dr = x.shape[-1]
            inv_freq = 1.0 / 10000.0 ** (jnp.arange(0, dr, 2, dtype=jnp.float32) / dr)
            t = jnp.arange(x.shape[1], dtype=jnp.float32)
            freqs = t[:, None] * inv_freq[None, :]
            emb = jnp.concatenate([freqs, freqs], axis=-1)[None, :, None, :]
            x1, x2 = jnp.split(x, 2, axis=-1)
            rot = jnp.concatenate([-x2, x1], axis=-1)
            return x * jnp.cos(emb) + rot * jnp.sin(emb)
        b, s = (h_t.shape[0], h_t.shape[1])
        cq = h_t @ Wc + bc
        q = (cq @ Wcq + bcq).reshape(b, s, H, DH)
        qr = _rope((cq @ Wqr + bqr).reshape(b, s, H, DRH))
        q = jnp.concatenate([q, qr], axis=-1)
        ckv = h_t @ Wckv + bckv
        k = (ckv @ Wck + bck).reshape(b, s, H, DH)
        kr = _rope((h_t @ Wkr + bkr).reshape(b, s, H, DRH))
        k = jnp.concatenate([k, kr], axis=-1)
        v = (ckv @ Wv + bv).reshape(b, s, H, DH)
        scores = jnp.einsum('bsid,bsjd->bsij', q, k) * SCALER
        attn = jax.nn.softmax(scores, axis=-1)
        out = jnp.einsum('bsij,bsjd->bsid', attn, v).reshape(b, s, DKQV)
        return out @ Wo + bo

    def _L1_ffn_ref(hidden_states, gate_w, w_gate_up, w_down, shared_gate_up, shared_down):
        import jax, jax.numpy as jnp
        import numpy as np
        from jax import lax
        E = 8
        K = 2
        H = 256
        I = 512
        B, S = (2, 256)
        SCALE = 0.02

        def _silu_and_mul(gu):
            g, u = jnp.split(gu, 2, axis=-1)
            return jax.nn.silu(g) * u
        orig_shape = hidden_states.shape
        x = hidden_states.reshape(-1, orig_shape[-1])
        shared_out = _silu_and_mul(x @ shared_gate_up) @ shared_down
        router_logits = x @ gate_w
        probs = jax.nn.softmax(router_logits, axis=-1)
        topk_w, topk_i = lax.top_k(probs, K)
        topk_w = topk_w / jnp.sum(topk_w, axis=-1, keepdims=True)
        combine = jnp.sum(jax.nn.one_hot(topk_i, E, dtype=x.dtype) * topk_w[..., None], axis=1)

        def body(acc, we):
            wg, wd, cw = we
            h = _silu_and_mul(x @ wg) @ wd
            return (acc + cw[:, None] * h, None)
        moe_out, _ = lax.scan(body, jnp.zeros_like(x), (w_gate_up, w_down, combine.T))
        return (moe_out + shared_out).reshape(orig_shape)
    x = L0_attn_hidden_states
    mod = (_silu(L0_c) @ L0_wmod).reshape(L0_c.shape[0], 6, 1, -1)
    sa, ca, ga, sb, cb, gb = (mod[:, 0], mod[:, 1], mod[:, 2], mod[:, 3], mod[:, 4], mod[:, 5])
    ga = (2 * (ga >= 0) - 1) * jnp.maximum(jnp.abs(ga), 0.25)
    gb = (2 * (gb >= 0) - 1) * jnp.maximum(jnp.abs(gb), 0.25)
    h = _layernorm(x, axis=-1) * (1 + ca) + sa
    x = x + ga * _L0_attn_ref(h, L0_attn_W_DKV_w, L0_attn_W_DKV_b, L0_attn_W_UK_w, L0_attn_W_UK_b, L0_attn_W_UV_w, L0_attn_W_UV_b, L0_attn_W_KR_w, L0_attn_W_KR_b, L0_attn_W_DQ_w, L0_attn_W_DQ_b, L0_attn_W_UQ_w, L0_attn_W_UQ_b, L0_attn_W_QR_w, L0_attn_W_QR_b, L0_attn_W_O_w, L0_attn_W_O_b)
    h = _layernorm(x, axis=-1) * (1 + cb) + sb
    x = x + gb * _L0_ffn_ref(h, L0_ffn_router_w, L0_ffn_gate_w, L0_ffn_up_w, L0_ffn_down_w)
    mod = (_silu(L1_c) @ L1_wmod).reshape(L1_c.shape[0], 6, 1, -1)
    sa, ca, ga, sb, cb, gb = (mod[:, 0], mod[:, 1], mod[:, 2], mod[:, 3], mod[:, 4], mod[:, 5])
    ga = (2 * (ga >= 0) - 1) * jnp.maximum(jnp.abs(ga), 0.25)
    gb = (2 * (gb >= 0) - 1) * jnp.maximum(jnp.abs(gb), 0.25)
    h = _layernorm(x, axis=-1) * (1 + ca) + sa
    x = x + ga * _L1_attn_ref(h, L1_attn_Wc, L1_attn_bc, L1_attn_Wcq, L1_attn_bcq, L1_attn_Wqr, L1_attn_bqr, L1_attn_Wckv, L1_attn_bckv, L1_attn_Wck, L1_attn_bck, L1_attn_Wkr, L1_attn_bkr, L1_attn_Wv, L1_attn_bv, L1_attn_Wo, L1_attn_bo)
    h = _layernorm(x, axis=-1) * (1 + cb) + sb
    x = x + gb * _L1_ffn_ref(h, L1_ffn_gate_w, L1_ffn_w_gate_up, L1_ffn_w_down, L1_ffn_shared_gate_up, L1_ffn_shared_down)
    return x

_drawn_inputs = setup_inputs


def setup_inputs(seed=0):
    import zlib

    import numpy as np

    out = dict(_drawn_inputs(seed))
    spreads = {}
    factors = {'L0_attn_W_DKV_w': 8.0,
     'L0_attn_W_DKV_b': 8.0,
     'L0_attn_W_UK_w': 8.0,
     'L0_attn_W_UK_b': 64.0,
     'L0_attn_W_UV_w': 8.0,
     'L0_attn_W_UV_b': 8.0,
     'L0_attn_W_DQ_w': 8.0,
     'L0_attn_W_DQ_b': 8.0,
     'L0_attn_W_UQ_w': 8.0,
     'L0_attn_W_UQ_b': 8.0,
     'L0_attn_W_O_w': 8.0,
     'L0_attn_W_O_b': 8.0,
     'L0_ffn_router_w': 8.0,
     'L0_ffn_gate_w': 8.0,
     'L0_ffn_up_w': 8.0,
     'L0_ffn_down_w': 8.0,
     'L0_c': 6.56,
     'L0_wmod': 6.571,
     'L1_attn_Wc': 8.0,
     'L1_attn_bc': 8.0,
     'L1_attn_Wcq': 8.0,
     'L1_attn_bcq': 8.0,
     'L1_attn_Wqr': 8.0,
     'L1_attn_bqr': 8.0,
     'L1_attn_Wckv': 4.513,
     'L1_attn_bckv': 8.0,
     'L1_attn_Wck': 8.0,
     'L1_attn_bck': 8.0,
     'L1_attn_Wkr': 8.0,
     'L1_attn_bkr': 8.0,
     'L1_attn_Wv': 4.702,
     'L1_attn_bv': 8.0,
     'L1_attn_Wo': 4.387,
     'L1_attn_bo': 23.079,
     'L1_ffn_gate_w': 8.0,
     'L1_ffn_w_gate_up': 8.0,
     'L1_ffn_w_down': 8.0,
     'L1_ffn_shared_gate_up': 8.0,
     'L1_ffn_shared_down': 8.0,
     'L1_c': 3.263,
     'L1_wmod': 3.239}
    for name, (base, spread) in spreads.items():
        noise = np.random.default_rng([zlib.crc32(name.encode()), seed]).standard_normal(out[name].shape)
        drawn = base * np.exp(spread * noise) if base else spread * noise
        out[name] = jnp.asarray(drawn.astype(out[name].dtype))
    for name, factor in factors.items():
        out[name] = (out[name] * factor).astype(out[name].dtype)
    return out
```

```python
from contextlib import ExitStack

import numpy as np
import concourse.bass as bass
from concourse import mybir

F32 = mybir.dt.float32
U32 = mybir.dt.uint32
ALU = mybir.AluOpType
ACT = mybir.ActivationFunctionType
AX = mybir.AxisListType.X

P = 128
NBATCH, SEQ, HID = 8, 256, 256
TOK = NBATCH * SEQ
TILES = TOK // P
TPB = SEQ // P
HC = HID // P
NH = 16
QC, KVC, D0 = 192, 64, 128
SCALE0 = 1.0 / float(np.sqrt(D0))
DH, DRH = 16, 8
DQK = DH + DRH
CH, POOL_S, POOL_V = 4, 1, 1
SCALE1 = 1.0 / float(np.sqrt(DH + DRH))
NE = 8
F0, F1 = 688, 512
F0C = 6
F1C = 4
NSPARSE = (2 * TOK + NE * (P - 1)) // P
EPS = 1e-5
SA, CA, GA, SB, CB, GB = range(6)
CT_SA, CT_CA = 0, 2


class Sems:

    def __init__(self, nc, ctx):
        self.nc, self.all = nc, []
        ctx.callback(self.free)

    def free(self):
        self.nc.clear_and_free_semaphores(self.all)
        self.nc.all_engine_barrier()

    def __call__(self, name):
        self.all.append(self.nc.alloc_semaphore(name))
        return self.all[-1]


class Steps:

    def __init__(self, eng, sem):
        self.eng, self.sem, self.base, self.n = eng, sem, 0, 0

    def start(self, base):
        self.base, self.n = base, 0

    def done(self, ins):
        self.n += 1
        ins.then_inc(self.sem, 1)
        self.eng.wait_ge(self.sem, self.base + self.n)


ROW_STEPS = 6


def row_scales(dve, own, sb, var_ready, root_done):
    var, rstd, t = sb["var"][:], sb["rstd"][:], sb["root"][:]
    for k in range(TILES):
        ins = dve.bn_stats(sb["stats"][:, k, :], sb["x"][:, k, :])
    own.done(ins)
    for k in range(TILES):
        ins = dve.bn_aggr(sb["mv"][:, k, :], sb["stats"][:, k, :])
    own.done(ins)
    dve.tensor_scalar(var, sb["mv"][:, :, 1], EPS, None, ALU.add).then_inc(var_ready, 1)
    dve.wait_ge(root_done, 1)
    own.done(dve.reciprocal(rstd, t))
    own.done(dve.tensor_tensor(t, rstd, rstd, ALU.mult))
    own.done(dve.tensor_tensor(t, t, var, ALU.mult))
    own.done(dve.tensor_scalar(t, t, -0.5, 1.5, ALU.mult, ALU.add))
    dve.tensor_tensor(rstd, rstd, t, ALU.mult).then_inc(root_done, 1)
    dve.wait_ge(root_done, 2)


def row_roots(act, sb, var_ready, root_done):
    act.wait_ge(var_ready, 1)
    act.activation(sb["root"][:], sb["var"][:], ACT.Sqrt).then_inc(root_done, 1)


def normalise(dve, sb, tile, xn):
    return dve.tensor_scalar(xn, sb["x"][:, bass.ds(tile, 1), :].rearrange("p o c -> p (o c)"),
                             sb["mv"][:, bass.ds(tile, 1), 0], sb["rstd"][:, bass.ds(tile, 1)], ALU.subtract, ALU.mult)


def setup(nc, io, sb, modd, xs_dram):
    with ExitStack() as ctx:
        cT = ctx.enter_context(nc.sbuf_tensor("cT", [P, 2, HC, NBATCH], F32))
        wmod = ctx.enter_context(nc.sbuf_tensor("wmod", [P, 2, HC, 6 * HID], F32))
        mod = ctx.enter_context(nc.sbuf_tensor("mod", [NBATCH, 2, 6 * HID], F32))
        zero = ctx.enter_context(nc.sbuf_tensor("zero", [P, 4 * HID], F32))
        ps = ctx.enter_context(nc.psum_tensor("mod_ps", [P, 8, 512], F32))
        sem = Sems(nc, ctx)
        loaded, ident_loaded, zeroed, cleared = sem("su_loaded"), sem("su_ident"), sem("su_zeroed"), sem("su_cleared")
        silu_done, mod_ps_done, mod_rows, mod_cols_ps, mod_cols, stored, own_s = (
            sem("su_silu"), sem("su_mod_ps"), sem("su_mod_rows"), sem("su_cols_ps"), sem("su_cols"), sem("su_stored"), sem("su_own"))
        block = ctx.enter_context(nc.Block())

        @block.sync
        def _(sp):
            sp.dma_start(cT[:], io["cT"]).then_inc(loaded, 16)
            sp.dma_start(wmod[:], io["wmod"]).then_inc(loaded, 16)
            sp.dma_start(sb["ident"][:], io["ident"]).then_inc(ident_loaded, 16)
            sp.dma_start(sb["x"][:], io["x"].rearrange("(t p) c -> p t c", p=P)).then_inc(ident_loaded, 16)
            sp.wait_ge(zeroed, 1)
            for l in range(2):
                v = xs_dram[l][0:(NSPARSE + 1) * P, :].rearrange("(n p r) c -> n p (r c)", p=P, r=4)
                for n in range((NSPARSE + 1) // 4):
                    sp.dma_start(v[n], zero[:]).then_inc(cleared, 16)
            sp.dma_start(xs_dram[1][(NSPARSE + TILES) * P:(NSPARSE + TILES + 1) * P, :], zero[:, 0:HID]).then_inc(cleared, 16)
            sp.wait_ge(mod_rows, 1)
            sp.dma_start(modd.rearrange("l b n -> b l n"), mod[:]).then_inc(stored, 16)
            sp.wait_ge(cleared, 16 * (2 * ((NSPARSE + 1) // 4) + 1))
            sp.wait_ge(stored, 16)
            sp.wait_ge(ident_loaded, 32)

        @block.gpsimd
        def _(pool):
            pool.memset(zero[:], 0.0).then_inc(zeroed, 1)

        @block.scalar
        def _(act):
            act.wait_ge(loaded, 32)
            act.activation(cT[:], cT[:], ACT.Silu).then_inc(silu_done, 1)

        @block.tensor
        def _(pe):
            pe.wait_ge(silu_done, 1)
            for l in range(2):
                for n in range(3):
                    for c in range(HC):
                        last = pe.matmul(ps[0:NBATCH, 3 * l + n, :], cT[:, l, c, :], wmod[:, l, c, n * 512:(n + 1) * 512],
                                         start=(c == 0), stop=(c == HC - 1))
            last.then_inc(mod_ps_done, 1)
            pe.wait_ge(ident_loaded, 32)
            pe.wait_ge(mod_rows, 1)
            for l in range(2):
                for j in range(4):
                    src = mod[:, l, j * P:(j + 1) * P]
                    last = pe.transpose(ps[:, 6, (l * 4 + j) * NBATCH:(l * 4 + j + 1) * NBATCH], src, sb["ident"][0:NBATCH, 0:NBATCH])
            last.then_inc(mod_cols_ps, 1)

        @block.vector
        def _(dve):
            own = Steps(dve, own_s)
            dve.wait_ge(mod_ps_done, 1)
            for l in range(2):
                own.done(dve.tensor_copy(mod[:, l, :].rearrange("p (n c) -> p n c", n=3), ps[0:NBATCH, 3 * l:3 * l + 3, :]))
            for l in range(2):
                for k in (CA, CB):
                    v = mod[:, l, k * HID:(k + 1) * HID]
                    own.done(dve.tensor_scalar(v, v, 1.0, None, ALU.add))
                for k in (GA, GB):
                    v = mod[:, l, k * HID:(k + 1) * HID]
                    s = ps[0:NBATCH, 7, 0:HID]
                    own.done(dve.tensor_scalar(s, v, 0.0, 2.0, ALU.is_ge, ALU.mult))
                    own.done(dve.scalar_tensor_tensor(v, v, -1.0, v, ALU.mult, ALU.max))
                    own.done(dve.tensor_scalar(v, v, 0.25, None, ALU.max))
                    ins = dve.scalar_tensor_tensor(v, s, -1.0, v, ALU.add, ALU.mult)
                    if (l, k) == (1, GB):
                        ins.then_inc(mod_rows, 1)
                    else:
                        own.done(ins)
            dve.wait_ge(mod_cols_ps, 1)
            dve.tensor_copy(sb["modT"][:].rearrange("p l j b -> p (l j b)"), ps[:, 6, 0:2 * 4 * NBATCH]).then_inc(mod_cols, 1)
            dve.wait_ge(mod_cols, 1)


class Attn:

    def __init__(self, nc, ctx, l, cw):
        s = lambda n, shape: ctx.enter_context(nc.sbuf_tensor(f"a{l}_{n}", shape, F32))
        sems = Sems(nc, ctx)
        q = lambda n: sems(f"a{l}_{n}")
        self.l = l
        self.xn = s("xn", [P, TPB, HID])
        self.var_ready, self.root_done = q("var_ready"), q("root_done")
        self.hT = s("hT", [P, HC, SEQ])
        self.mx, self.sums, self.rinv = s("mx", [P, 8, 4]), s("sums", [P, 8, 4]), s("rinv", [P, 8, 4])
        self.prob = s("prob", [P, 2, 4, SEQ])
        self.probT = s("probT", [P, 4, TPB, P])
        self.ctxT = s("ctxT", [P, 2, cw])
        self.ga = s("ga", [P, 2, HID])
        self.y = s("y", [P, HID])
        self.bo = s("bo", [P, HID])
        self.ps = ctx.enter_context(nc.psum_tensor(f"a{l}_ps", [P, 8, 512], F32))
        self.own_s = q("own")
        self.xn_ready, self.hT_ps, self.hT_sb = q("xn_ready"), q("hT_ps"), q("hT_sb")
        self.q_ready, self.scores, self.max_ready, self.exp_done, self.prob_ready = (
            q("q_ready"), q("scores"), q("max_ready"), q("exp_done"), q("prob_ready"))
        self.pT_ps, self.pT_act, self.pT_dve, self.ctx_ps, self.ctx_sb, self.out_ps, self.x_done = (
            q("pT_ps"), q("pT_act"), q("pT_dve"), q("ctx_ps"), q("ctx_sb"), q("out_ps"), q("x_done"))
        self.ga_loaded, self.gated = q("ga_loaded"), q("gated")
        self.S = lambda k: self.ps[:, 2 * (k % 2):2 * (k % 2) + 2, :]
        self.T = self.ps[:, 4:6, :]
        self.C = self.ps[:, 6, :]
        self.O = self.ps[:, 7, 0:HID]


STEPS = 8


def attn_act_steps(nc, act, A, i, scale):
    for s in range(STEPS):
        act.wait_ge(A.max_ready, STEPS * i + s + 1)
        if s < 2:
            act.wait_ge(A.out_ps, 2 * i + 1)
        else:
            act.wait_ge(A.pT_ps, STEPS * i + s - 1)
        for j in range(4):
            ins = act.activation(A.prob[:, s % 2, j, :], A.S(s)[:, j // 2, (j % 2) * SEQ:(j % 2 + 1) * SEQ], ACT.Exp,
                                 bias=A.mx[:, s, j:j + 1], scale=scale, accum_out=A.sums[:, s, j:j + 1])
        ins.then_inc(A.exp_done, 1)
        if s >= 1:
            act_evacuate(act, A, i, s - 1)
    act_evacuate(act, A, i, STEPS - 1)


def act_evacuate(act, A, i, s):
    act.wait_ge(A.pT_ps, STEPS * i + s + 1)
    act.activation(A.probT[:, 0:2, :, :].rearrange("p h k q -> p (h k q)"), A.T[:, 0, :], ACT.Copy).then_inc(A.pT_act, 1)
    act.wait_ge(A.ctx_ps, STEPS * i + s + 1)
    w = A.ctxT.shape[2]
    act.activation(A.ctxT[:, s % 2, :], A.C[:, 0:w], ACT.Copy).then_inc(A.ctx_sb, 1)


def attn_dve_max(nc, dve, A, own, i, s, scale):
    dve.wait_ge(A.scores, STEPS * i + s + 1)
    own.done(dve.tensor_reduce(A.mx[:, s, :], A.S(s).rearrange("p b (h k) -> p (b h) k", h=2), AX, ALU.max))
    dve.tensor_scalar(A.mx[:, s, :], A.mx[:, s, :], -scale, None, ALU.mult).then_inc(A.max_ready, 1)


def attn_dve_steps(nc, dve, A, own, i, scale):
    attn_dve_max(nc, dve, A, own, i, 0, scale)
    attn_dve_max(nc, dve, A, own, i, 1, scale)
    for s in range(STEPS):
        dve.wait_ge(A.exp_done, STEPS * i + s + 1)
        own.done(dve.reciprocal(A.rinv[:, s, :], A.sums[:, s, :]))
        for j in range(4):
            ins = dve.tensor_scalar(A.prob[:, s % 2, j, :], A.prob[:, s % 2, j, :], A.rinv[:, s, j:j + 1], None, ALU.mult)
        ins.then_inc(A.prob_ready, 1)
        if s + 2 < STEPS:
            attn_dve_max(nc, dve, A, own, i, s + 2, scale)
        dve.wait_ge(A.pT_ps, STEPS * i + s + 1)
        dve.tensor_copy(A.probT[:, 2:4, :, :].rearrange("p h k q -> p (h k q)"), A.T[:, 1, :]).then_inc(A.pT_dve, 1)
        if s % 4 == 0 and s > 0:
            attn_dve_out(nc, dve, A, own, i, 0)
    attn_dve_out(nc, dve, A, own, i, 1)


def attn_dve_out(nc, dve, A, own, i, qt):
    x = A.x[:, bass.ds(TPB * i + qt, 1), :].rearrange("p o c -> p (o c)")
    dve.wait_ge(A.out_ps, 2 * i + qt + 2)
    dve.tensor_tensor(A.y[:], A.O, A.bo[:], ALU.add).then_inc(A.x_done, 1)
    dve.wait_ge(A.x_done, 2 * i + qt + 2)
    if qt == 0:
        dve.wait_ge(A.ga_loaded, 16 * i + 16)
    dve.tensor_tensor(A.y[:], A.y[:], A.ga[:, 0, :], ALU.mult).then_inc(A.gated, 1)
    dve.wait_ge(A.gated, 2 * i + qt + 2)
    own.done(dve.tensor_tensor(x, x, A.y[:], ALU.add))


def attn_pe_scores(pe, A, i, s, lhs, rhs):
    if s >= 2:
        pe.wait_ge(A.exp_done, STEPS * i + s - 1)
    for b in range(2):
        ins = pe.matmul(A.S(s)[:, b, :], lhs(s, b), rhs(s, b), start=True, stop=True)
    ins.then_inc(A.scores, 1)


def attn_pe_out(pe, A, i, s, wout):
    pe.wait_ge(A.ctx_sb, STEPS * i + s + 1)
    if s == 0:
        pe.wait_ge(A.x_done, 2 * i + 1)
    if s == 4:
        pe.wait_ge(A.x_done, 2 * i + 2)
    parts = wout(s)
    for n, w in enumerate(parts):
        ins = pe.matmul(A.O, A.ctxT[:, s % 2, n * P:(n + 1) * P], w, start=(s % 4 == 0 and n == 0),
                        stop=(s % 4 == 3 and n == len(parts) - 1))
    if s % 4 == 3:
        ins.then_inc(A.out_ps, 1)


def attn_pe_steps(pe, A, i, lhs, rhs, context, wout, ident):
    attn_pe_scores(pe, A, i, 0, lhs, rhs)
    attn_pe_scores(pe, A, i, 1, lhs, rhs)
    for s in range(STEPS):
        pe.wait_ge(A.prob_ready, STEPS * i + s + 1)
        if s > 0:
            pe.wait_ge(A.pT_act, STEPS * i + s)
            pe.wait_ge(A.pT_dve, STEPS * i + s)
        for j in range(4):
            for k in range(TPB):
                ins = pe.transpose(A.T[:, j // 2, ((j % 2) * TPB + k) * P:((j % 2) * TPB + k + 1) * P],
                                   A.prob[:, s % 2, j, k * P:(k + 1) * P], ident[:])
        ins.then_inc(A.pT_ps, 1)
        if s + 2 < STEPS:
            attn_pe_scores(pe, A, i, s + 2, lhs, rhs)
        if s > 0:
            attn_pe_out(pe, A, i, s - 1, wout)
        pe.wait_ge(A.pT_act, STEPS * i + s + 1)
        pe.wait_ge(A.pT_dve, STEPS * i + s + 1)
        context(s).then_inc(A.ctx_ps, 1)
    attn_pe_out(pe, A, i, STEPS - 1, wout)


def attn_pe_norm(pe, A, i, ident):
    for t in range(TPB):
        pe.wait_ge(A.xn_ready, TPB * i + t + 1)
        for c in range(HC):
            ins = pe.transpose(A.ps[:, 4, c * SEQ + t * P:c * SEQ + (t + 1) * P], A.xn[:, t, c * P:(c + 1) * P], ident[:])
    ins.then_inc(A.hT_ps, 1)


def attn_act_norm(act, A, i, modT):
    act.wait_ge(A.hT_ps, i + 1)
    for c in range(HC):
        ins = act.activation(A.hT[:, c, :], A.ps[:, 4, c * SEQ:(c + 1) * SEQ], ACT.Identity,
                             scale=modT[:, A.l, CT_CA + c, bass.ds(i, 1)], bias=modT[:, A.l, CT_SA + c, bass.ds(i, 1)])
    ins.then_inc(A.hT_sb, 1)


def attn_dve_norm(dve, A, sb, i):
    for t in range(TPB):
        normalise(dve, sb, TPB * i + t, A.xn[:, t, :]).then_inc(A.xn_ready, 1)


def attn_sync(sp, A, modd):
    with sp.Fori(0, NBATCH) as i:
        sp.wait_ge(A.gated, 2 * i + 1)
        sp.dma_start(A.ga[:, 0, :], modd[A.l, bass.ds(i, 1), GA * HID:(GA + 1) * HID].to_broadcast([P, HID])).then_inc(A.ga_loaded, 16)


def attention0(nc, io, sb, modd):
    with ExitStack() as ctx:
        s = lambda n, shape: ctx.enter_context(nc.sbuf_tensor(f"l0_{n}", shape, F32))
        sems = Sems(nc, ctx)
        q = lambda n: sems(f"l0_{n}")
        wlat = s("wlat", [P, HC, QC + 2 * KVC])
        blat = s("blat", [P, 3])
        aq = s("aq", [P, 2, NH * KVC])
        aqb = s("aqb", [P, NH // 2])
        wvo = s("wvo", [P, NH // 2, HID])
        A = Attn(nc, ctx, 0, 2 * P)
        A.x = sb["x"]
        ident = sb["ident"]
        q_ps, q_act, q_dve = q("q_ps"), q("q_act"), q("q_dve")
        lat_ps, lat_sb, tok_ps, tok_sb = q("lat_ps"), q("lat_sb"), q("tok_ps"), q("tok_sb")

        with ExitStack() as pre:
            t = lambda n, shape: pre.enter_context(nc.sbuf_tensor(f"l0_{n}", shape, F32))
            pre_sems = Sems(nc, pre)
            r = lambda n: pre_sems(f"l0_{n}")
            wuq, wuk, wuv, woT = t("wuq", [P, NH, QC]), t("wuk", [P, NH, KVC]), t("wuv", [P, NH, KVC]), t("woT", [P, NH, HID])
            bup, bo_row, ones = t("bup", [P, 2, NH]), t("bo_row", [1, 2, HID]), t("ones", [1, P])
            loaded, onesd, fold_ps, fold_sb, bias_row, bias_ps = r("pw_loaded"), r("pw_ones"), r("fold_ps"), r("fold_sb"), r("bias_row"), r("bias_ps")
            block = pre.enter_context(nc.Block())

            @block.sync
            def _(sp):
                for dst, name in ((wuq, "l0_wuq"), (wuk, "l0_wuk"), (wuv, "l0_wuv"), (woT, "l0_woT"), (bup, "l0_bup"),
                                  (wlat, "l0_wlat"), (blat, "l0_blat")):
                    sp.dma_start(dst[:], io[name]).then_inc(loaded, 16)
                sp.dma_start(bo_row[:, 0, :], io["l0_bo"]).then_inc(loaded, 16)

            @block.tensor
            def _(pe):
                pe.wait_ge(loaded, 16 * 8)
                for h in range(NH):
                    cols = slice((h % 8) * KVC, (h % 8 + 1) * KVC)
                    pe.matmul(A.ps[:, h // 8, cols], wuq[:, h, 0:P], wuk[:, h, :], start=True, stop=True)
                    pe.matmul(A.ps[0:QC - P, 2 + h // 8, cols], wuq[:, h, P:QC], wuk[:, h, :], start=True, stop=True)
                    r0 = (h % 2) * KVC
                    ins = pe.matmul(A.ps[r0:r0 + KVC, 4, h // 2:h // 2 + 1], wuk[:, h, :], bup[:, 0, h:h + 1], start=True, stop=True)
                ins.then_inc(fold_ps, 1)
                pe.wait_ge(fold_sb, 1)
                for h in range(NH):
                    r0, c0 = (h % 2) * KVC, (h // 2 % 2) * HID
                    pe.matmul(A.ps[r0:r0 + KVC, h // 4, c0:c0 + HID], wuv[:, h, :], woT[:, h, :], start=True, stop=True)
                for h in range(NH):
                    ins = pe.matmul(A.ps[0:1, 5, 0:HID], bup[:, 1, h:h + 1], woT[:, h, :], start=(h == 0), stop=(h == NH - 1))
                ins.then_inc(fold_ps, 1)
                pe.wait_ge(bias_row, 1)
                pe.matmul(A.ps[:, 6, 0:HID], ones[:], bo_row[:, 1, :], start=True, stop=True).then_inc(bias_ps, 1)

            @block.vector
            def _(dve):
                dve.memset(ones[:], 1.0).then_inc(onesd, 1)
                dve.wait_ge(fold_ps, 1)
                dve.tensor_copy(aq[:, 0, :].rearrange("p (b c) -> p b c", b=2), A.ps[:, 0:2, :])
                dve.tensor_copy(aqb[:], A.ps[:, 4, 0:NH // 2])
                dve.tensor_copy(aq[0:QC - P, 1, :].rearrange("p (b c) -> p b c", b=2), A.ps[0:QC - P, 2:4, :]).then_inc(fold_sb, 1)
                dve.wait_ge(fold_ps, 2)
                dve.tensor_copy(wvo[:].rearrange("p (b h) c -> p b (h c)", b=4), A.ps[:, 0:4, :])
                dve.wait_ge(onesd, 1)
                dve.wait_ge(loaded, 16 * 8)
                dve.tensor_tensor(bo_row[:, 1, :], A.ps[0:1, 5, 0:HID], bo_row[:, 0, :], ALU.add).then_inc(bias_row, 1)
                dve.wait_ge(bias_ps, 1)
                dve.tensor_copy(A.bo[:], A.ps[:, 6, 0:HID])

        cq = s("cq", [P, 2, SEQ])
        ckv = s("ckv", [P, 2, SEQ])
        ckvt = s("ckvt", [P, TPB, KVC])
        qT = s("qT", [P, NH // 2, SEQ])
        block = ctx.enter_context(nc.Block())

        @block.sync
        def _(sp):
            attn_sync(sp, A, modd)
            sp.wait_ge(A.ga_loaded, 16 * NBATCH)

        @block.tensor
        def _(pe):
            pe.wait_ge(A.q_ready, 1)
            with pe.Fori(0, NBATCH) as i:
                attn_pe_norm(pe, A, i, ident)
                pe.wait_ge(A.hT_sb, i + 1)
                for c in range(HC):
                    pe.matmul(A.ps[:, 0, 0:SEQ], wlat[:, c, 0:P], A.hT[:, c, :], start=(c == 0), stop=(c == HC - 1))
                for c in range(HC):
                    pe.matmul(A.ps[0:QC - P, 1, 0:SEQ], wlat[:, c, P:QC], A.hT[:, c, :], start=(c == 0), stop=(c == HC - 1))
                for c in range(HC):
                    ins = pe.matmul(A.ps[:, 2, 0:SEQ], wlat[:, c, QC:QC + P], A.hT[:, c, :], start=(c == 0), stop=(c == HC - 1))
                ins.then_inc(lat_ps, 1)
                pe.wait_ge(lat_sb, i + 1)
                for p in range(NH // 2):
                    dst = A.ps[:, p // 2, (p % 2) * SEQ:(p % 2 + 1) * SEQ]
                    pe.matmul(dst, aq[:, 0, p * P:(p + 1) * P], cq[:, 0, :], start=True, stop=False)
                    ins = pe.matmul(dst, aq[0:QC - P, 1, p * P:(p + 1) * P], cq[0:QC - P, 1, :], start=False, stop=True)
                    if p % 2:
                        ins.then_inc(q_ps, 1)
                    if p == 0:
                        for t in range(TPB):
                            ins = pe.transpose(A.ps[:, 4, t * KVC:(t + 1) * KVC], ckv[0:KVC, 0, t * P:(t + 1) * P], ident[0:KVC, 0:KVC])
                        ins.then_inc(tok_ps, 1)
                pe.wait_ge(q_act, 4 * i + 4)
                pe.wait_ge(q_dve, 4 * i + 4)
                pe.wait_ge(tok_sb, i + 1)

                def context(st):
                    for j in range(4):
                        for k in range(TPB):
                            pr = j // 2
                            ins = pe.matmul(A.C[(j % 2) * KVC:(j % 2 + 1) * KVC, pr * P:(pr + 1) * P], ckvt[:, k, :],
                                            A.probT[:, j, k, :], start=(k == 0), stop=(k == TPB - 1))
                    return ins

                attn_pe_steps(pe, A, i,
                              lhs=lambda st, b: qT[:, (st % 4) * 2 + b, (st // 4) * P:(st // 4 + 1) * P],
                              rhs=lambda st, b: ckv[:].rearrange("p h k -> p (h k)"),
                              context=context,
                              wout=lambda st: [wvo[:, (st % 4) * 2 + n, :] for n in range(2)],
                              ident=ident)

        @block.scalar
        def _(act):
            row_roots(act, sb, A.var_ready, A.root_done)
            with act.Fori(0, NBATCH) as i:
                attn_act_norm(act, A, i, sb["modT"])
                act.wait_ge(lat_ps, i + 1)
                act.activation(cq[:, 0, :], A.ps[:, 0, 0:SEQ], ACT.Identity, bias=blat[:, 0:1])
                act.activation(cq[0:QC - P, 1, :], A.ps[0:QC - P, 1, 0:SEQ], ACT.Identity, bias=blat[0:QC - P, 1:2])
                for h in range(2):
                    ins = act.activation(ckv[h * KVC:(h + 1) * KVC, h, :], A.ps[h * KVC:(h + 1) * KVC, 2, 0:SEQ], ACT.Identity,
                                         bias=blat[h * KVC:(h + 1) * KVC, 2:3])
                ins.then_inc(lat_sb, 1)
                for b in range(0, 4, 2):
                    act.wait_ge(q_ps, 4 * i + b + 1)
                    for n in range(2):
                        p = 2 * b + n
                        act.activation(qT[:, p, :], A.ps[:, b, n * SEQ:(n + 1) * SEQ], ACT.Identity, bias=aqb[:, p:p + 1]).then_inc(q_act, 1)
                attn_act_steps(nc, act, A, i, SCALE0)

        @block.vector
        def _(dve):
            own = Steps(dve, A.own_s)
            dve.memset(ckv[:], 0.0).then_inc(A.q_ready, 1)
            dve.memset(A.y[:], 0.0).then_inc(A.x_done, 1)
            dve.memset(A.mx[:], 0.0).then_inc(A.out_ps, 1)
            dve.memset(A.sums[:], 0.0).then_inc(A.gated, 1)
            own_per_batch = STEPS * 2 + 2
            row_scales(dve, own, sb, A.var_ready, A.root_done)
            with dve.Fori(0, NBATCH) as i:
                own.start(own_per_batch * i + ROW_STEPS)
                attn_dve_norm(dve, A, sb, i)
                dve.wait_ge(tok_ps, i + 1)
                dve.tensor_copy(ckvt[:].rearrange("p t c -> p (t c)"), A.ps[:, 4, 0:TPB * KVC]).then_inc(tok_sb, 1)
                for b in range(1, 4, 2):
                    dve.wait_ge(q_ps, 4 * i + b + 1)
                    for n in range(2):
                        p = 2 * b + n
                        dve.tensor_scalar(qT[:, p, :], A.ps[:, b, n * SEQ:(n + 1) * SEQ], aqb[:, p:p + 1], None, ALU.add).then_inc(q_dve, 1)
                attn_dve_steps(nc, dve, A, own, i, SCALE0)
                assert own.n == own_per_batch, own.n


def attention1(nc, io, sb, modd):
    with ExitStack() as ctx:
        s = lambda n, shape: ctx.enter_context(nc.sbuf_tensor(f"l1_{n}", shape, F32))
        sems = Sems(nc, ctx)
        q = lambda n: sems(f"l1_{n}")
        wlat = s("wlat", [P, HC, P])
        blat = s("blat", [P, 1])
        wqkv = s("wqkv", [P, 384 + 512])
        wkr = s("wkr", [P, HC, P])
        btok = s("btok", [P, 1024])
        wo = s("wo", [P, HC, HID])
        rope = s("rope", [P, 2, TPB, DRH])
        bo = s("bo", [P, HID])
        ga = s("ga", [P, NBATCH, HID])
        shift = s("shift", [P, TILES])
        xn = s("xn", [P, HID])
        hT = s("hT", [P, HC, P])
        cT = s("cT", [P, P])
        qk = s("qk", [P, 2, NH, DQK])
        rt = s("rt", [P, 2, 2 * NH, DRH])
        v = s("v", [P, DH, NH])
        prod = s("prod", [P, CH, NH // CH, NH * DQK])
        sc = s("sc", [P, NH, NH])
        red = s("red", [P, 3, NH])
        o = s("o", [P, NH, DH])
        oT = s("oT", [P, HC, P])
        y = s("y", [P, HID])
        ps = ctx.enter_context(nc.psum_tensor("l1_ps", [P, 8, 512], F32))
        var_ready, root_done, shift_ready, loaded, own_s, pool_own = (
            q("var_ready"), q("root_done"), q("shift_ready"), q("loaded"), q("own"), q("pool_own"))
        xn_ready, xT_ps, hT_sb, lat_ps, lat_sb, tok_ps, tok_read, qk_ready = (
            q("xn_ready"), q("xT_ps"), q("hT_sb"), q("lat_ps"), q("lat_sb"), q("tok_ps"), q("tok_read"), q("qk_ready"))
        s_prod, s_red, sc_ready, exp_done, p_ready, v_prod, o_ready, oT_ps, oT_sb, out_ps, out_read = (
            q("s_prod"), q("s_red"), q("sc_ready"), q("exp_done"), q("p_ready"), q("v_prod"), q("o_ready"), q("oT_ps"), q("oT_sb"),
            q("out_ps"), q("out_read"))
        block = ctx.enter_context(nc.Block())
        LOADS = 9
        ident = sb["ident"]
        HG = NH // CH

        def pipeline(eng, first, both, last):
            first(0)
            with eng.Fori(0, TILES // 2 - 1) as i:
                both(2 * i, 0, i)
                both(2 * i + 1, 1, i)
            both(TILES - 2, 0, NBATCH - 1)
            last(TILES - 1)

        def score_product(eng, c):
            return eng.tensor_tensor(prod[:, c, :, :].rearrange("p i (j d) -> p i j d", j=NH),
                                     qk[:, 0, c * HG:(c + 1) * HG, :].rearrange("p i (o d) -> p i o d", o=1).to_broadcast([P, HG, NH, DQK]),
                                     qk[:, 1, :, :].rearrange("p (o j) d -> p o j d", o=1).to_broadcast([P, HG, NH, DQK]), ALU.mult)

        def value_product(eng, c):
            return eng.tensor_tensor(prod[:, c, :, 0:DH * NH].rearrange("p i (d j) -> p i d j", d=DH),
                                     sc[:, c * HG:(c + 1) * HG, :].rearrange("p i (o j) -> p i o j", o=1).to_broadcast([P, HG, DH, NH]),
                                     v[:].rearrange("p (o d) j -> p o d j", o=1).to_broadcast([P, HG, DH, NH]), ALU.mult)

        @block.sync
        def _(sp):
            for dst, name in ((wlat, "l1_wlat"), (blat, "l1_blat"), (wqkv, "l1_wqkv"), (wkr, "l1_wkr"), (wo, "l1_wo"), (rope, "l1_rope")):
                sp.dma_start(dst[:], io[name]).then_inc(loaded, 16)
            sp.dma_start(btok[:], io["l1_btok"].to_broadcast([P, 1024])).then_inc(loaded, 16)
            sp.dma_start(bo[:], io["l1_bo"].to_broadcast([P, HID])).then_inc(loaded, 16)
            sp.dma_start(ga[:], modd[1:2, :, GA * HID:(GA + 1) * HID].to_broadcast([P, NBATCH, HID])).then_inc(loaded, 16)

        @block.tensor
        def _(pe):
            def front(t, u):
                pe.wait_ge(xn_ready, t + 1)
                for c in range(HC):
                    ins = pe.transpose(ps[:, 0, c * P:(c + 1) * P], xn[:, c * P:(c + 1) * P], ident[:])
                ins.then_inc(xT_ps, 1)
                pe.wait_ge(hT_sb, t + 1)
                for c in range(HC):
                    ins = pe.matmul(ps[:, 1, 0:P], wlat[:, c, :], hT[:, c, :], start=(c == 0), stop=(c == HC - 1))
                ins.then_inc(lat_ps, 1)
                pe.wait_ge(tok_read, t + 1)
                for c in range(HC):
                    pe.matmul(ps[:, 2 + 2 * u, 384:512], hT[:, c, :], wkr[:, c, :], start=(c == 0), stop=(c == HC - 1))
                pe.wait_ge(lat_sb, t + 1)
                pe.matmul(ps[:, 2 + 2 * u, 0:384], cT[:], wqkv[:, 0:384], start=True, stop=True)
                pe.matmul(ps[:, 3 + 2 * u, :], cT[:], wqkv[:, 384:896], start=True, stop=True).then_inc(tok_ps, 1)

            def tail(t):
                pe.wait_ge(o_ready, t + 1)
                for c in range(HC):
                    ins = pe.transpose(ps[:, 6, c * P:(c + 1) * P], o[:, c * (NH // HC):(c + 1) * (NH // HC), :].rearrange("p i d -> p (i d)"), ident[:])
                ins.then_inc(oT_ps, 1)
                pe.wait_ge(oT_sb, t + 1)
                pe.wait_ge(out_read, t + 1)
                for c in range(HC):
                    ins = pe.matmul(ps[:, 7, 0:HID], oT[:, c, :], wo[:, c, :], start=(c == 0), stop=(c == HC - 1))
                ins.then_inc(out_ps, 1)

            def both(t, u, b):
                front(t + 1, 1 - u)
                tail(t)

            pe.wait_ge(loaded, 16 * LOADS)
            pipeline(pe, lambda t: front(t, 0), both, tail)

        @block.scalar
        def _(act):
            def front(t, b):
                act.activation(xn[:], sb["x"][:, bass.ds(t, 1), :].rearrange("p o c -> p (o c)"), ACT.Identity,
                               scale=sb["rstd"][:, bass.ds(t, 1)], bias=shift[:, bass.ds(t, 1)]).then_inc(xn_ready, 1)
                act.wait_ge(xT_ps, t + 1)
                for c in range(HC):
                    ins = act.activation(hT[:, c, :], ps[:, 0, c * P:(c + 1) * P], ACT.Identity,
                                         scale=sb["modT"][:, 1, CT_CA + c, bass.ds(b, 1)], bias=sb["modT"][:, 1, CT_SA + c, bass.ds(b, 1)])
                ins.then_inc(hT_sb, 1)
                act.wait_ge(lat_ps, t + 1)
                act.activation(cT[:], ps[:, 1, 0:P], ACT.Identity, bias=blat[:]).then_inc(lat_sb, 1)

            def middle(t):
                act.wait_ge(sc_ready, t + 1)
                act.activation(sc[:], sc[:], ACT.Exp, scale=SCALE1).then_inc(exp_done, 1)

            def tail(t):
                act.wait_ge(oT_ps, t + 2)
                act.activation(oT[:].rearrange("p c q -> p (c q)"), ps[:, 6, 0:HID], ACT.Copy).then_inc(oT_sb, 1)

            def both(t, u, b):
                middle(t)
                front(t + 1, b + u)
                tail(t)

            def last(t):
                middle(t)
                tail(t)

            act.wait_ge(loaded, 16 * LOADS)
            row_roots(act, sb, var_ready, root_done)
            act.wait_ge(shift_ready, 1)
            pipeline(act, lambda t: front(t, 0), both, last)

        @block.gpsimd
        def _(pool):
            with pool.Fori(0, TILES) as t:
                pool.wait_ge(qk_ready, t + 1)
                for c in range(POOL_S):
                    score_product(pool, c).then_inc(s_prod, 1)
                pool.wait_ge(p_ready, t + 1)
                for c in range(POOL_V):
                    value_product(pool, c).then_inc(v_prod, 1)

        @block.vector
        def _(dve):
            own = Steps(dve, own_s)
            per_tile = 6 + (CH > POOL_S) + (CH > POOL_V) + 1

            def output(t, b):
                x = sb["x"][:, bass.ds(t, 1), :].rearrange("p o c -> p (o c)")
                dve.wait_ge(out_ps, t + 1)
                dve.tensor_tensor(y[:], ps[:, 7, 0:HID], bo[:], ALU.add).then_inc(out_read, 1)
                dve.wait_ge(out_read, t + 2)
                own.done(dve.tensor_tensor(y[:], y[:], ga[:, bass.ds(b, 1), :].rearrange("p o c -> p (o c)"), ALU.mult))
                dve.tensor_tensor(x, x, y[:], ALU.add)

            def heavy(t, u, pending):
                own.start(ROW_STEPS if pending is None else per_tile * t + ROW_STEPS - 1)
                bank = 2 + 2 * u
                dve.wait_ge(tok_ps, t + 1)
                heads = lambda a, w: a.rearrange("p (h d) -> p h d", d=w)
                dve.tensor_tensor(qk[:, 0, :, 0:DH], heads(ps[:, bank, 0:256], DH), heads(btok[:, 0:256], DH), ALU.add)
                dve.tensor_tensor(qk[:, :, :, DH:DQK], ps[:, bank, 256:512].rearrange("p (n h d) -> p n h d", n=2, d=DRH),
                                  btok[:, 256:512].rearrange("p (n h d) -> p n h d", n=2, d=DRH), ALU.add)
                dve.tensor_tensor(qk[:, 1, :, 0:DH], heads(ps[:, bank + 1, 0:256], DH), heads(btok[:, 512:768], DH), ALU.add)
                own.done(dve.tensor_tensor(v[:].rearrange("p d j -> p j d"), heads(ps[:, bank + 1, 256:512], DH), heads(btok[:, 768:1024], DH), ALU.add))
                r = qk[:].rearrange("p n h d -> p (n h) d")[:, :, DH:DQK]
                cs = lambda n, a, b: rope[:, n, u:u + 1, a:b].to_broadcast([P, 2 * NH, b - a])
                hf = DRH // 2
                dve.tensor_tensor(rt[:, 0, :, :], r, cs(0, 0, DRH), ALU.mult)
                dve.tensor_tensor(rt[:, 1, :, 0:hf], r[:, :, hf:DRH], cs(1, 0, hf), ALU.mult).then_inc(tok_read, 1)
                own.done(dve.tensor_tensor(rt[:, 1, :, hf:DRH], r[:, :, 0:hf], cs(1, hf, DRH), ALU.mult))
                own_ins = dve.tensor_tensor(r, rt[:, 0, :, :], rt[:, 1, :, :], ALU.add)
                own_ins.then_inc(qk_ready, 1)
                dve.wait_ge(qk_ready, t + 1)
                for c in range(POOL_S, CH):
                    ins = score_product(dve, c)
                if POOL_S < CH:
                    own.done(ins)
                if pending is not None:
                    output(*pending)
                for c in [*range(POOL_S, CH), *range(POOL_S)]:
                    if c < POOL_S:
                        dve.wait_ge(s_prod, POOL_S * t + c + 1)
                    ins = dve.tensor_reduce(sc[:, c * HG:(c + 1) * HG, :], prod[:, c, :, :].rearrange("p i (j d) -> p i j d", j=NH), AX, ALU.add)
                own.done(ins)
                row = lambda k: red[:, k, :].rearrange("p (i o) -> p i o", o=1).to_broadcast([P, NH, NH])
                own.done(dve.tensor_reduce(red[:, 0, :], sc[:], AX, ALU.max))
                dve.tensor_tensor(sc[:], sc[:], row(0), ALU.subtract).then_inc(sc_ready, 1)
                dve.wait_ge(exp_done, t + 1)
                own.done(dve.tensor_reduce(red[:, 1, :], sc[:], AX, ALU.add))
                own.done(dve.reciprocal(red[:, 2, :], red[:, 1, :]))
                dve.tensor_tensor(sc[:], sc[:], row(2), ALU.mult).then_inc(p_ready, 1)
                dve.wait_ge(p_ready, t + 1)
                for c in range(POOL_V, CH):
                    ins = value_product(dve, c)
                if POOL_V < CH:
                    own.done(ins)
                dve.wait_ge(oT_ps, t + 1)
                for c in [*range(POOL_V, CH), *range(POOL_V)]:
                    if c < POOL_V:
                        dve.wait_ge(v_prod, POOL_V * t + c + 1)
                    ins = dve.tensor_reduce(o[:, c * HG:(c + 1) * HG, :], prod[:, c, :, 0:DH * NH].rearrange("p i (d j) -> p i d j", d=DH), AX, ALU.add)
                ins.then_inc(o_ready, 1)

                assert own.n == per_tile - (pending is None), own.n

            dve.memset(prod[:, 0, 0, 0:1], 0.0).then_inc(tok_read, 2)
            dve.memset(prod[:, 0, 0, 1:2], 0.0).then_inc(out_read, 1)
            dve.memset(prod[:, 0, 0, 2:3], 0.0).then_inc(oT_ps, 1)
            dve.wait_ge(loaded, 16 * LOADS)
            row_scales(dve, own, sb, var_ready, root_done)
            dve.scalar_tensor_tensor(shift[:], sb["mv"][:, :, 0], -1.0, sb["rstd"][:], ALU.mult, ALU.mult).then_inc(shift_ready, 1)
            pipeline(dve, lambda t: heavy(t, 0, None), lambda t, u, b: heavy(t + 1, 1 - u, (t, b)), lambda t: output(t, NBATCH - 1))


def mixture(nc, io, sb, modd, l, xs, ys, out):
    F, FC = ((F0, F0C), (F1, F1C))[l]
    ne = NE + l
    shared = TILES if l else 0
    nt = NSPARSE + shared
    FP = FC * P
    half = F // 2
    with ExitStack() as ctx:
        s = lambda n, shape, dt=F32: ctx.enter_context(nc.sbuf_tensor(f"m{l}_{n}", shape, dt))
        sems = Sems(nc, ctx)
        q = lambda n: sems(f"m{l}_{n}")
        wg, wu = s("wg", [P, HC, ne, F]), s("wu", [P, HC, ne, F])
        wd = s("wd", [P, ne * FC, HID])
        pos = s("pos", [P, 2, TILES], U32)
        prob = s("prob", [P, 2, TILES])
        eid = s("eid", [1, nt], U32)
        w_loaded = q("w_loaded")

        with ExitStack() as rc:
            t_ = lambda n, shape, dt=F32: rc.enter_context(nc.sbuf_tensor(f"r{l}_{n}", shape, dt))
            part_sems = Sems(nc, rc)
            r = lambda n, part_sems=part_sems: part_sems(f"r{l}_{n}")
            h = t_("h", [P, TILES, HID])
            hcur = t_("hcur", [P, TPB, HID])
            modb = t_("modb", [P, 2, 2, HID])
            wr = t_("wr", [P, HC, NE])
            var_ready, root_done = r("var_ready"), r("root_done")
            hT = t_("hT", [P, 2, HC, P])
            rk = t_("rk", [P, 10, TILES, NE])
            sm = t_("sm", [P, 8, TILES])
            cst = t_("cst", [P, 3 * P + 64 + 16])
            tri, ones_m, rev = cst[:, 0:P], cst[:, P:2 * P], cst[:, 2 * P:2 * P + NE]
            thr, tile_no = cst[:, 2 * P + 16:2 * P + 32], cst[0:1, 2 * P + 32:2 * P + 32 + NSPARSE]
            ex = t_("ex", [P, 4, NE])
            ecmp = t_("ecmp", [P, NE * TILES])
            ejc = t_("ejc", [1, NSPARSE, NE])
            ejs = t_("ejs", [1, nt])
            ps = rc.enter_context(nc.psum_tensor(f"r{l}_ps", [P, 8, 512], F32))
            mods, shared_sent = [r("mods0"), r("mods1")], r("shared_sent")
            own_s, loaded, mods_free, h_ready, hT_ps, hT_sb, logits, masks, ranks, diff, e2, pos_ready, sent = (
                r("own"), r("loaded"), r("mods_free"), r("h_ready"), r("hT_ps"), r("hT_sb"), r("logits"), r("masks"),
                r("ranks"), r("diff"), r("e2"), r("pos_ready"), r("sent"))
            block = rc.enter_context(nc.Block())

            @block.sync
            def _(sp):
                sp.dma_start(wr[:], io[f"l{l}_wr"]).then_inc(loaded, 16)
                sp.dma_start(cst[:, 0:2 * P + 96], io["cst"]).then_inc(loaded, 16)
                sp.dma_start(wd[:], io[f"l{l}_wd"]).then_inc(w_loaded, 16)
                sp.dma_start(wg[:], io[f"l{l}_wg"]).then_inc(w_loaded, 16)
                sp.dma_start(wu[:], io[f"l{l}_wu"]).then_inc(w_loaded, 16)
                if l:
                    for b in range(4):
                        sp.wait_ge(h_ready, 4 * b + 4)
                        sp.dma_start(xs[NSPARSE * P + b * 4 * P:NSPARSE * P + (b + 1) * 4 * P, :].rearrange("(t p) c -> p t c", p=P),
                                     h[:, 4 * b:4 * b + 4, :]).then_inc(shared_sent, 16)
                    sp.wait_ge(shared_sent, 16 * 4)

            @block.scalar
            def _(act):
                row_roots(act, sb, var_ready, root_done)
                with act.Fori(0, NBATCH) as i:
                    for t in range(TPB):
                        act.wait_ge(hT_ps, TPB * i + t + 1)
                        act.activation(hT[:, t, :, :].rearrange("p c q -> p (c q)"), ps[:, t, 0:HID], ACT.Copy).then_inc(hT_sb, 1)
                act.wait_ge(diff, 1)
                act.activation(sm[:, 3, :], sm[:, 2, :], ACT.Exp).then_inc(e2, 1)

            @block.tensor
            def _(pe):
                pe.wait_ge(loaded, 32)
                with pe.Fori(0, NBATCH) as i:
                    for t in range(TPB):
                        pe.wait_ge(h_ready, TPB * i + t + 1)
                        pe.wait_ge(hT_sb, TPB * i + t + 1)
                        for c in range(HC):
                            ins = pe.transpose(ps[:, t, c * P:(c + 1) * P], hcur[:, t, c * P:(c + 1) * P], sb["ident"][:])
                        ins.then_inc(hT_ps, 1)
                        pe.wait_ge(hT_sb, TPB * i + t + 3)
                        for c in range(HC):
                            ins = pe.matmul(ps[:, 2, bass.ds((TPB * i + t) * NE, NE)], hT[:, t, c, :], wr[:, c, :], start=(c == 0), stop=(c == HC - 1))
                        ins.then_inc(logits, 1)
                pe.wait_ge(masks, 1)
                m = rk[:, 4, :, :].rearrange("p t e -> p (t e)")
                pe.matmul(ps[:, 3, 0:P], tri, m, start=True, stop=True)
                pe.matmul(ps[:, 4, 0:P], ones_m, m, start=True, stop=True).then_inc(ranks, 1)

            @block.vector
            def _(dve):
                own = Steps(dve, own_s)
                dve.memset(rk[:, 0, :, :], 0.0).then_inc(mods_free, 2)
                dve.memset(rk[:, 1, :, :], 0.0).then_inc(hT_sb, 2)
                dve.wait_ge(loaded, 32)
                row_scales(dve, own, sb, var_ready, root_done)
                per = TPB * 2 * 2
                with dve.Fori(0, NBATCH // 2) as i:
                    own.start(per * i + ROW_STEPS)
                    for u in range(2):
                        dve.wait_ge(mods[u], 16 * i + 16)
                        for t in range(TPB):
                            tile = 4 * i + 2 * u + t
                            hd = h[:, bass.ds(tile, 1), :].rearrange("p o c -> p (o c)")
                            own.done(normalise(dve, sb, tile, hd))
                            own.done(dve.tensor_tensor(hd, hd, modb[:, u, 1, :], ALU.mult))
                            dve.wait_ge(hT_sb, tile + 1)
                            dve.tensor_tensor(hcur[:, t, :], hd, modb[:, u, 0, :], ALU.add)
                            ins = dve.tensor_tensor(hd, hd, modb[:, u, 0, :], ALU.add)
                            ins.then_inc(h_ready, 1)
                        dve.wait_ge(h_ready, 4 * i + 2 * u + 2)
                        dve.memset(ecmp[:, 0:1], 0.0).then_inc(mods_free, 1)
                own.start(per * (NBATCH // 2) + ROW_STEPS)
                dve.wait_ge(logits, TILES)
                v = lambda k: rk[:, k, :, :]
                bc = lambda k: sm[:, k, :].rearrange("p (t o) -> p t o", o=1).to_broadcast([P, TILES, NE])
                rev_b = rev.rearrange("p (o e) -> p o e", o=1).to_broadcast([P, TILES, NE])
                own.done(dve.tensor_copy(v(0).rearrange("p t e -> p (t e)"), ps[:, 2, 0:P]))
                for n in range(2):
                    own.done(dve.tensor_reduce(sm[:, n, :], v(0), AX, ALU.max))
                    own.done(dve.tensor_tensor(v(1), v(0), bc(n), ALU.is_equal))
                    own.done(dve.tensor_tensor(v(1), v(1), rev_b, ALU.mult))
                    own.done(dve.tensor_reduce(sm[:, 4, :], v(1), AX, ALU.max))
                    own.done(dve.tensor_tensor(v(2 + n), bc(4), rev_b, ALU.is_equal))
                    if n == 0:
                        own.done(dve.scalar_tensor_tensor(v(0), v(2), -3.0e38, v(0), ALU.mult, ALU.add))
                dve.tensor_tensor(v(4), v(2), v(3), ALU.add).then_inc(masks, 1)
                dve.tensor_tensor(sm[:, 2, :], sm[:, 1, :], sm[:, 0, :], ALU.subtract).then_inc(diff, 1)
                dve.wait_ge(e2, 1)
                own.done(dve.tensor_scalar(sm[:, 5, :], sm[:, 3, :], 1.0, None, ALU.add))
                own.done(dve.reciprocal(prob[:, 0, :], sm[:, 5, :]))
                own.done(dve.tensor_tensor(prob[:, 1, :], prob[:, 0, :], sm[:, 3, :], ALU.mult))
                dve.wait_ge(ranks, 1)
                own.done(dve.tensor_copy(v(5).rearrange("p t e -> p (t e)"), ps[:, 4, 0:P]))
                a, b = 5, 6
                for d in (1, 2, 4, 8):
                    dve.tensor_copy(rk[:, b, 0:d, :], rk[:, a, 0:d, :])
                    own.done(dve.tensor_tensor(rk[:, b, d:, :], rk[:, a, d:, :], rk[:, a, 0:TILES - d, :], ALU.add))
                    a, b = b, a
                cnt = rk[:, a, TILES - 1, :]
                ec = ecmp[:].rearrange("p (e k) -> p e k", e=NE)
                own.done(dve.tensor_tensor(ec, cnt.rearrange("p (e o) -> p e o", o=1).to_broadcast([P, NE, TILES]),
                                           thr.rearrange("p (o k) -> p o k", o=1).to_broadcast([P, NE, TILES]), ALU.is_gt))
                own.done(dve.tensor_reduce(ex[:, 0, :], ec, AX, ALU.add))
                for d, ea, eb in ((1, 0, 1), (2, 1, 2), (4, 2, 1)):
                    dve.tensor_copy(ex[:, eb, 0:d], ex[:, ea, 0:d])
                    own.done(dve.tensor_tensor(ex[:, eb, d:], ex[:, ea, d:], ex[:, ea, 0:NE - d], ALU.add))
                incl = ex[:, 1, :]
                own.done(dve.memset(ex[:, 3, 0:1], 0.0))
                own.done(dve.tensor_scalar(ex[:, 3, 1:NE], incl[:, 0:NE - 1], float(P), None, ALU.mult))
                own.done(dve.tensor_tensor(v(7), ex[:, 3, :].rearrange("p (o e) -> p o e", o=1).to_broadcast([P, TILES, NE]),
                                           ps[:, 3, 0:P].rearrange("p (t e) -> p t e", e=NE), ALU.add))
                own.done(dve.tensor_tensor(rk[:, 7, 1:, :], rk[:, 7, 1:, :], rk[:, a, 0:TILES - 1, :], ALU.add))
                for n in range(2):
                    own.done(dve.tensor_tensor(v(8), v(7), v(2 + n), ALU.mult))
                    own.done(dve.tensor_reduce(sm[:, 6 + n, :], v(8), AX, ALU.add))
                    own.done(dve.tensor_copy(pos[:, n, :], sm[:, 6 + n, :]))
                dve.memset(ecmp[:, 0:1], 0.0).then_inc(pos_ready, 1)
                own.done(dve.tensor_tensor(ejc[:, :, 0:NE - 1],
                                           tile_no.rearrange("p (j o) -> p j o", o=1).to_broadcast([1, NSPARSE, NE - 1]),
                                           incl[0:1, 0:NE - 1].rearrange("p (o e) -> p o e", o=1).to_broadcast([1, NSPARSE, NE - 1]), ALU.is_ge))
                if l:
                    own.done(dve.memset(ejs[:, NSPARSE:nt], float(NE)))
                own.done(dve.tensor_reduce(ejs[:, 0:NSPARSE], ejc[:, :, 0:NE - 1], AX, ALU.add))
                own.done(dve.tensor_copy(eid[:], ejs[:]))

            @block.gpsimd
            def _(pool):
                with pool.Fori(0, NBATCH // 2) as i:
                    for u in range(2):
                        pool.wait_ge(mods_free, 2 * i + u + 1)
                        pool.dma_start(modb[:, u, :, :].rearrange("p k c -> p (k c)"),
                                       modd[l, bass.ds(2 * i + u, 1), SB * HID:(CB + 1) * HID].to_broadcast([P, 2 * HID])).then_inc(mods[u], 16)
                pool.wait_ge(pos_ready, 1)
                for t in range(TILES):
                    for n in range(2):
                        pool.indirect_dma_start(xs[0:NSPARSE * P, :], bass.IndirectOffsetOnAxis(ap=pos[:, n, t:t + 1], axis=0),
                                                h[:, t, :], None, bounds_check=NSPARSE * P - 1).then_inc(sent, 16)
                pool.wait_ge(sent, 16 * 2 * TILES)

        with ExitStack() as ec:
            t_ = lambda n, shape, dt=F32: ec.enter_context(nc.sbuf_tensor(f"e{l}_{n}", shape, dt))
            part_sems = Sems(nc, ec)
            r = lambda n, part_sems=part_sems: part_sems(f"e{l}_{n}")
            xin = t_("xin", [P, 2, HID])
            xT = t_("xT", [P, 2, HC, P])
            sg = t_("sg", [P, F])
            a = t_("a", [P, 2, FP])
            aT = t_("aT", [P, FC, P])
            yo = t_("yo", [P, 2, HID])
            ps = ec.enter_context(nc.psum_tensor(f"e{l}_ps", [P, 8, 512], F32))
            pad_zero, x_loaded, xT_ps, xT_sb, g_ps, u_ps, silu_done, a_ready, aT_ps, aT_act, aT_dve, y_ps, y_sb, y_st = (
                r("pad_zero"), [r("x_loaded0"), r("x_loaded1")], r("xT_ps"), r("xT_sb"), r("g_ps"), r("u_ps"), r("silu"), r("a_ready"), r("aT_ps"),
                r("aT_act"), r("aT_dve"), r("y_ps"), r("y_sb"), [r("y_st0"), r("y_st1")])
            block = ec.enter_context(nc.Block())
            NA = min(FC, 4)

            assert nt % 2 == 1

            @block.sync
            def _(sp):
                def load(j, u):
                    src = xs[bass.ds(j * P, P), :] if not isinstance(j, int) else xs[j * P:(j + 1) * P, :]
                    sp.dma_start(xin[:, u, :], src).then_inc(x_loaded[u], 16)
                load(0, 0)
                load(1, 1)
                with sp.Fori(0, (nt - 1) // 2) as i:
                    for u in (0, 1):
                        sp.wait_ge(xT_ps, 2 * i + u + 1)
                        load(2 * i + u + 2, u)
                        sp.wait_ge(y_sb, 2 * i + u + 2)
                        sp.dma_start(ys[bass.ds((2 * i + u) * P, P), :], yo[:, u, :]).then_inc(y_st[u], 16)
                sp.wait_ge(y_sb, nt + 1)
                sp.dma_start(ys[(nt - 1) * P:nt * P, :], yo[:, 0, :]).then_inc(y_st[0], 16)
                sp.wait_ge(y_st[0], 16 * ((nt + 1) // 2))
                sp.wait_ge(y_st[1], 16 * ((nt - 1) // 2))
                sp.wait_ge(x_loaded[1], 16 * ((nt + 1) // 2))

            @block.tensor
            def _(pe):
                def rows(j, u, loads):
                    pe.wait_ge(x_loaded[u], loads)
                    pe.wait_ge(xT_sb, j + 1)
                    for c in range(HC):
                        ins = pe.transpose(ps[:, 6, c * P:(c + 1) * P], xin[:, u, c * P:(c + 1) * P], sb["ident"][:])
                    ins.then_inc(xT_ps, 1)

                def gate_up(j, u):
                    ej = pe.value_load(eid[0:1, bass.ds(j, 1)] if not isinstance(j, int) else eid[0:1, j:j + 1], min_val=0, max_val=ne - 1)
                    pe.wait_ge(xT_sb, j + 2)
                    for n in range(2):
                        for w, bank, signal in ((wg, n, g_ps), (wu, 2 + n, u_ps)):
                            for c in range(HC):
                                ins = pe.matmul(ps[:, bank, 0:half], xT[:, u, c, :],
                                                w[:, c, bass.ds(ej, 1), n * half:(n + 1) * half].rearrange("p o f -> p (o f)"),
                                                start=(c == 0), stop=(c == HC - 1))
                            ins.then_inc(signal, 1)

                def turn(j, u):
                    pe.wait_ge(a_ready, 2 * j + 4)
                    for k in range(FC):
                        ins = pe.transpose(ps[:, 4 + k // 4, (k % 4) * P:(k % 4 + 1) * P], a[:, u, k * P:(k + 1) * P], sb["ident"][:])
                    ins.then_inc(aT_ps, 1)

                def down(j, u):
                    ej = pe.value_load(eid[0:1, bass.ds(j, 1)] if not isinstance(j, int) else eid[0:1, j:j + 1], min_val=0, max_val=ne - 1)
                    pe.wait_ge(aT_act, j + 1)
                    if FC > 4:
                        pe.wait_ge(aT_dve, j + 1)
                    pe.wait_ge(y_sb, j + 1)
                    for k in range(FC):
                        ins = pe.matmul(ps[:, 7, 0:HID], aT[:, k, :], wd[:, bass.ds(ej * FC + k, 1), :].rearrange("p o c -> p (o c)"),
                                        start=(k == 0), stop=(k == FC - 1))
                    ins.then_inc(y_ps, 1)

                pe.wait_ge(w_loaded, 48)
                pe.wait_ge(pad_zero, 1)
                rows(0, 0, 16)
                gate_up(0, 0)
                rows(1, 1, 16)
                with pe.Fori(0, (nt - 1) // 2) as i:
                    turn(2 * i, 0)
                    gate_up(2 * i + 1, 1)
                    rows(2 * i + 2, 0, 16 * i + 32)
                    down(2 * i, 0)
                    turn(2 * i + 1, 1)
                    gate_up(2 * i + 2, 0)
                    rows(2 * i + 3, 1, 16 * i + 32)
                    down(2 * i + 1, 1)
                turn(nt - 1, 0)
                down(nt - 1, 0)

            @block.scalar
            def _(act):
                def xt(j, u):
                    act.wait_ge(xT_ps, j + 1)
                    act.activation(xT[:, u, :, :].rearrange("p c q -> p (c q)"), ps[:, 6, 0:HID], ACT.Copy).then_inc(xT_sb, 1)

                def silu(j, u):
                    for n in range(2):
                        act.wait_ge(g_ps, 2 * j + n + 1)
                        act.wait_ge(a_ready, 2 * j + n + 1)
                        act.activation(sg[:, n * half:(n + 1) * half], ps[:, n, 0:half], ACT.Silu).then_inc(silu_done, 1)

                def at(j):
                    act.wait_ge(aT_ps, j + 1)
                    act.activation(aT[:, 0:NA, :].rearrange("p k q -> p (k q)"), ps[:, 4, 0:NA * P], ACT.Copy).then_inc(aT_act, 1)

                xt(0, 0)
                silu(0, 0)
                xt(1, 1)
                with act.Fori(0, (nt - 1) // 2) as i:
                    at(2 * i)
                    silu(2 * i + 1, 1)
                    xt(2 * i + 2, 0)
                    at(2 * i + 1)
                    silu(2 * i + 2, 0)
                    xt(2 * i + 3, 1)
                at(nt - 1)

            @block.vector
            def _(dve):
                dve.memset(yo[:, 0, 0:1], 0.0).then_inc(a_ready, 2)
                dve.memset(yo[:, 0, 1:2], 0.0).then_inc(xT_sb, 1)
                dve.memset(yo[:, 0, 2:3], 0.0).then_inc(y_sb, 1)
                dve.memset(a[:], 0.0).then_inc(pad_zero, 1)
                dve.wait_ge(pad_zero, 1)

                def mul(j, u):
                    for n in range(2):
                        dve.wait_ge(silu_done, 2 * j + n + 1)
                        dve.wait_ge(u_ps, 2 * j + n + 1)
                        dve.tensor_tensor(a[:, u, n * half:(n + 1) * half], sg[:, n * half:(n + 1) * half], ps[:, 2 + n, 0:half],
                                          ALU.mult).then_inc(a_ready, 1)

                def at(j):
                    if FC > 4:
                        dve.wait_ge(aT_ps, j + 1)
                        dve.tensor_copy(aT[:, 4:FC, :].rearrange("p k q -> p (k q)"), ps[:, 5, 0:(FC - 4) * P]).then_inc(aT_dve, 1)

                def y(j, u, stores=None):
                    dve.wait_ge(y_ps, j + 1)
                    if stores is not None:
                        dve.wait_ge(y_st[u], stores)
                    dve.tensor_copy(yo[:, u, :], ps[:, 7, 0:HID]).then_inc(y_sb, 1)

                mul(0, 0)
                at(0)
                mul(1, 1)
                y(0, 0)
                at(1)
                mul(2, 0)
                y(1, 1)
                with dve.Fori(1, (nt - 1) // 2) as i:
                    at(2 * i)
                    mul(2 * i + 1, 1)
                    y(2 * i, 0, 16 * i)
                    at(2 * i + 1)
                    mul(2 * i + 2, 0)
                    y(2 * i + 1, 1, 16 * i)
                at(nt - 1)
                y(nt - 1, 0, 16 * ((nt - 1) // 2))

        with ExitStack() as fc:
            t_ = lambda n, shape, dt=F32: fc.enter_context(nc.sbuf_tensor(f"c{l}_{n}", shape, dt))
            part_sems = Sems(nc, fc)
            r = lambda n, part_sems=part_sems: part_sems(f"c{l}_{n}")
            g = t_("g", [P, 4, 2, HID])
            ysh = t_("ysh", [P, 4, HID])
            gb = t_("gb", [P, NBATCH, HID])
            tmp = t_("tmp", [P, 2, HID])
            got, got_shared = [r(f"got{n}") for n in range(4)], [r(f"got_shared{n}") for n in range(4)]
            gb_loaded, x_new, own_s, out_st = r("gb_loaded"), r("x_new"), r("own"), r("out_st")
            block = fc.enter_context(nc.Block())

            @block.sync
            def _(sp):
                sp.dma_start(gb[:], modd[l:l + 1, :, GB * HID:(GB + 1) * HID].to_broadcast([P, NBATCH, HID])).then_inc(gb_loaded, 16)
                if l:
                    for t in range(TILES):
                        if t >= 4:
                            sp.wait_ge(x_new, t - 3)
                        sp.dma_start(ysh[:, t % 4, :], ys[(NSPARSE + t) * P:(NSPARSE + t + 1) * P, :]).then_inc(got_shared[t % 4], 16)
                    for t in range(0, TILES, 2):
                        sp.wait_ge(x_new, t + 2)
                        sp.dma_start(out[t * P:(t + 2) * P, :].rearrange("(t p) c -> p t c", p=P), sb["x"][:, t:t + 2, :]).then_inc(out_st, 16)
                    sp.wait_ge(out_st, 16 * TILES // 2)

            @block.gpsimd
            def _(pool):
                for t in range(TILES):
                    if t >= 4:
                        pool.wait_ge(x_new, t - 3)
                    for n in range(2):
                        pool.indirect_dma_start(g[:, t % 4, n, :], None, ys[0:NSPARSE * P, :],
                                                bass.IndirectOffsetOnAxis(ap=pos[:, n, t:t + 1], axis=0),
                                                bounds_check=NSPARSE * P - 1).then_inc(got[t % 4], 16)

            @block.vector
            def _(dve):
                own = Steps(dve, own_s)
                dve.wait_ge(gb_loaded, 16)
                for t in range(TILES):
                    k = t % 4
                    dve.wait_ge(got[k], 32 * (t // 4 + 1))
                    if l:
                        dve.wait_ge(got_shared[k], 16 * (t // 4 + 1))
                    acc = tmp[:, t % 2, :]
                    own.done(dve.tensor_scalar(acc, g[:, k, 0, :], prob[:, 0, t:t + 1], None, ALU.mult))
                    own.done(dve.scalar_tensor_tensor(acc, g[:, k, 1, :], prob[:, 1, t:t + 1], acc, ALU.mult, ALU.add))
                    if l:
                        own.done(dve.tensor_tensor(acc, acc, ysh[:, k, :], ALU.add))
                    own.done(dve.tensor_tensor(acc, acc, gb[:, t // TPB, :], ALU.mult))
                    dve.tensor_tensor(sb["x"][:, t, :], sb["x"][:, t, :], acc, ALU.add).then_inc(x_new, 1)


def program(nc, io, out):
    with ExitStack() as ctx:
        sb = {
            "x": ctx.enter_context(nc.sbuf_tensor("x_tok", [P, TILES, HID], F32)),
            "ident": ctx.enter_context(nc.sbuf_tensor("ident_sb", [P, P], F32)),
            "stats": ctx.enter_context(nc.sbuf_tensor("row_stats", [P, TILES, 6], F32)),
            "mv": ctx.enter_context(nc.sbuf_tensor("row_mv", [P, TILES, 2], F32)),
            "var": ctx.enter_context(nc.sbuf_tensor("row_var", [P, TILES], F32)),
            "root": ctx.enter_context(nc.sbuf_tensor("row_root", [P, TILES], F32)),
            "rstd": ctx.enter_context(nc.sbuf_tensor("row_rstd", [P, TILES], F32)),
            "modT": ctx.enter_context(nc.sbuf_tensor("modT", [P, 2, 4, NBATCH], F32)),
        }
        modd = nc.dram_tensor("mod_rows", [2, NBATCH, 6 * HID], F32, kind="Internal").ap()
        xs = [nc.dram_tensor(f"xs{l}", [(NSPARSE + l * TILES + 1) * P, HID], F32, kind="Internal").ap() for l in range(2)]
        ys = [nc.dram_tensor(f"ys{l}", [(NSPARSE + l * TILES) * P, HID], F32, kind="Internal").ap() for l in range(2)]
        setup(nc, io, sb, modd, xs)
        attention0(nc, io, sb, modd)
        mixture(nc, io, sb, modd, 0, xs[0], ys[0], None)
        attention1(nc, io, sb, modd)
        mixture(nc, io, sb, modd, 1, xs[1], ys[1], out)


def layout(i):
    f = np.float32
    a = {k: np.asarray(v) for k, v in i.items()}
    o = {}
    o["x"] = a["L0_attn_hidden_states"].reshape(TOK, HID)
    chunks = lambda w: np.ascontiguousarray(w.reshape(-1, P, w.shape[1]).transpose(1, 0, 2))
    o["cT"] = np.ascontiguousarray(np.stack([chunks(a[f"L{l}_c"].T) for l in range(2)], 1))
    o["wmod"] = np.ascontiguousarray(np.stack([chunks(a[f"L{l}_wmod"]) for l in range(2)], 1))
    o["ident"] = np.eye(P, dtype=f)
    cst = np.zeros((P, 2 * P + 96), f)
    cst[:, 0:P] = np.triu(np.ones((P, P), f), 1)
    cst[:, P:2 * P] = 1.0
    cst[:, 2 * P:2 * P + NE] = np.arange(NE, 0, -1)
    cst[:, 2 * P + 16:2 * P + 32] = np.arange(TILES) * P
    cst[:, 2 * P + 32:2 * P + 32 + NSPARSE] = np.arange(NSPARSE)
    o["cst"] = cst
    heads = lambda w: np.ascontiguousarray(w.reshape(NH, D0, -1).transpose(1, 0, 2))
    o["l0_wuq"], o["l0_wuk"], o["l0_wuv"] = (heads(a[f"L0_attn_W_{k}_w"]) for k in ("UQ", "UK", "UV"))
    o["l0_woT"] = heads(a["L0_attn_W_O_w"].T)
    o["l0_bup"] = np.ascontiguousarray(np.stack([a[f"L0_attn_W_{k}_b"].reshape(NH, D0).T for k in ("UQ", "UV")], 1))
    dq, dkv = a["L0_attn_W_DQ_w"].T, a["L0_attn_W_DKV_w"].T
    o["l0_wlat"] = chunks(np.concatenate([dq, dkv, dkv], 1))
    bl = np.zeros((P, 3), f)
    bl[:, 0] = a["L0_attn_W_DQ_b"][:P]
    bl[0:QC - P, 1] = a["L0_attn_W_DQ_b"][P:]
    bl[0:KVC, 2] = a["L0_attn_W_DKV_b"]
    bl[KVC:, 2] = a["L0_attn_W_DKV_b"]
    o["l0_blat"] = bl
    o["l0_bo"] = a["L0_attn_W_O_b"].reshape(1, HID)
    o["l0_wr"] = chunks(a["L0_ffn_router_w"].T)
    ffn = lambda w: np.ascontiguousarray(w.reshape(w.shape[0], HC, P, -1).transpose(2, 1, 0, 3))
    o["l0_wg"], o["l0_wu"] = (ffn(a[f"L0_ffn_{k}_w"].transpose(0, 2, 1)) for k in ("gate", "up"))
    wd = np.zeros((NE, F0C * P, HID), f)
    wd[:, 0:F0, :] = a["L0_ffn_down_w"].transpose(0, 2, 1)
    o["l0_wd"] = np.ascontiguousarray(wd.reshape(NE * F0C, P, HID).transpose(1, 0, 2))
    o["l1_wlat"] = chunks(np.concatenate([a["L1_attn_Wc"], a["L1_attn_Wckv"]], 1))
    o["l1_blat"] = np.concatenate([a["L1_attn_bc"], a["L1_attn_bckv"]]).reshape(P, 1)
    wqkv = np.zeros((P, 896), f)
    wqkv[0:64, 0:256], wqkv[0:64, 256:384] = a["L1_attn_Wcq"], a["L1_attn_Wqr"]
    wqkv[64:128, 384:640], wqkv[64:128, 640:896] = a["L1_attn_Wck"], a["L1_attn_Wv"]
    o["l1_wqkv"] = wqkv
    o["l1_wkr"] = chunks(a["L1_attn_Wkr"])
    o["l1_btok"] = np.concatenate([a[f"L1_attn_{k}"] for k in ("bcq", "bqr", "bkr", "bck", "bv")]).reshape(1, 1024)
    o["l1_wo"] = chunks(a["L1_attn_Wo"])
    o["l1_bo"] = a["L1_attn_bo"].reshape(1, HID)
    inv = (1.0 / 10000.0 ** (np.arange(0, DRH, 2, dtype=f) / DRH)).astype(f)
    fr = np.arange(SEQ, dtype=f)[:, None] * inv[None, :]
    cos, sin = np.cos(fr).astype(f), np.sin(fr).astype(f)
    tab = np.stack([np.concatenate([cos, cos], 1), np.concatenate([-sin, sin], 1)])
    o["l1_rope"] = np.ascontiguousarray(tab.reshape(2, TPB, P, DRH).transpose(2, 0, 1, 3))
    o["l1_wr"] = chunks(a["L1_ffn_gate_w"])
    gu = np.concatenate([a["L1_ffn_w_gate_up"], a["L1_ffn_shared_gate_up"][None]], 0)
    o["l1_wg"], o["l1_wu"] = ffn(gu[:, :, 0:F1]), ffn(gu[:, :, F1:])
    dn = np.concatenate([a["L1_ffn_w_down"], a["L1_ffn_shared_down"][None]], 0)
    o["l1_wd"] = np.ascontiguousarray(dn.reshape((NE + 1) * F1C, P, HID).transpose(1, 0, 2))
    return {k: np.ascontiguousarray(v, dtype=f) for k, v in o.items()}


def kernel(**inputs):
    import concourse.bacc as bacc
    from concourse.bass_utils import run_bass_kernel_spmd

    nc = bacc.Bacc("TRN2", target_bir_lowering=False, num_devices=1)
    arrays = layout(inputs)
    io = {k: nc.dram_tensor(f"in_{k}", v.shape, F32, kind="ExternalInput").ap() for k, v in arrays.items()}
    out = nc.dram_tensor("out_x", (TOK, HID), F32, kind="ExternalOutput").ap()
    program(nc, io, out)
    r = run_bass_kernel_spmd(nc, [{f"in_{k}": v for k, v in arrays.items()}], core_ids=[0])
    return r.results[0]["out_x"].reshape(NBATCH, SEQ, HID)
```

```python
from contextlib import ExitStack

import numpy as np
import concourse.bass as bass
from concourse import mybir

F32 = mybir.dt.float32
U32 = mybir.dt.uint32
ALU = mybir.AluOpType
ACT = mybir.ActivationFunctionType
AX = mybir.AxisListType.X

P = 128
NBATCH, SEQ, HID = 8, 256, 256
TOK = NBATCH * SEQ
TILES = TOK // P
TPB = SEQ // P
HC = HID // P
NH = 16
QC, KVC, D0 = 192, 64, 128
SCALE0 = 1.0 / float(np.sqrt(D0))
DH, DRH = 16, 8
DQK = DH + DRH
POOL_S, POOL_V = 12, 11
SCALE1 = 1.0 / float(np.sqrt(DH + DRH))
NE = 8
F0, F1 = 688, 512
F0C = 6
F1C = 4
NSPARSE = (2 * TOK + NE * (P - 1)) // P
EPS = 1e-5
SA, CA, GA, SB, CB, GB = range(6)
CT_SA, CT_CA = 0, 2


class Sems:

    def __init__(self, nc, ctx):
        self.nc, self.all = nc, []
        ctx.callback(self.free)

    def free(self):
        self.nc.clear_and_free_semaphores(self.all)
        self.nc.all_engine_barrier()

    def __call__(self, name):
        self.all.append(self.nc.alloc_semaphore(name))
        return self.all[-1]


class Steps:

    def __init__(self, eng, sem):
        self.eng, self.sem, self.base, self.n = eng, sem, 0, 0

    def start(self, base):
        self.base, self.n = base, 0

    def done(self, ins):
        self.n += 1
        ins.then_inc(self.sem, 1)
        self.eng.wait_ge(self.sem, self.base + self.n)


ROW_STEPS = 6


def row_scales(dve, own, sb, var_ready, root_done):
    var, rstd, t = sb["var"][:], sb["rstd"][:], sb["root"][:]
    for k in range(TILES):
        ins = dve.bn_stats(sb["stats"][:, k, :], sb["x"][:, k, :])
    own.done(ins)
    for k in range(TILES):
        ins = dve.bn_aggr(sb["mv"][:, k, :], sb["stats"][:, k, :])
    own.done(ins)
    dve.tensor_scalar(var, sb["mv"][:, :, 1], EPS, None, ALU.add).then_inc(var_ready, 1)
    dve.wait_ge(root_done, 1)
    own.done(dve.reciprocal(rstd, t))
    own.done(dve.tensor_tensor(t, rstd, rstd, ALU.mult))
    own.done(dve.tensor_tensor(t, t, var, ALU.mult))
    own.done(dve.tensor_scalar(t, t, -0.5, 1.5, ALU.mult, ALU.add))
    dve.tensor_tensor(rstd, rstd, t, ALU.mult).then_inc(root_done, 1)
    dve.wait_ge(root_done, 2)


def row_roots(act, sb, var_ready, root_done):
    act.wait_ge(var_ready, 1)
    act.activation(sb["root"][:], sb["var"][:], ACT.Sqrt).then_inc(root_done, 1)


def row(buf, k):
    return buf[:, bass.ds(k, 1), :].rearrange("p o c -> p (o c)")


def normalise(dve, sb, tile, xn):
    return dve.tensor_scalar(xn, sb["x"][:, bass.ds(tile, 1), :].rearrange("p o c -> p (o c)"),
                             sb["mv"][:, bass.ds(tile, 1), 0], sb["rstd"][:, bass.ds(tile, 1)], ALU.subtract, ALU.mult)


def setup(nc, io, sb, modd, xs_dram):
    with ExitStack() as ctx:
        cT = ctx.enter_context(nc.sbuf_tensor("cT", [P, 2, HC, NBATCH], F32))
        wmod = ctx.enter_context(nc.sbuf_tensor("wmod", [P, 2, HC, 6 * HID], F32))
        mod = ctx.enter_context(nc.sbuf_tensor("mod", [NBATCH, 2, 6 * HID], F32))
        zero = ctx.enter_context(nc.sbuf_tensor("zero", [P, 4 * HID], F32))
        ps = ctx.enter_context(nc.psum_tensor("mod_ps", [P, 8, 512], F32))
        sem = Sems(nc, ctx)
        loaded, ident_loaded, zeroed, cleared = sem("su_loaded"), sem("su_ident"), sem("su_zeroed"), sem("su_cleared")
        silu_done, mod_ps_done, mod_rows, mod_cols_ps, mod_cols, stored, own_s = (
            sem("su_silu"), sem("su_mod_ps"), sem("su_mod_rows"), sem("su_cols_ps"), sem("su_cols"), sem("su_stored"), sem("su_own"))
        block = ctx.enter_context(nc.Block())

        @block.sync
        def _(sp):
            sp.dma_start(cT[:], io["cT"]).then_inc(loaded, 16)
            sp.dma_start(wmod[:], io["wmod"]).then_inc(loaded, 16)
            sp.dma_start(sb["ident"][:], io["ident"]).then_inc(ident_loaded, 16)
            sp.dma_start(sb["x"][:], io["x"].rearrange("(t p) c -> p t c", p=P)).then_inc(ident_loaded, 16)
            sp.wait_ge(zeroed, 1)
            for l in range(2):
                v = xs_dram[l][0:(NSPARSE + 1) * P, :].rearrange("(n p r) c -> n p (r c)", p=P, r=4)
                for n in range((NSPARSE + 1) // 4):
                    sp.dma_start(v[n], zero[:]).then_inc(cleared, 16)
            sp.dma_start(xs_dram[1][(NSPARSE + TILES) * P:(NSPARSE + TILES + 1) * P, :], zero[:, 0:HID]).then_inc(cleared, 16)
            sp.wait_ge(mod_rows, 1)
            sp.dma_start(modd.rearrange("l b n -> b l n"), mod[:]).then_inc(stored, 16)
            sp.wait_ge(cleared, 16 * (2 * ((NSPARSE + 1) // 4) + 1))
            sp.wait_ge(stored, 16)
            sp.wait_ge(ident_loaded, 32)

        @block.gpsimd
        def _(pool):
            pool.memset(zero[:], 0.0).then_inc(zeroed, 1)

        @block.scalar
        def _(act):
            act.wait_ge(loaded, 32)
            act.activation(cT[:], cT[:], ACT.Silu).then_inc(silu_done, 1)

        @block.tensor
        def _(pe):
            pe.wait_ge(silu_done, 1)
            for l in range(2):
                for n in range(3):
                    for c in range(HC):
                        last = pe.matmul(ps[0:NBATCH, 3 * l + n, :], cT[:, l, c, :], wmod[:, l, c, n * 512:(n + 1) * 512],
                                         start=(c == 0), stop=(c == HC - 1))
            last.then_inc(mod_ps_done, 1)
            pe.wait_ge(ident_loaded, 32)
            pe.wait_ge(mod_rows, 1)
            for l in range(2):
                for j in range(4):
                    src = mod[:, l, j * P:(j + 1) * P]
                    last = pe.transpose(ps[:, 6, (l * 4 + j) * NBATCH:(l * 4 + j + 1) * NBATCH], src, sb["ident"][0:NBATCH, 0:NBATCH])
            last.then_inc(mod_cols_ps, 1)

        @block.vector
        def _(dve):
            own = Steps(dve, own_s)
            dve.wait_ge(mod_ps_done, 1)
            for l in range(2):
                own.done(dve.tensor_copy(mod[:, l, :].rearrange("p (n c) -> p n c", n=3), ps[0:NBATCH, 3 * l:3 * l + 3, :]))
            for l in range(2):
                for k in (CA, CB):
                    v = mod[:, l, k * HID:(k + 1) * HID]
                    own.done(dve.tensor_scalar(v, v, 1.0, None, ALU.add))
                for k in (GA, GB):
                    v = mod[:, l, k * HID:(k + 1) * HID]
                    s = ps[0:NBATCH, 7, 0:HID]
                    own.done(dve.tensor_scalar(s, v, 0.0, 2.0, ALU.is_ge, ALU.mult))
                    own.done(dve.scalar_tensor_tensor(v, v, -1.0, v, ALU.mult, ALU.max))
                    own.done(dve.tensor_scalar(v, v, 0.25, None, ALU.max))
                    ins = dve.scalar_tensor_tensor(v, s, -1.0, v, ALU.add, ALU.mult)
                    if (l, k) == (1, GB):
                        ins.then_inc(mod_rows, 1)
                    else:
                        own.done(ins)
            dve.wait_ge(mod_cols_ps, 1)
            dve.tensor_copy(sb["modT"][:].rearrange("p l j b -> p (l j b)"), ps[:, 6, 0:2 * 4 * NBATCH]).then_inc(mod_cols, 1)
            dve.wait_ge(mod_cols, 1)


STEPS = 8


def attention0(nc, io, sb, modd):
    with ExitStack() as ctx:
        s = lambda n, shape: ctx.enter_context(nc.sbuf_tensor(f"l0_{n}", shape, F32))
        sems = Sems(nc, ctx)
        q = lambda n: sems(f"l0_{n}")
        wlat = s("wlat", [P, HC, QC + 2 * KVC])
        blat = s("blat", [P, 3])
        aq = s("aq", [P, 2, NH * KVC])
        aqb = s("aqb", [P, NH // 2])
        wvo = s("wvo", [P, NH // 2, HID])
        bo = s("bo", [P, HID])
        ps = ctx.enter_context(nc.psum_tensor("l0_ps", [P, 8, 512], F32))
        ident = sb["ident"]
        var_ready, root_done, own_s, zeroed, ga_loaded, xn_ready, unit_ps, unit_sb = (
            q("var_ready"), q("root_done"), q("own"), q("zeroed"), q("ga_loaded"), q("xn_ready"), q("unit_ps"), q("unit_sb"))
        scores, max_ready, exp_done, prob_ready, pT_ps, pT_act, pT_dve, ctx_ps, ctx_sb, out_ps, out_read = (
            q("scores"), q("max_ready"), q("exp_done"), q("prob_ready"), q("pT_ps"), q("pT_act"), q("pT_dve"), q("ctx_ps"), q("ctx_sb"),
            q("out_ps"), q("out_read"))

        with ExitStack() as pre:
            t = lambda n, shape: pre.enter_context(nc.sbuf_tensor(f"l0_{n}", shape, F32))
            pre_sems = Sems(nc, pre)
            r = lambda n: pre_sems(f"l0_{n}")
            wuq, wuk, wuv, woT = t("wuq", [P, NH, QC]), t("wuk", [P, NH, KVC]), t("wuv", [P, NH, KVC]), t("woT", [P, NH, HID])
            bup, bo_row, ones = t("bup", [P, 2, NH]), t("bo_row", [1, 2, HID]), t("ones", [1, P])
            loaded, onesd, fold_ps, fold_sb, bias_row, bias_ps = r("pw_loaded"), r("pw_ones"), r("fold_ps"), r("fold_sb"), r("bias_row"), r("bias_ps")
            block = pre.enter_context(nc.Block())

            @block.sync
            def _(sp):
                for dst, name in ((wuq, "l0_wuq"), (wuk, "l0_wuk"), (wuv, "l0_wuv"), (woT, "l0_woT"), (bup, "l0_bup"),
                                  (wlat, "l0_wlat"), (blat, "l0_blat")):
                    sp.dma_start(dst[:], io[name]).then_inc(loaded, 16)
                sp.dma_start(bo_row[:, 0, :], io["l0_bo"]).then_inc(loaded, 16)

            @block.tensor
            def _(pe):
                pe.wait_ge(loaded, 16 * 8)
                for h in range(NH):
                    cols = slice((h % 8) * KVC, (h % 8 + 1) * KVC)
                    pe.matmul(ps[:, h // 8, cols], wuq[:, h, 0:P], wuk[:, h, :], start=True, stop=True)
                    pe.matmul(ps[0:QC - P, 2 + h // 8, cols], wuq[:, h, P:QC], wuk[:, h, :], start=True, stop=True)
                    r0 = (h % 2) * KVC
                    ins = pe.matmul(ps[r0:r0 + KVC, 4, h // 2:h // 2 + 1], wuk[:, h, :], bup[:, 0, h:h + 1], start=True, stop=True)
                ins.then_inc(fold_ps, 1)
                pe.wait_ge(fold_sb, 1)
                for h in range(NH):
                    r0, c0 = (h % 2) * KVC, (h // 2 % 2) * HID
                    pe.matmul(ps[r0:r0 + KVC, h // 4, c0:c0 + HID], wuv[:, h, :], woT[:, h, :], start=True, stop=True)
                for h in range(NH):
                    ins = pe.matmul(ps[0:1, 5, 0:HID], bup[:, 1, h:h + 1], woT[:, h, :], start=(h == 0), stop=(h == NH - 1))
                ins.then_inc(fold_ps, 1)
                pe.wait_ge(bias_row, 1)
                pe.matmul(ps[:, 6, 0:HID], ones[:], bo_row[:, 1, :], start=True, stop=True).then_inc(bias_ps, 1)

            @block.vector
            def _(dve):
                dve.memset(ones[:], 1.0).then_inc(onesd, 1)
                dve.wait_ge(fold_ps, 1)
                dve.tensor_copy(aq[:, 0, :].rearrange("p (b c) -> p b c", b=2), ps[:, 0:2, :])
                dve.tensor_copy(aqb[:], ps[:, 4, 0:NH // 2])
                dve.tensor_copy(aq[0:QC - P, 1, :].rearrange("p (b c) -> p b c", b=2), ps[0:QC - P, 2:4, :]).then_inc(fold_sb, 1)
                dve.wait_ge(fold_ps, 2)
                dve.tensor_copy(wvo[:].rearrange("p (b h) c -> p b (h c)", b=4), ps[:, 0:4, :])
                dve.wait_ge(onesd, 1)
                dve.wait_ge(loaded, 16 * 8)
                dve.tensor_tensor(bo_row[:, 1, :], ps[0:1, 5, 0:HID], bo_row[:, 0, :], ALU.add).then_inc(bias_row, 1)
                dve.wait_ge(bias_ps, 1)
                dve.tensor_copy(bo[:], ps[:, 6, 0:HID])

        hT = s("hT", [P, HC, SEQ])
        xn = s("xn", [P, TPB, HID])
        cq = s("cq", [P, 2, SEQ])
        ckv = s("ckv", [P, 2, 2, SEQ])
        ckvt = s("ckvt", [P, 2, TPB, KVC])
        qT = s("qT", [P, 2, NH // 2, SEQ])
        mx, sums, rinv = s("mx", [P, 2, 4]), s("sums", [P, 2, 4]), s("rinv", [P, 2, 4])
        prob = s("prob", [P, 2, 4, SEQ])
        probT = s("probT", [P, 4, TPB, P])
        ctxT = s("ctxT", [P, 2, NH // 2 * P])
        ga = s("ga", [P, NBATCH, HID])
        y = s("y", [P, HID])
        S = lambda st: ps[:, 2 * (st % 2):2 * (st % 2) + 2, :]
        C, O, U = ps[:, 6, 0:2 * P], ps[:, 6, 2 * P:2 * P + HID], ps[:, 7, :]
        block = ctx.enter_context(nc.Block())

        ACT_UNITS, DVE_UNITS = (0, 1, 5, 6, 7), (2, 3, 4)

        def batches(eng, batch):
            batch(0, 0, True, False)
            with eng.Fori(0, NBATCH // 2 - 1) as k:
                batch(2 * k + 1, 1, False, False)
                batch(2 * k + 2, 0, False, False)
            batch(NBATCH - 1, 1, False, True)

        @block.sync
        def _(sp):
            sp.dma_start(ga[:], modd[0:1, :, GA * HID:(GA + 1) * HID].to_broadcast([P, NBATCH, HID])).then_inc(ga_loaded, 16)
            sp.wait_ge(ga_loaded, 16)

        @block.tensor
        def _(pe):
            def unit(i, u, b):
                if u != 3 and not (isinstance(i, int) and STEPS * i + u == 0):
                    pe.wait_ge(unit_sb, STEPS * i + u)
                if u == 0:
                    pe.wait_ge(xn_ready, i + 1)
                    for t in range(TPB):
                        for c in range(HC):
                            ins = pe.transpose(U[:, c * SEQ + t * P:c * SEQ + (t + 1) * P], xn[:, t, c * P:(c + 1) * P], ident[:])
                elif u == 1:
                    for c in range(HC):
                        pe.matmul(U[:, 0:SEQ], wlat[:, c, 0:P], hT[:, c, :], start=(c == 0), stop=(c == HC - 1))
                    for c in range(HC):
                        ins = pe.matmul(U[0:QC - P, SEQ:2 * SEQ], wlat[:, c, P:QC], hT[:, c, :], start=(c == 0), stop=(c == HC - 1))
                elif u == 2:
                    for c in range(HC):
                        ins = pe.matmul(U[:, 0:SEQ], wlat[:, c, QC:QC + P], hT[:, c, :], start=(c == 0), stop=(c == HC - 1))
                elif u == 3:
                    for t in range(TPB):
                        ins = pe.transpose(U[:, t * KVC:(t + 1) * KVC], ckv[0:KVC, b, 0, t * P:(t + 1) * P], ident[0:KVC, 0:KVC])
                else:
                    for n in range(2):
                        p = 2 * (u - 4) + n
                        pe.matmul(U[:, n * SEQ:(n + 1) * SEQ], aq[:, 0, p * P:(p + 1) * P], cq[:, 0, :], start=True, stop=False)
                        ins = pe.matmul(U[:, n * SEQ:(n + 1) * SEQ], aq[0:QC - P, 1, p * P:(p + 1) * P], cq[0:QC - P, 1, :],
                                        start=False, stop=True)
                ins.then_inc(unit_ps, 1)

            def score(st, b):
                for n in range(2):
                    ins = pe.matmul(S(st)[:, n, :], qT[:, b, (st % 4) * 2 + n, (st // 4) * P:(st // 4 + 1) * P],
                                    ckv[:, b, :, :].rearrange("p h k -> p (h k)"), start=True, stop=True)
                ins.then_inc(scores, 1)

            def out(n, half):
                pe.wait_ge(ctx_sb, n + 1)
                for p in range(NH // 2):
                    ins = pe.matmul(O, ctxT[:, half, p * P:(p + 1) * P], wvo[:, p, :], start=(p == 0), stop=(p == NH // 2 - 1))
                ins.then_inc(out_ps, 1)

            def batch(i, b, first, last):
                for st in range(STEPS):
                    n = STEPS * i + st
                    pe.wait_ge(prob_ready, n + 1)
                    for j in range(4):
                        for k in range(TPB):
                            ins = pe.transpose(ps[:, 4 + j // 2, ((j % 2) * TPB + k) * P:((j % 2) * TPB + k + 1) * P],
                                               prob[:, st % 2, j, k * P:(k + 1) * P], ident[:])
                    ins.then_inc(pT_ps, 1)
                    if st % 4 == 0 and not (first and st == 0):
                        out(n - 1, 1 - st // 4)
                    if not (last and st + 2 >= STEPS):
                        ahead = (st + 2) % STEPS
                        if ahead < 4:
                            pe.wait_ge(unit_sb, STEPS * (i + (st + 2) // STEPS) + 4 + ahead + 1)
                        if st == 3 and not last:
                            pe.wait_ge(unit_sb, STEPS * (i + 1) + 3)
                        pe.wait_ge(exp_done, n + 1)
                        score(ahead, (b + (st + 2) // STEPS) % 2)
                    if not last:
                        unit(i + 1, st, 1 - b)
                    pe.wait_ge(pT_act, n + 1)
                    pe.wait_ge(pT_dve, n + 1)
                    if not (first and st == 0):
                        pe.wait_ge(ctx_sb, n)
                    if st % 4 == 0 and not (first and st == 0):
                        pe.wait_ge(out_read, 2 * i + st // 4)
                    for j in range(4):
                        for k in range(TPB):
                            ins = pe.matmul(C[(j % 2) * KVC:(j % 2 + 1) * KVC, j // 2 * P:(j // 2 + 1) * P], ckvt[:, b, k, :],
                                            probT[:, j, k, :], start=(k == 0), stop=(k == TPB - 1))
                    ins.then_inc(ctx_ps, 1)

            pe.wait_ge(zeroed, 1)
            for u in range(STEPS):
                if u == 3:
                    pe.wait_ge(unit_sb, 3)
                unit(0, u, 0)
            pe.wait_ge(unit_sb, STEPS)
            score(0, 0)
            score(1, 0)
            batches(pe, batch)
            out(STEPS * NBATCH - 1, 1)

        @block.scalar
        def _(act):
            def unit(i, u, b):
                act.wait_ge(unit_ps, STEPS * i + u + 1)
                if u == 0:
                    for c in range(HC):
                        ins = act.activation(hT[:, c, :], U[:, c * SEQ:(c + 1) * SEQ], ACT.Identity,
                                             scale=sb["modT"][:, 0, CT_CA + c, bass.ds(i, 1)], bias=sb["modT"][:, 0, CT_SA + c, bass.ds(i, 1)])
                elif u == 1:
                    act.activation(cq[:, 0, :], U[:, 0:SEQ], ACT.Identity, bias=blat[:, 0:1])
                    ins = act.activation(cq[0:QC - P, 1, :], U[0:QC - P, SEQ:2 * SEQ], ACT.Identity, bias=blat[0:QC - P, 1:2])
                else:
                    for n in range(2):
                        p = 2 * (u - 4) + n
                        ins = act.activation(qT[:, b, p, :], U[:, n * SEQ:(n + 1) * SEQ], ACT.Identity, bias=aqb[:, p:p + 1])
                ins.then_inc(unit_sb, 1)

            def exp(n, st):
                act.wait_ge(max_ready, n + 1)
                for j in range(4):
                    ins = act.activation(prob[:, st % 2, j, :], S(st)[:, j // 2, (j % 2) * SEQ:(j % 2 + 1) * SEQ], ACT.Exp,
                                         bias=mx[:, st % 2, j:j + 1], scale=SCALE0, accum_out=sums[:, st % 2, j:j + 1])
                ins.then_inc(exp_done, 1)

            def batch(i, b, first, last):
                for st in range(STEPS):
                    n = STEPS * i + st
                    act.wait_ge(pT_ps, n + 1)
                    act.activation(probT[:, 0:2, :, :].rearrange("p h k q -> p (h k q)"), ps[:, 4, :], ACT.Copy).then_inc(pT_act, 1)
                    if not (last and st + 2 >= STEPS):
                        exp(n + 2, st)
                    if not last and st in ACT_UNITS:
                        unit(i + 1, st, 1 - b)

            row_roots(act, sb, var_ready, root_done)
            for u in ACT_UNITS:
                unit(0, u, 0)
            exp(0, 0)
            exp(1, 1)
            batches(act, batch)

        @block.vector
        def _(dve):
            own = Steps(dve, own_s)

            def rows(i):
                for t in range(TPB):
                    ins = normalise(dve, sb, TPB * i + t, xn[:, t, :])
                ins.then_inc(xn_ready, 1)

            def unit(i, u, b):
                dve.wait_ge(unit_ps, STEPS * i + u + 1)
                if u == 2:
                    for h in range(2):
                        r = slice(h * KVC, (h + 1) * KVC)
                        ins = dve.tensor_scalar(ckv[r, b, h, :], U[r, 0:SEQ], blat[r, 2:3], None, ALU.add)
                elif u == 3:
                    ins = dve.tensor_copy(ckvt[:, b, :, :].rearrange("p t c -> p (t c)"), U[:, 0:TPB * KVC])
                else:
                    for n in range(2):
                        p = 2 * (u - 4) + n
                        ins = dve.tensor_scalar(qT[:, b, p, :], U[:, n * SEQ:(n + 1) * SEQ], aqb[:, p:p + 1], None, ALU.add)
                ins.then_inc(unit_sb, 1)

            def maxima(n, st):
                dve.wait_ge(scores, n + 1)
                own.done(dve.tensor_reduce(mx[:, st % 2, :], S(st).rearrange("p b (h k) -> p (b h) k", h=2), AX, ALU.max))
                dve.tensor_scalar(mx[:, st % 2, :], mx[:, st % 2, :], -SCALE0, None, ALU.mult).then_inc(max_ready, 1)

            def divide(n, st):
                dve.wait_ge(exp_done, n + 1)
                own.done(dve.reciprocal(rinv[:, st % 2, :], sums[:, st % 2, :]))
                for j in range(4):
                    ins = dve.tensor_scalar(prob[:, st % 2, j, :], prob[:, st % 2, j, :], rinv[:, st % 2, j:j + 1], None, ALU.mult)
                ins.then_inc(prob_ready, 1)

            def context(n, st):
                dve.wait_ge(ctx_ps, n + 1)
                dve.tensor_copy(ctxT[:, st // 4 % 2, st % 4 * 2 * P:(st % 4 + 1) * 2 * P], C).then_inc(ctx_sb, 1)

            def add_bias(tile):
                dve.wait_ge(out_ps, tile + 1)
                dve.tensor_tensor(y[:], O, bo[:], ALU.add).then_inc(out_read, 1)

            def residual(tile, i):
                x = row(sb["x"], tile)
                dve.wait_ge(out_read, tile + 1)
                own.done(dve.tensor_tensor(y[:], y[:], row(ga, i), ALU.mult))
                dve.tensor_tensor(x, x, y[:], ALU.add)

            def batch(i, b, first, last):
                if not first:
                    own.start(before + per_batch * (i - 1))
                for st in range(STEPS):
                    n = STEPS * i + st
                    if not (first and st == 0):
                        context(n - 1, st - 1)
                    if st == 0 and not last:
                        rows(i + 1)
                    dve.wait_ge(pT_ps, n + 1)
                    dve.tensor_copy(probT[:, 2:4, :, :].rearrange("p h k q -> p (h k q)"), ps[:, 5, :]).then_inc(pT_dve, 1)
                    if not (last and st == STEPS - 1):
                        divide(n + 1, st + 1)
                    finished = st % 4 == 0 and not (first and st == 0)
                    tile = TPB * i + st // 4 - 1
                    if finished:
                        add_bias(tile)
                    if not (last and st + 2 >= STEPS):
                        maxima(n + 2, st)
                    if finished:
                        residual(tile, i if st else i - 1)
                    if not last and st in DVE_UNITS:
                        unit(i + 1, st, 1 - b)
                if not first:
                    assert last or own.n == per_batch, own.n

            dve.memset(ckv[:], 0.0).then_inc(zeroed, 1)
            row_scales(dve, own, sb, var_ready, root_done)
            dve.wait_ge(ga_loaded, 16)
            dve.wait_ge(zeroed, 1)
            rows(0)
            for u in DVE_UNITS:
                unit(0, u, 0)
            maxima(0, 0)
            maxima(1, 1)
            divide(0, 0)
            per_batch = 2 * STEPS + 2
            before = own.n + per_batch - 1
            batches(dve, batch)
            context(STEPS * NBATCH - 1, STEPS - 1)
            add_bias(TILES - 1)
            residual(TILES - 1, NBATCH - 1)


def attention1(nc, io, sb, modd):
    with ExitStack() as ctx:
        s = lambda n, shape: ctx.enter_context(nc.sbuf_tensor(f"l1_{n}", shape, F32))
        sems = Sems(nc, ctx)
        q = lambda n: sems(f"l1_{n}")
        wlat = s("wlat", [P, HC, P])
        blat = s("blat", [P, 1])
        wqkv = s("wqkv", [P, 384 + 512])
        wkr = s("wkr", [P, HC, P])
        btok = s("btok", [1, 1024])
        bo = s("bo", [1, HID])
        ones = s("ones", [1, P])
        wo = s("wo", [P, HC, HID])
        rope = s("rope", [P, 2, TPB, DRH])
        ga = s("ga", [P, NBATCH, HID])
        shift = s("shift", [P, TILES])
        xn = s("xn", [P, HID])
        hT = s("hT", [P, HC, P])
        cT = s("cT", [P, P])
        raw = s("raw", [P, 2, 2 * NH, DRH])
        qk = s("qk", [P, 2, 2, NH, DQK])
        rt = s("rt", [P, 2, 2 * NH, DRH])
        v = s("v", [P, TILES, DH, NH])
        sprod = s("sprod", [P, 2, NH, NH * DQK])
        vprod = s("vprod", [P, NH, DH * NH])
        sc = s("sc", [P, 2, NH, NH])
        red = s("red", [P, 3, NH])
        o = s("o", [P, NH * DH])
        oT = s("oT", [P, HC, P])
        y = s("y", [P, HID])
        ps = ctx.enter_context(nc.psum_tensor("l1_ps", [P, 8, 512], F32))
        var_ready, root_done, shift_ready, loaded, own_s, onesd = (
            q("var_ready"), q("root_done"), q("shift_ready"), q("loaded"), q("own"), q("ones"))
        xn_ready, xT_ps, hT_sb, lat_ps, lat_sb, tok_ps, tok_sb, qk_ready = (
            q("xn_ready"), q("xT_ps"), q("hT_sb"), q("lat_ps"), q("lat_sb"), q("tok_ps"), q("tok_sb"), q("qk_ready"))
        pool_sprod, dve_sprod, sc_ready, exp_done, p_ready, pool_vprod, o_ready, oT_ps, oT_sb, out_ps, out_read = (
            q("pool_sprod"), q("dve_sprod"), q("sc_ready"), q("exp_done"), q("p_ready"), q("pool_vprod"), q("o_ready"), q("oT_ps"),
            q("oT_sb"), q("out_ps"), q("out_read"))
        block = ctx.enter_context(nc.Block())
        LOADS = 9
        ident = sb["ident"]

        def tiles(eng, turn):
            for t in (0, 1):
                turn(t, t, 0, t == 0, TILES)
            with eng.Fori(1, TILES // 2 - 2) as i:
                turn(2 * i, 0, i, False, TILES)
                turn(2 * i + 1, 1, i, False, TILES)
            for t in range(TILES - 4, TILES):
                turn(t, t % 2, t // 2, False, TILES - 1 - t)

        def score_product(eng, u, a, b):
            n = b - a
            return eng.tensor_tensor(sprod[:, u, a:b, :].rearrange("p i (j d) -> p i j d", j=NH),
                                     qk[:, u, 0, a:b, :].rearrange("p i (o d) -> p i o d", o=1).to_broadcast([P, n, NH, DQK]),
                                     qk[:, u, 1, :, :].rearrange("p (o j) d -> p o j d", o=1).to_broadcast([P, n, NH, DQK]), ALU.mult)

        def value_product(eng, t, u, a, b):
            n = b - a
            return eng.tensor_tensor(vprod[:, a:b, :].rearrange("p i (d j) -> p i d j", d=DH),
                                     sc[:, u, a:b, :].rearrange("p i (o j) -> p i o j", o=1).to_broadcast([P, n, DH, NH]),
                                     v[:, bass.ds(t, 1), :, :].to_broadcast([P, n, DH, NH]), ALU.mult)

        @block.sync
        def _(sp):
            for dst, name in ((wlat, "l1_wlat"), (blat, "l1_blat"), (wqkv, "l1_wqkv"), (wkr, "l1_wkr"), (wo, "l1_wo"), (rope, "l1_rope"),
                              (btok, "l1_btok"), (bo, "l1_bo")):
                sp.dma_start(dst[:], io[name]).then_inc(loaded, 16)
            sp.dma_start(ga[:], modd[1:2, :, GA * HID:(GA + 1) * HID].to_broadcast([P, NBATCH, HID])).then_inc(loaded, 16)

        @block.tensor
        def _(pe):
            def front(t, u):
                bank = 2 + 2 * u
                pe.wait_ge(xn_ready, t + 1)
                for c in range(HC):
                    ins = pe.transpose(ps[:, 0, c * P:(c + 1) * P], xn[:, c * P:(c + 1) * P], ident[:])
                ins.then_inc(xT_ps, 1)
                if not isinstance(t, int) or t > 1:
                    pe.wait_ge(tok_sb, t - 1)
                for n in range(2):
                    pe.matmul(ps[:, bank + n, :], ones[:], btok[:, n * 512:(n + 1) * 512], start=True, stop=False)
                pe.wait_ge(hT_sb, t + 1)
                for c in range(HC):
                    ins = pe.matmul(ps[:, 1, 0:P], wlat[:, c, :], hT[:, c, :], start=(c == 0), stop=(c == HC - 1))
                ins.then_inc(lat_ps, 1)
                for c in range(HC):
                    pe.matmul(ps[:, bank, 384:512], hT[:, c, :], wkr[:, c, :], start=False, stop=False)
                pe.wait_ge(lat_sb, t + 1)
                pe.matmul(ps[:, bank, 0:384], cT[:], wqkv[:, 0:384], start=False, stop=True)
                pe.matmul(ps[:, bank + 1, :], cT[:], wqkv[:, 384:896], start=False, stop=True).then_inc(tok_ps, 1)

            def tail(t, first):
                pe.wait_ge(o_ready, t + 1)
                for c in range(HC):
                    ins = pe.transpose(ps[:, 6, c * P:(c + 1) * P], o[:, c * P:(c + 1) * P], ident[:])
                ins.then_inc(oT_ps, 1)
                if not first:
                    pe.wait_ge(out_read, t)
                pe.matmul(ps[:, 7, 0:HID], ones[:], bo[:], start=True, stop=False)
                pe.wait_ge(oT_sb, t + 1)
                for c in range(HC):
                    ins = pe.matmul(ps[:, 7, 0:HID], oT[:, c, :], wo[:, c, :], start=False, stop=(c == HC - 1))
                ins.then_inc(out_ps, 1)

            def turn(t, u, i, first, left):
                if left >= 3:
                    front(t + 3, 1 - u)
                tail(t, first)

            pe.wait_ge(loaded, 16 * LOADS)
            pe.wait_ge(onesd, 1)
            for t in range(3):
                front(t, t % 2)
            tiles(pe, turn)

        @block.scalar
        def _(act):
            def front(t, u, b):
                act.activation(xn[:], row(sb["x"], t), ACT.Identity, scale=sb["rstd"][:, bass.ds(t, 1)],
                               bias=shift[:, bass.ds(t, 1)]).then_inc(xn_ready, 1)
                act.wait_ge(xT_ps, t + 1)
                for c in range(HC):
                    ins = act.activation(hT[:, c, :], ps[:, 0, c * P:(c + 1) * P], ACT.Identity,
                                         scale=sb["modT"][:, 1, CT_CA + c, bass.ds(b, 1)], bias=sb["modT"][:, 1, CT_SA + c, bass.ds(b, 1)])
                ins.then_inc(hT_sb, 1)
                act.wait_ge(lat_ps, t + 1)
                act.activation(cT[:], ps[:, 1, 0:P], ACT.Identity, bias=blat[:]).then_inc(lat_sb, 1)
                act.wait_ge(tok_ps, t + 1)
                if not isinstance(t, int) or t > 1:
                    act.wait_ge(pool_sprod, t - 1)
                    act.wait_ge(dve_sprod, t - 1)
                bank = 2 + 2 * u
                heads = lambda a: a.rearrange("p (h d) -> p h d", h=NH)
                act.activation(qk[:, u, 0, :, 0:DH], heads(ps[:, bank, 0:256]), ACT.Copy)
                act.activation(raw[:, u, :, :].rearrange("p h d -> p (h d)"), ps[:, bank, 256:512], ACT.Copy)
                act.activation(qk[:, u, 1, :, 0:DH], heads(ps[:, bank + 1, 0:256]), ACT.Copy)
                act.activation(v[:, bass.ds(t, 1), :, :].rearrange("p o d j -> p j (o d)"), heads(ps[:, bank + 1, 256:512]),
                               ACT.Copy).then_inc(tok_sb, 1)

            def exp(t, u):
                act.wait_ge(sc_ready, t + 1)
                act.activation(sc[:, u, :, :], sc[:, u, :, :], ACT.Exp, scale=SCALE1).then_inc(exp_done, 1)

            def turn(t, u, i, first, left):
                if left >= 3:
                    front(t + 3, 1 - u, i + (u + 3) // 2)
                if left >= 1:
                    exp(t + 1, 1 - u)
                act.wait_ge(oT_ps, t + 1)
                act.activation(oT[:].rearrange("p c q -> p (c q)"), ps[:, 6, 0:HID], ACT.Copy).then_inc(oT_sb, 1)

            act.wait_ge(loaded, 16 * LOADS)
            row_roots(act, sb, var_ready, root_done)
            act.wait_ge(shift_ready, 1)
            for t in range(3):
                front(t, t % 2, t // 2)
            exp(0, 0)
            tiles(act, turn)

        @block.gpsimd
        def _(pool):
            def scores(t, u):
                pool.wait_ge(qk_ready, t + 1)
                if not isinstance(t, int) or t > 1:
                    pool.wait_ge(sc_ready, t - 1)
                score_product(pool, u, NH - POOL_S, NH).then_inc(pool_sprod, 1)

            def turn(t, u, i, first, left):
                pool.wait_ge(p_ready, t + 1)
                value_product(pool, t, u, NH - POOL_V, NH).then_inc(pool_vprod, 1)
                if left >= 2:
                    scores(t + 2, u)

            scores(0, 0)
            scores(1, 1)
            tiles(pool, turn)

        @block.vector
        def _(dve):
            own = Steps(dve, own_s)

            def rotate(t, u):
                dve.wait_ge(tok_sb, t + 1)
                r = raw[:, u, :, :]
                table = lambda n, a, b: rope[:, n, u:u + 1, a:b].to_broadcast([P, 2 * NH, b - a])
                hf = DRH // 2
                dve.tensor_tensor(rt[:, 0, :, :], r, table(0, 0, DRH), ALU.mult)
                dve.tensor_tensor(rt[:, 1, :, 0:hf], r[:, :, hf:DRH], table(1, 0, hf), ALU.mult)
                own.done(dve.tensor_tensor(rt[:, 1, :, hf:DRH], r[:, :, 0:hf], table(1, hf, DRH), ALU.mult))
                dve.tensor_tensor(qk[:, u, :, :, DH:DQK].rearrange("p n h d -> p (n h) d"), rt[:, 0, :, :], rt[:, 1, :, :],
                                  ALU.add).then_inc(qk_ready, 1)
                dve.wait_ge(qk_ready, t + 1)
                score_product(dve, u, 0, NH - POOL_S).then_inc(dve_sprod, 1)

            def scores(t, u):
                dve.wait_ge(dve_sprod, t + 1)
                dve.wait_ge(pool_sprod, t + 1)
                own.done(dve.tensor_reduce(sc[:, u, :, :], sprod[:, u, :, :].rearrange("p i (j d) -> p i j d", j=NH), AX, ALU.add))
                own.done(dve.tensor_reduce(red[:, 0, :], sc[:, u, :, :], AX, ALU.max))
                dve.tensor_tensor(sc[:, u, :, :], sc[:, u, :, :], each(0), ALU.subtract).then_inc(sc_ready, 1)

            each = lambda k: red[:, k, :].rearrange("p (i o) -> p i o", o=1).to_broadcast([P, NH, NH])

            def probabilities(t, u):
                dve.wait_ge(exp_done, t + 1)
                own.done(dve.tensor_reduce(red[:, 1, :], sc[:, u, :, :], AX, ALU.add))
                own.done(dve.reciprocal(red[:, 2, :], red[:, 1, :]))
                dve.tensor_tensor(sc[:, u, :, :], sc[:, u, :, :], each(2), ALU.mult).then_inc(p_ready, 1)

            def values(t, u, first):
                dve.wait_ge(p_ready, t + 1)
                own.done(value_product(dve, t, u, 0, NH - POOL_V))
                dve.wait_ge(pool_vprod, t + 1)
                if not first:
                    dve.wait_ge(oT_ps, t)
                dve.tensor_reduce(o[:], vprod[:].rearrange("p i (d j) -> p (i d) j", d=DH), AX, ALU.add).then_inc(o_ready, 1)

            def output(t, b):
                x = row(sb["x"], t)
                dve.wait_ge(out_ps, t + 1)
                dve.tensor_tensor(y[:], ps[:, 7, 0:HID], row(ga, b), ALU.mult).then_inc(out_read, 1)
                dve.wait_ge(out_read, t + 1)
                dve.tensor_tensor(x, x, y[:], ALU.add)

            def turn(t, u, i, first, left):
                if left > 0:
                    own.start(before + 6 * t)
                if left >= 2:
                    rotate(t + 2, u)
                if not first:
                    output(t - 1, i - (1 - u))
                if left >= 1:
                    scores(t + 1, 1 - u)
                values(t, u, first)
                if left >= 1:
                    probabilities(t + 1, 1 - u)
                assert left < 2 or own.n == 6, own.n

            dve.memset(ones[:], 1.0).then_inc(onesd, 1)
            dve.wait_ge(loaded, 16 * LOADS)
            row_scales(dve, own, sb, var_ready, root_done)
            dve.scalar_tensor_tensor(shift[:], sb["mv"][:, :, 0], -1.0, sb["rstd"][:], ALU.mult, ALU.mult).then_inc(shift_ready, 1)
            rotate(0, 0)
            rotate(1, 1)
            scores(0, 0)
            probabilities(0, 0)
            before = own.n
            tiles(dve, turn)
            output(TILES - 1, NBATCH - 1)


def mixture(nc, io, sb, modd, l, xs, ys, out):
    F, FC = ((F0, F0C), (F1, F1C))[l]
    ne = NE + l
    shared = TILES if l else 0
    nt = NSPARSE + shared
    FP = FC * P
    half = F // 2
    with ExitStack() as ctx:
        s = lambda n, shape, dt=F32: ctx.enter_context(nc.sbuf_tensor(f"m{l}_{n}", shape, dt))
        sems = Sems(nc, ctx)
        q = lambda n: sems(f"m{l}_{n}")
        wg, wu = s("wg", [P, HC, ne, F]), s("wu", [P, HC, ne, F])
        wd = s("wd", [P, ne * FC, HID])
        pos = s("pos", [P, 2, TILES], U32)
        prob = s("prob", [P, 2, TILES])
        eid = s("eid", [1, nt], U32)
        w_loaded = q("w_loaded")

        with ExitStack() as rc:
            t_ = lambda n, shape, dt=F32: rc.enter_context(nc.sbuf_tensor(f"r{l}_{n}", shape, dt))
            part_sems = Sems(nc, rc)
            r = lambda n, part_sems=part_sems: part_sems(f"r{l}_{n}")
            h = t_("h", [P, TILES, HID])
            hcur = t_("hcur", [P, TPB, HID])
            modb = t_("modb", [P, 2, 2, HID])
            wr = t_("wr", [P, HC, NE])
            var_ready, root_done = r("var_ready"), r("root_done")
            hT = t_("hT", [P, 2, HC, P])
            rk = t_("rk", [P, 10, TILES, NE])
            sm = t_("sm", [P, 8, TILES])
            cst = t_("cst", [P, 3 * P + 64 + 16])
            tri, ones_m, rev = cst[:, 0:P], cst[:, P:2 * P], cst[:, 2 * P:2 * P + NE]
            thr, tile_no = cst[:, 2 * P + 16:2 * P + 32], cst[0:1, 2 * P + 32:2 * P + 32 + NSPARSE]
            ex = t_("ex", [P, 4, NE])
            ecmp = t_("ecmp", [P, NE * TILES])
            ejc = t_("ejc", [1, NSPARSE, NE])
            ejs = t_("ejs", [1, nt])
            ps = rc.enter_context(nc.psum_tensor(f"r{l}_ps", [P, 8, 512], F32))
            mods, shared_sent = [r("mods0"), r("mods1")], r("shared_sent")
            own_s, loaded, mods_free, h_ready, hT_ps, hT_sb, logits, masks, ranks, diff, e2, pos_ready, sent = (
                r("own"), r("loaded"), r("mods_free"), r("h_ready"), r("hT_ps"), r("hT_sb"), r("logits"), r("masks"),
                r("ranks"), r("diff"), r("e2"), r("pos_ready"), r("sent"))
            block = rc.enter_context(nc.Block())

            @block.sync
            def _(sp):
                sp.dma_start(wr[:], io[f"l{l}_wr"]).then_inc(loaded, 16)
                sp.dma_start(cst[:, 0:2 * P + 96], io["cst"]).then_inc(loaded, 16)
                sp.dma_start(wd[:], io[f"l{l}_wd"]).then_inc(w_loaded, 16)
                sp.dma_start(wg[:], io[f"l{l}_wg"]).then_inc(w_loaded, 16)
                sp.dma_start(wu[:], io[f"l{l}_wu"]).then_inc(w_loaded, 16)
                if l:
                    for b in range(4):
                        sp.wait_ge(h_ready, 4 * b + 4)
                        sp.dma_start(xs[NSPARSE * P + b * 4 * P:NSPARSE * P + (b + 1) * 4 * P, :].rearrange("(t p) c -> p t c", p=P),
                                     h[:, 4 * b:4 * b + 4, :]).then_inc(shared_sent, 16)
                    sp.wait_ge(shared_sent, 16 * 4)

            @block.scalar
            def _(act):
                row_roots(act, sb, var_ready, root_done)
                with act.Fori(0, NBATCH) as i:
                    for t in range(TPB):
                        act.wait_ge(hT_ps, TPB * i + t + 1)
                        act.activation(hT[:, t, :, :].rearrange("p c q -> p (c q)"), ps[:, t, 0:HID], ACT.Copy).then_inc(hT_sb, 1)
                act.wait_ge(diff, 1)
                act.activation(sm[:, 3, :], sm[:, 2, :], ACT.Exp).then_inc(e2, 1)

            @block.tensor
            def _(pe):
                pe.wait_ge(loaded, 32)
                with pe.Fori(0, NBATCH) as i:
                    for t in range(TPB):
                        pe.wait_ge(h_ready, TPB * i + t + 1)
                        pe.wait_ge(hT_sb, TPB * i + t + 1)
                        for c in range(HC):
                            ins = pe.transpose(ps[:, t, c * P:(c + 1) * P], hcur[:, t, c * P:(c + 1) * P], sb["ident"][:])
                        ins.then_inc(hT_ps, 1)
                        pe.wait_ge(hT_sb, TPB * i + t + 3)
                        for c in range(HC):
                            ins = pe.matmul(ps[:, 2, bass.ds((TPB * i + t) * NE, NE)], hT[:, t, c, :], wr[:, c, :], start=(c == 0), stop=(c == HC - 1))
                        ins.then_inc(logits, 1)
                pe.wait_ge(masks, 1)
                m = rk[:, 4, :, :].rearrange("p t e -> p (t e)")
                pe.matmul(ps[:, 3, 0:P], tri, m, start=True, stop=True)
                pe.matmul(ps[:, 4, 0:P], ones_m, m, start=True, stop=True).then_inc(ranks, 1)

            @block.vector
            def _(dve):
                own = Steps(dve, own_s)
                dve.memset(rk[:, 0, :, :], 0.0).then_inc(mods_free, 2)
                dve.memset(rk[:, 1, :, :], 0.0).then_inc(hT_sb, 2)
                dve.wait_ge(loaded, 32)
                row_scales(dve, own, sb, var_ready, root_done)
                per = TPB * 2 * 2
                with dve.Fori(0, NBATCH // 2) as i:
                    own.start(per * i + ROW_STEPS)
                    for u in range(2):
                        dve.wait_ge(mods[u], 16 * i + 16)
                        for t in range(TPB):
                            tile = 4 * i + 2 * u + t
                            hd = h[:, bass.ds(tile, 1), :].rearrange("p o c -> p (o c)")
                            own.done(normalise(dve, sb, tile, hd))
                            own.done(dve.tensor_tensor(hd, hd, modb[:, u, 1, :], ALU.mult))
                            dve.wait_ge(hT_sb, tile + 1)
                            dve.tensor_tensor(hcur[:, t, :], hd, modb[:, u, 0, :], ALU.add)
                            ins = dve.tensor_tensor(hd, hd, modb[:, u, 0, :], ALU.add)
                            ins.then_inc(h_ready, 1)
                        dve.wait_ge(h_ready, 4 * i + 2 * u + 2)
                        dve.memset(ecmp[:, 0:1], 0.0).then_inc(mods_free, 1)
                own.start(per * (NBATCH // 2) + ROW_STEPS)
                dve.wait_ge(logits, TILES)
                v = lambda k: rk[:, k, :, :]
                bc = lambda k: sm[:, k, :].rearrange("p (t o) -> p t o", o=1).to_broadcast([P, TILES, NE])
                rev_b = rev.rearrange("p (o e) -> p o e", o=1).to_broadcast([P, TILES, NE])
                own.done(dve.tensor_copy(v(0).rearrange("p t e -> p (t e)"), ps[:, 2, 0:P]))
                for n in range(2):
                    own.done(dve.tensor_reduce(sm[:, n, :], v(0), AX, ALU.max))
                    own.done(dve.tensor_tensor(v(1), v(0), bc(n), ALU.is_equal))
                    own.done(dve.tensor_tensor(v(1), v(1), rev_b, ALU.mult))
                    own.done(dve.tensor_reduce(sm[:, 4, :], v(1), AX, ALU.max))
                    own.done(dve.tensor_tensor(v(2 + n), bc(4), rev_b, ALU.is_equal))
                    if n == 0:
                        own.done(dve.scalar_tensor_tensor(v(0), v(2), -3.0e38, v(0), ALU.mult, ALU.add))
                dve.tensor_tensor(v(4), v(2), v(3), ALU.add).then_inc(masks, 1)
                dve.tensor_tensor(sm[:, 2, :], sm[:, 1, :], sm[:, 0, :], ALU.subtract).then_inc(diff, 1)
                dve.wait_ge(e2, 1)
                own.done(dve.tensor_scalar(sm[:, 5, :], sm[:, 3, :], 1.0, None, ALU.add))
                own.done(dve.reciprocal(prob[:, 0, :], sm[:, 5, :]))
                own.done(dve.tensor_tensor(prob[:, 1, :], prob[:, 0, :], sm[:, 3, :], ALU.mult))
                dve.wait_ge(ranks, 1)
                own.done(dve.tensor_copy(v(5).rearrange("p t e -> p (t e)"), ps[:, 4, 0:P]))
                a, b = 5, 6
                for d in (1, 2, 4, 8):
                    dve.tensor_copy(rk[:, b, 0:d, :], rk[:, a, 0:d, :])
                    own.done(dve.tensor_tensor(rk[:, b, d:, :], rk[:, a, d:, :], rk[:, a, 0:TILES - d, :], ALU.add))
                    a, b = b, a
                cnt = rk[:, a, TILES - 1, :]
                ec = ecmp[:].rearrange("p (e k) -> p e k", e=NE)
                own.done(dve.tensor_tensor(ec, cnt.rearrange("p (e o) -> p e o", o=1).to_broadcast([P, NE, TILES]),
                                           thr.rearrange("p (o k) -> p o k", o=1).to_broadcast([P, NE, TILES]), ALU.is_gt))
                own.done(dve.tensor_reduce(ex[:, 0, :], ec, AX, ALU.add))
                for d, ea, eb in ((1, 0, 1), (2, 1, 2), (4, 2, 1)):
                    dve.tensor_copy(ex[:, eb, 0:d], ex[:, ea, 0:d])
                    own.done(dve.tensor_tensor(ex[:, eb, d:], ex[:, ea, d:], ex[:, ea, 0:NE - d], ALU.add))
                incl = ex[:, 1, :]
                own.done(dve.memset(ex[:, 3, 0:1], 0.0))
                own.done(dve.tensor_scalar(ex[:, 3, 1:NE], incl[:, 0:NE - 1], float(P), None, ALU.mult))
                own.done(dve.tensor_tensor(v(7), ex[:, 3, :].rearrange("p (o e) -> p o e", o=1).to_broadcast([P, TILES, NE]),
                                           ps[:, 3, 0:P].rearrange("p (t e) -> p t e", e=NE), ALU.add))
                own.done(dve.tensor_tensor(rk[:, 7, 1:, :], rk[:, 7, 1:, :], rk[:, a, 0:TILES - 1, :], ALU.add))
                for n in range(2):
                    own.done(dve.tensor_tensor(v(8), v(7), v(2 + n), ALU.mult))
                    own.done(dve.tensor_reduce(sm[:, 6 + n, :], v(8), AX, ALU.add))
                    own.done(dve.tensor_copy(pos[:, n, :], sm[:, 6 + n, :]))
                dve.memset(ecmp[:, 0:1], 0.0).then_inc(pos_ready, 1)
                own.done(dve.tensor_tensor(ejc[:, :, 0:NE - 1],
                                           tile_no.rearrange("p (j o) -> p j o", o=1).to_broadcast([1, NSPARSE, NE - 1]),
                                           incl[0:1, 0:NE - 1].rearrange("p (o e) -> p o e", o=1).to_broadcast([1, NSPARSE, NE - 1]), ALU.is_ge))
                if l:
                    own.done(dve.memset(ejs[:, NSPARSE:nt], float(NE)))
                own.done(dve.tensor_reduce(ejs[:, 0:NSPARSE], ejc[:, :, 0:NE - 1], AX, ALU.add))
                own.done(dve.tensor_copy(eid[:], ejs[:]))

            @block.gpsimd
            def _(pool):
                with pool.Fori(0, NBATCH // 2) as i:
                    for u in range(2):
                        pool.wait_ge(mods_free, 2 * i + u + 1)
                        pool.dma_start(modb[:, u, :, :].rearrange("p k c -> p (k c)"),
                                       modd[l, bass.ds(2 * i + u, 1), SB * HID:(CB + 1) * HID].to_broadcast([P, 2 * HID])).then_inc(mods[u], 16)
                pool.wait_ge(pos_ready, 1)
                for t in range(TILES):
                    for n in range(2):
                        pool.indirect_dma_start(xs[0:NSPARSE * P, :], bass.IndirectOffsetOnAxis(ap=pos[:, n, t:t + 1], axis=0),
                                                h[:, t, :], None, bounds_check=NSPARSE * P - 1).then_inc(sent, 16)
                pool.wait_ge(sent, 16 * 2 * TILES)

        with ExitStack() as ec:
            t_ = lambda n, shape, dt=F32: ec.enter_context(nc.sbuf_tensor(f"e{l}_{n}", shape, dt))
            part_sems = Sems(nc, ec)
            r = lambda n, part_sems=part_sems: part_sems(f"e{l}_{n}")
            xin = t_("xin", [P, 2, HID])
            xT = t_("xT", [P, 2, HC, P])
            sg = t_("sg", [P, F])
            a = t_("a", [P, 2, FP])
            aT = t_("aT", [P, FC, P])
            yo = t_("yo", [P, 2, HID])
            ps = ec.enter_context(nc.psum_tensor(f"e{l}_ps", [P, 8, 512], F32))
            pad_zero, x_loaded, xT_ps, xT_sb, g_ps, u_ps, silu_done, a_ready, aT_ps, aT_act, aT_dve, y_ps, y_sb, y_st = (
                r("pad_zero"), [r("x_loaded0"), r("x_loaded1")], r("xT_ps"), r("xT_sb"), r("g_ps"), r("u_ps"), r("silu"), r("a_ready"), r("aT_ps"),
                r("aT_act"), r("aT_dve"), r("y_ps"), r("y_sb"), [r("y_st0"), r("y_st1")])
            block = ec.enter_context(nc.Block())
            NA = min(FC, 4)

            assert nt % 2 == 1

            @block.sync
            def _(sp):
                def load(j, u):
                    src = xs[bass.ds(j * P, P), :] if not isinstance(j, int) else xs[j * P:(j + 1) * P, :]
                    sp.dma_start(xin[:, u, :], src).then_inc(x_loaded[u], 16)
                load(0, 0)
                load(1, 1)
                with sp.Fori(0, (nt - 1) // 2) as i:
                    for u in (0, 1):
                        sp.wait_ge(xT_ps, 2 * i + u + 1)
                        load(2 * i + u + 2, u)
                        sp.wait_ge(y_sb, 2 * i + u + 2)
                        sp.dma_start(ys[bass.ds((2 * i + u) * P, P), :], yo[:, u, :]).then_inc(y_st[u], 16)
                sp.wait_ge(y_sb, nt + 1)
                sp.dma_start(ys[(nt - 1) * P:nt * P, :], yo[:, 0, :]).then_inc(y_st[0], 16)
                sp.wait_ge(y_st[0], 16 * ((nt + 1) // 2))
                sp.wait_ge(y_st[1], 16 * ((nt - 1) // 2))
                sp.wait_ge(x_loaded[1], 16 * ((nt + 1) // 2))

            @block.tensor
            def _(pe):
                def rows(j, u, loads):
                    pe.wait_ge(x_loaded[u], loads)
                    pe.wait_ge(xT_sb, j + 1)
                    for c in range(HC):
                        ins = pe.transpose(ps[:, 6, c * P:(c + 1) * P], xin[:, u, c * P:(c + 1) * P], sb["ident"][:])
                    ins.then_inc(xT_ps, 1)

                def gate_up(j, u):
                    ej = pe.value_load(eid[0:1, bass.ds(j, 1)] if not isinstance(j, int) else eid[0:1, j:j + 1], min_val=0, max_val=ne - 1)
                    pe.wait_ge(xT_sb, j + 2)
                    for n in range(2):
                        for w, bank, signal in ((wg, n, g_ps), (wu, 2 + n, u_ps)):
                            for c in range(HC):
                                ins = pe.matmul(ps[:, bank, 0:half], xT[:, u, c, :],
                                                w[:, c, bass.ds(ej, 1), n * half:(n + 1) * half].rearrange("p o f -> p (o f)"),
                                                start=(c == 0), stop=(c == HC - 1))
                            ins.then_inc(signal, 1)

                def turn(j, u):
                    pe.wait_ge(a_ready, 2 * j + 4)
                    for k in range(FC):
                        ins = pe.transpose(ps[:, 4 + k // 4, (k % 4) * P:(k % 4 + 1) * P], a[:, u, k * P:(k + 1) * P], sb["ident"][:])
                    ins.then_inc(aT_ps, 1)

                def down(j, u):
                    ej = pe.value_load(eid[0:1, bass.ds(j, 1)] if not isinstance(j, int) else eid[0:1, j:j + 1], min_val=0, max_val=ne - 1)
                    pe.wait_ge(aT_act, j + 1)
                    if FC > 4:
                        pe.wait_ge(aT_dve, j + 1)
                    pe.wait_ge(y_sb, j + 1)
                    for k in range(FC):
                        ins = pe.matmul(ps[:, 7, 0:HID], aT[:, k, :], wd[:, bass.ds(ej * FC + k, 1), :].rearrange("p o c -> p (o c)"),
                                        start=(k == 0), stop=(k == FC - 1))
                    ins.then_inc(y_ps, 1)

                pe.wait_ge(w_loaded, 48)
                pe.wait_ge(pad_zero, 1)
                rows(0, 0, 16)
                gate_up(0, 0)
                rows(1, 1, 16)
                with pe.Fori(0, (nt - 1) // 2) as i:
                    turn(2 * i, 0)
                    gate_up(2 * i + 1, 1)
                    rows(2 * i + 2, 0, 16 * i + 32)
                    down(2 * i, 0)
                    turn(2 * i + 1, 1)
                    gate_up(2 * i + 2, 0)
                    rows(2 * i + 3, 1, 16 * i + 32)
                    down(2 * i + 1, 1)
                turn(nt - 1, 0)
                down(nt - 1, 0)

            @block.scalar
            def _(act):
                def xt(j, u):
                    act.wait_ge(xT_ps, j + 1)
                    act.activation(xT[:, u, :, :].rearrange("p c q -> p (c q)"), ps[:, 6, 0:HID], ACT.Copy).then_inc(xT_sb, 1)

                def silu(j, u):
                    for n in range(2):
                        act.wait_ge(g_ps, 2 * j + n + 1)
                        act.wait_ge(a_ready, 2 * j + n + 1)
                        act.activation(sg[:, n * half:(n + 1) * half], ps[:, n, 0:half], ACT.Silu).then_inc(silu_done, 1)

                def at(j):
                    act.wait_ge(aT_ps, j + 1)
                    act.activation(aT[:, 0:NA, :].rearrange("p k q -> p (k q)"), ps[:, 4, 0:NA * P], ACT.Copy).then_inc(aT_act, 1)

                xt(0, 0)
                silu(0, 0)
                xt(1, 1)
                with act.Fori(0, (nt - 1) // 2) as i:
                    at(2 * i)
                    silu(2 * i + 1, 1)
                    xt(2 * i + 2, 0)
                    at(2 * i + 1)
                    silu(2 * i + 2, 0)
                    xt(2 * i + 3, 1)
                at(nt - 1)

            @block.vector
            def _(dve):
                dve.memset(yo[:, 0, 0:1], 0.0).then_inc(a_ready, 2)
                dve.memset(yo[:, 0, 1:2], 0.0).then_inc(xT_sb, 1)
                dve.memset(yo[:, 0, 2:3], 0.0).then_inc(y_sb, 1)
                dve.memset(a[:], 0.0).then_inc(pad_zero, 1)
                dve.wait_ge(pad_zero, 1)

                def mul(j, u):
                    for n in range(2):
                        dve.wait_ge(silu_done, 2 * j + n + 1)
                        dve.wait_ge(u_ps, 2 * j + n + 1)
                        dve.tensor_tensor(a[:, u, n * half:(n + 1) * half], sg[:, n * half:(n + 1) * half], ps[:, 2 + n, 0:half],
                                          ALU.mult).then_inc(a_ready, 1)

                def at(j):
                    if FC > 4:
                        dve.wait_ge(aT_ps, j + 1)
                        dve.tensor_copy(aT[:, 4:FC, :].rearrange("p k q -> p (k q)"), ps[:, 5, 0:(FC - 4) * P]).then_inc(aT_dve, 1)

                def y(j, u, stores=None):
                    dve.wait_ge(y_ps, j + 1)
                    if stores is not None:
                        dve.wait_ge(y_st[u], stores)
                    dve.tensor_copy(yo[:, u, :], ps[:, 7, 0:HID]).then_inc(y_sb, 1)

                mul(0, 0)
                at(0)
                mul(1, 1)
                y(0, 0)
                at(1)
                mul(2, 0)
                y(1, 1)
                with dve.Fori(1, (nt - 1) // 2) as i:
                    at(2 * i)
                    mul(2 * i + 1, 1)
                    y(2 * i, 0, 16 * i)
                    at(2 * i + 1)
                    mul(2 * i + 2, 0)
                    y(2 * i + 1, 1, 16 * i)
                at(nt - 1)
                y(nt - 1, 0, 16 * ((nt - 1) // 2))

        with ExitStack() as fc:
            t_ = lambda n, shape, dt=F32: fc.enter_context(nc.sbuf_tensor(f"c{l}_{n}", shape, dt))
            part_sems = Sems(nc, fc)
            r = lambda n, part_sems=part_sems: part_sems(f"c{l}_{n}")
            g = t_("g", [P, 4, 2, HID])
            ysh = t_("ysh", [P, 4, HID])
            gb = t_("gb", [P, NBATCH, HID])
            tmp = t_("tmp", [P, 2, HID])
            got, got_shared = [r(f"got{n}") for n in range(4)], [r(f"got_shared{n}") for n in range(4)]
            gb_loaded, x_new, own_s, out_st = r("gb_loaded"), r("x_new"), r("own"), r("out_st")
            block = fc.enter_context(nc.Block())

            @block.sync
            def _(sp):
                sp.dma_start(gb[:], modd[l:l + 1, :, GB * HID:(GB + 1) * HID].to_broadcast([P, NBATCH, HID])).then_inc(gb_loaded, 16)
                if l:
                    for t in range(TILES):
                        if t >= 4:
                            sp.wait_ge(x_new, t - 3)
                        sp.dma_start(ysh[:, t % 4, :], ys[(NSPARSE + t) * P:(NSPARSE + t + 1) * P, :]).then_inc(got_shared[t % 4], 16)
                    for t in range(0, TILES, 2):
                        sp.wait_ge(x_new, t + 2)
                        sp.dma_start(out[t * P:(t + 2) * P, :].rearrange("(t p) c -> p t c", p=P), sb["x"][:, t:t + 2, :]).then_inc(out_st, 16)
                    sp.wait_ge(out_st, 16 * TILES // 2)

            @block.gpsimd
            def _(pool):
                for t in range(TILES):
                    if t >= 4:
                        pool.wait_ge(x_new, t - 3)
                    for n in range(2):
                        pool.indirect_dma_start(g[:, t % 4, n, :], None, ys[0:NSPARSE * P, :],
                                                bass.IndirectOffsetOnAxis(ap=pos[:, n, t:t + 1], axis=0),
                                                bounds_check=NSPARSE * P - 1).then_inc(got[t % 4], 16)

            @block.vector
            def _(dve):
                own = Steps(dve, own_s)
                dve.wait_ge(gb_loaded, 16)
                for t in range(TILES):
                    k = t % 4
                    dve.wait_ge(got[k], 32 * (t // 4 + 1))
                    if l:
                        dve.wait_ge(got_shared[k], 16 * (t // 4 + 1))
                    acc = tmp[:, t % 2, :]
                    own.done(dve.tensor_scalar(acc, g[:, k, 0, :], prob[:, 0, t:t + 1], None, ALU.mult))
                    own.done(dve.scalar_tensor_tensor(acc, g[:, k, 1, :], prob[:, 1, t:t + 1], acc, ALU.mult, ALU.add))
                    if l:
                        own.done(dve.tensor_tensor(acc, acc, ysh[:, k, :], ALU.add))
                    own.done(dve.tensor_tensor(acc, acc, gb[:, t // TPB, :], ALU.mult))
                    dve.tensor_tensor(sb["x"][:, t, :], sb["x"][:, t, :], acc, ALU.add).then_inc(x_new, 1)


def program(nc, io, out):
    with ExitStack() as ctx:
        sb = {
            "x": ctx.enter_context(nc.sbuf_tensor("x_tok", [P, TILES, HID], F32)),
            "ident": ctx.enter_context(nc.sbuf_tensor("ident_sb", [P, P], F32)),
            "stats": ctx.enter_context(nc.sbuf_tensor("row_stats", [P, TILES, 6], F32)),
            "mv": ctx.enter_context(nc.sbuf_tensor("row_mv", [P, TILES, 2], F32)),
            "var": ctx.enter_context(nc.sbuf_tensor("row_var", [P, TILES], F32)),
            "root": ctx.enter_context(nc.sbuf_tensor("row_root", [P, TILES], F32)),
            "rstd": ctx.enter_context(nc.sbuf_tensor("row_rstd", [P, TILES], F32)),
            "modT": ctx.enter_context(nc.sbuf_tensor("modT", [P, 2, 4, NBATCH], F32)),
        }
        modd = nc.dram_tensor("mod_rows", [2, NBATCH, 6 * HID], F32, kind="Internal").ap()
        xs = [nc.dram_tensor(f"xs{l}", [(NSPARSE + l * TILES + 1) * P, HID], F32, kind="Internal").ap() for l in range(2)]
        ys = [nc.dram_tensor(f"ys{l}", [(NSPARSE + l * TILES) * P, HID], F32, kind="Internal").ap() for l in range(2)]
        setup(nc, io, sb, modd, xs)
        attention0(nc, io, sb, modd)
        mixture(nc, io, sb, modd, 0, xs[0], ys[0], None)
        attention1(nc, io, sb, modd)
        mixture(nc, io, sb, modd, 1, xs[1], ys[1], out)


def layout(i):
    f = np.float32
    a = {k: np.asarray(v) for k, v in i.items()}
    o = {}
    o["x"] = a["L0_attn_hidden_states"].reshape(TOK, HID)
    chunks = lambda w: np.ascontiguousarray(w.reshape(-1, P, w.shape[1]).transpose(1, 0, 2))
    o["cT"] = np.ascontiguousarray(np.stack([chunks(a[f"L{l}_c"].T) for l in range(2)], 1))
    o["wmod"] = np.ascontiguousarray(np.stack([chunks(a[f"L{l}_wmod"]) for l in range(2)], 1))
    o["ident"] = np.eye(P, dtype=f)
    cst = np.zeros((P, 2 * P + 96), f)
    cst[:, 0:P] = np.triu(np.ones((P, P), f), 1)
    cst[:, P:2 * P] = 1.0
    cst[:, 2 * P:2 * P + NE] = np.arange(NE, 0, -1)
    cst[:, 2 * P + 16:2 * P + 32] = np.arange(TILES) * P
    cst[:, 2 * P + 32:2 * P + 32 + NSPARSE] = np.arange(NSPARSE)
    o["cst"] = cst
    heads = lambda w: np.ascontiguousarray(w.reshape(NH, D0, -1).transpose(1, 0, 2))
    o["l0_wuq"], o["l0_wuk"], o["l0_wuv"] = (heads(a[f"L0_attn_W_{k}_w"]) for k in ("UQ", "UK", "UV"))
    o["l0_woT"] = heads(a["L0_attn_W_O_w"].T)
    o["l0_bup"] = np.ascontiguousarray(np.stack([a[f"L0_attn_W_{k}_b"].reshape(NH, D0).T for k in ("UQ", "UV")], 1))
    dq, dkv = a["L0_attn_W_DQ_w"].T, a["L0_attn_W_DKV_w"].T
    o["l0_wlat"] = chunks(np.concatenate([dq, dkv, dkv], 1))
    bl = np.zeros((P, 3), f)
    bl[:, 0] = a["L0_attn_W_DQ_b"][:P]
    bl[0:QC - P, 1] = a["L0_attn_W_DQ_b"][P:]
    bl[0:KVC, 2] = a["L0_attn_W_DKV_b"]
    bl[KVC:, 2] = a["L0_attn_W_DKV_b"]
    o["l0_blat"] = bl
    o["l0_bo"] = a["L0_attn_W_O_b"].reshape(1, HID)
    o["l0_wr"] = chunks(a["L0_ffn_router_w"].T)
    ffn = lambda w: np.ascontiguousarray(w.reshape(w.shape[0], HC, P, -1).transpose(2, 1, 0, 3))
    o["l0_wg"], o["l0_wu"] = (ffn(a[f"L0_ffn_{k}_w"].transpose(0, 2, 1)) for k in ("gate", "up"))
    wd = np.zeros((NE, F0C * P, HID), f)
    wd[:, 0:F0, :] = a["L0_ffn_down_w"].transpose(0, 2, 1)
    o["l0_wd"] = np.ascontiguousarray(wd.reshape(NE * F0C, P, HID).transpose(1, 0, 2))
    o["l1_wlat"] = chunks(np.concatenate([a["L1_attn_Wc"], a["L1_attn_Wckv"]], 1))
    o["l1_blat"] = np.concatenate([a["L1_attn_bc"], a["L1_attn_bckv"]]).reshape(P, 1)
    wqkv = np.zeros((P, 896), f)
    wqkv[0:64, 0:256], wqkv[0:64, 256:384] = a["L1_attn_Wcq"], a["L1_attn_Wqr"]
    wqkv[64:128, 384:640], wqkv[64:128, 640:896] = a["L1_attn_Wck"], a["L1_attn_Wv"]
    o["l1_wqkv"] = wqkv
    o["l1_wkr"] = chunks(a["L1_attn_Wkr"])
    o["l1_btok"] = np.concatenate([a[f"L1_attn_{k}"] for k in ("bcq", "bqr", "bkr", "bck", "bv")]).reshape(1, 1024)
    o["l1_wo"] = chunks(a["L1_attn_Wo"])
    o["l1_bo"] = a["L1_attn_bo"].reshape(1, HID)
    inv = (1.0 / 10000.0 ** (np.arange(0, DRH, 2, dtype=f) / DRH)).astype(f)
    fr = np.arange(SEQ, dtype=f)[:, None] * inv[None, :]
    cos, sin = np.cos(fr).astype(f), np.sin(fr).astype(f)
    tab = np.stack([np.concatenate([cos, cos], 1), np.concatenate([-sin, sin], 1)])
    o["l1_rope"] = np.ascontiguousarray(tab.reshape(2, TPB, P, DRH).transpose(2, 0, 1, 3))
    o["l1_wr"] = chunks(a["L1_ffn_gate_w"])
    gu = np.concatenate([a["L1_ffn_w_gate_up"], a["L1_ffn_shared_gate_up"][None]], 0)
    o["l1_wg"], o["l1_wu"] = ffn(gu[:, :, 0:F1]), ffn(gu[:, :, F1:])
    dn = np.concatenate([a["L1_ffn_w_down"], a["L1_ffn_shared_down"][None]], 0)
    o["l1_wd"] = np.ascontiguousarray(dn.reshape((NE + 1) * F1C, P, HID).transpose(1, 0, 2))
    return {k: np.ascontiguousarray(v, dtype=f) for k, v in o.items()}


def kernel(**inputs):
    import concourse.bacc as bacc
    from concourse.bass_utils import run_bass_kernel_spmd

    nc = bacc.Bacc("TRN2", target_bir_lowering=False, num_devices=1)
    arrays = layout(inputs)
    io = {k: nc.dram_tensor(f"in_{k}", v.shape, F32, kind="ExternalInput").ap() for k, v in arrays.items()}
    out = nc.dram_tensor("out_x", (TOK, HID), F32, kind="ExternalOutput").ap()
    program(nc, io, out)
    r = run_bass_kernel_spmd(nc, [{f"in_{k}": v for k, v in arrays.items()}], core_ids=[0])
    return r.results[0]["out_x"].reshape(NBATCH, SEQ, HID)
```

```python
from contextlib import ExitStack

import numpy as np
import concourse.bass as bass
from concourse import mybir

F32 = mybir.dt.float32
U32 = mybir.dt.uint32
ALU = mybir.AluOpType
ACT = mybir.ActivationFunctionType
AX = mybir.AxisListType.X

P = 128
NBATCH, SEQ, HID = 8, 256, 256
TOK = NBATCH * SEQ
TILES = TOK // P
TPB = SEQ // P
HC = HID // P
NH = 16
QC, KVC, D0 = 192, 64, 128
SCALE0 = 1.0 / float(np.sqrt(D0))
DH, DRH = 16, 8
DQK = DH + DRH
SCALE1 = 1.0 / float(np.sqrt(DQK))
POOL_S, POOL_V = 13, 12
NE = 8
F0, F1 = 688, 512
F0C, F1C = -(-F0 // P), F1 // P
NSPARSE = (2 * TOK + NE * (P - 1)) // P
EPS = 1e-5
SA, CA, GA, SB, CB, GB = range(6)
CT_SA, CT_CA = 0, 2


class Sems:

    def __init__(self, nc, ctx):
        self.nc, self.all = nc, []
        ctx.callback(self.free)

    def free(self):
        self.nc.clear_and_free_semaphores(self.all)
        self.nc.all_engine_barrier()

    def __call__(self, name):
        self.all.append(self.nc.alloc_semaphore(name))
        return self.all[-1]


class Steps:

    def __init__(self, eng, sem):
        self.eng, self.sem, self.base, self.n = eng, sem, 0, 0

    def start(self, base):
        self.base, self.n = base, 0

    def done(self, ins):
        self.n += 1
        ins.then_inc(self.sem, 1)
        self.eng.wait_ge(self.sem, self.base + self.n)


def row_scales(dve, own, sb, var_ready, root_done, part=slice(0, TILES), before=0):
    var, rstd, t = sb["var"][:, part], sb["rstd"][:, part], sb["root"][:, part]
    for k in range(part.start, part.stop):
        ins = dve.bn_aggr(sb["mv"][:, k, :], sb["stats"][:, k, :])
    own.done(ins)
    dve.tensor_scalar(var, sb["mv"][:, part, 1], EPS, None, ALU.add).then_inc(var_ready, 1)
    dve.wait_ge(root_done, 2 * before + 1)
    own.done(dve.reciprocal(rstd, t))
    own.done(dve.tensor_tensor(t, rstd, rstd, ALU.mult))
    own.done(dve.tensor_tensor(t, t, var, ALU.mult))
    own.done(dve.tensor_scalar(t, t, -0.5, 1.5, ALU.mult, ALU.add))
    own.done(dve.tensor_tensor(rstd, rstd, t, ALU.mult))
    dve.scalar_tensor_tensor(sb["shift"][:, part], sb["mv"][:, part, 0], -1.0, rstd, ALU.mult, ALU.mult).then_inc(root_done, 1)
    dve.wait_ge(root_done, 2 * before + 2)


def row_stats(dve, sb, tile):
    return dve.bn_stats(row(sb["stats"], tile), row(sb["x"], tile))


def row_roots(act, sb, var_ready, root_done, part=slice(0, TILES), before=0):
    act.wait_ge(var_ready, before + 1)
    act.activation(sb["root"][:, part], sb["var"][:, part], ACT.Sqrt).then_inc(root_done, 1)


def row(buf, k):
    return buf[:, bass.ds(k, 1), :].rearrange("p o c -> p (o c)")


def normalise(dve, sb, tile, xn):
    return dve.tensor_scalar(xn, row(sb["x"], tile),
                             sb["mv"][:, bass.ds(tile, 1), 0], sb["rstd"][:, bass.ds(tile, 1)], ALU.subtract, ALU.mult)


STEPS = 8


def attention0(nc, io, sb, modd, xs_dram):
    with ExitStack() as ctx:
        s = lambda n, shape: ctx.enter_context(nc.sbuf_tensor(f"l0_{n}", shape, F32))
        sems = Sems(nc, ctx)
        q = lambda n: sems(f"l0_{n}")
        wlat = s("wlat", [P, HC, QC + 2 * KVC])
        blat = s("blat", [P, 3])
        aq = s("aq", [P, 2, NH * KVC])
        aqb = s("aqb", [P, NH // 2])
        wvo = s("wvo", [P, NH // 2, HID])
        bo = s("bo", [P, HID])
        ps = ctx.enter_context(nc.psum_tensor("l0_ps", [P, 8, 512], F32))
        ident = sb["ident"]
        cleared, zero_set, gb_loaded = q("cleared"), q("zero_set"), q("gb_loaded")
        var_ready, root_done, own_s, zeroed, ga_loaded, xn_ready, unit_ps, unit_sb = (
            q("var_ready"), q("root_done"), q("own"), q("zeroed"), q("ga_loaded"), q("xn_ready"), q("unit_ps"), q("unit_sb"))
        scores, max_ready, exp_done, prob_ready, pT_ps, pT_act, pT_dve, ctx_ps, ctx_sb, out_ps, out_read = (
            q("scores"), q("max_ready"), q("exp_done"), q("prob_ready"), q("pT_ps"), q("pT_act"), q("pT_dve"), q("ctx_ps"), q("ctx_sb"),
            q("out_ps"), q("out_read"))

        with ExitStack() as pre:
            t = lambda n, shape: pre.enter_context(nc.sbuf_tensor(f"l0_{n}", shape, F32))
            pre_sems = Sems(nc, pre)
            r = lambda n: pre_sems(f"l0_{n}")
            cT, wmod = t("cT", [P, 2, HC, NBATCH]), t("wmod", [P, 2, HC, 6 * HID])
            mod, sign = t("mod", [NBATCH, 2, 6 * HID]), t("sign", [NBATCH, HID])
            wuq, wuk, wuv, woT = t("wuq", [P, NH, QC]), t("wuk", [P, NH, KVC]), t("wuv", [P, NH, KVC]), t("woT", [P, NH, HID])
            bup, bo_row, ones = t("bup", [P, 2, NH]), t("bo_row", [1, 2, HID]), t("ones", [1, P])
            c_loaded, wmod_loaded, qk_loaded, vo_loaded, rest_loaded = (
                r("c_loaded"), [r("wmod0_loaded"), r("wmod1_loaded")], r("qk_loaded"), r("vo_loaded"), r("rest_loaded"))
            silu_done, mod_ps, mod_sb, mod_rows, cols_ps, stored, pre_own = (
                r("silu_done"), r("mod_ps"), r("mod_sb"), r("mod_rows"), r("cols_ps"), r("stored"), r("pre_own"))
            onesd, fold_ps, fold_sb, bias_row, bias_ps = r("ones_set"), r("fold_ps"), r("fold_sb"), r("bias_row"), r("bias_ps")
            block = pre.enter_context(nc.Block())

            @block.sync
            def _(sp):
                sp.dma_start(cT[:], io["cT"]).then_inc(c_loaded, 16)
                for l in range(2):
                    sp.dma_start(wmod[:, l], io["wmod"][:, l]).then_inc(wmod_loaded[l], 16)
                for dst, name in ((wuk, "l0_wuk"), (wuq, "l0_wuq"), (bup, "l0_bup")):
                    sp.dma_start(dst[:], io[name]).then_inc(qk_loaded, 16)
                for dst, name in ((wuv, "l0_wuv"), (woT, "l0_woT")):
                    sp.dma_start(dst[:], io[name]).then_inc(vo_loaded, 16)
                sp.dma_start(sb["ident"][:], io["ident"]).then_inc(rest_loaded, 16)
                sp.dma_start(sb["x"][:], io["x"].rearrange("(t p) c -> p t c", p=P)).then_inc(rest_loaded, 16)
                sp.dma_start(wlat[:], io["l0_wlat"]).then_inc(rest_loaded, 16)
                sp.dma_start(blat[:], io["l0_blat"]).then_inc(rest_loaded, 16)
                sp.dma_start(bo_row[:, 0, :], io["l0_bo"]).then_inc(rest_loaded, 16)
                sp.wait_ge(mod_rows, 1)
                sp.dma_start(modd.rearrange("l b n -> b l n"), mod[:]).then_inc(stored, 16)
                sp.wait_ge(stored, 16)

            @block.scalar
            def _(act):
                act.wait_ge(c_loaded, 16)
                act.activation(cT[:], cT[:], ACT.Silu).then_inc(silu_done, 1)
                act.wait_ge(mod_ps, 2)
                act.activation(mod[:, 1, :].rearrange("p (n c) -> p n c", n=3), ps[0:NBATCH, 3:6, :], ACT.Copy).then_inc(mod_sb, 1)

            @block.tensor
            def _(pe):
                pe.wait_ge(silu_done, 1)
                for l in range(2):
                    pe.wait_ge(wmod_loaded[l], 16)
                    for n in range(3):
                        for c in range(HC):
                            last = pe.matmul(ps[0:NBATCH, 3 * l + n, :], cT[:, l, c, :], wmod[:, l, c, n * 512:(n + 1) * 512],
                                             start=(c == 0), stop=(c == HC - 1))
                    last.then_inc(mod_ps, 1)
                pe.wait_ge(qk_loaded, 48)
                pe.wait_ge(mod_sb, 2)
                for h in range(NH):
                    cols = slice((h % 8) * KVC, (h % 8 + 1) * KVC)
                    pe.matmul(ps[:, h // 8, cols], wuq[:, h, 0:P], wuk[:, h, :], start=True, stop=True)
                    pe.matmul(ps[0:QC - P, 2 + h // 8, cols], wuq[:, h, P:QC], wuk[:, h, :], start=True, stop=True)
                    r0 = (h % 2) * KVC
                    ins = pe.matmul(ps[r0:r0 + KVC, 4, h // 2:h // 2 + 1], wuk[:, h, :], bup[:, 0, h:h + 1], start=True, stop=True)
                ins.then_inc(fold_ps, 1)
                pe.wait_ge(vo_loaded, 32)
                for h in range(NH):
                    ins = pe.matmul(ps[0:1, 5, 0:HID], bup[:, 1, h:h + 1], woT[:, h, :], start=(h == 0), stop=(h == NH - 1))
                ins.then_inc(fold_ps, 1)
                pe.wait_ge(rest_loaded, 80)
                pe.wait_ge(mod_rows, 1)
                for l in range(2):
                    for j in range(4):
                        ins = pe.transpose(ps[:, 6, (l * 4 + j) * NBATCH:(l * 4 + j + 1) * NBATCH], mod[:, l, j * P:(j + 1) * P],
                                           sb["ident"][0:NBATCH, 0:NBATCH])
                ins.then_inc(cols_ps, 1)
                pe.wait_ge(fold_sb, 1)
                for h in range(NH):
                    r0, c0 = (h % 2) * KVC, (h // 2 % 2) * HID
                    ins = pe.matmul(ps[r0:r0 + KVC, h // 4, c0:c0 + HID], wuv[:, h, :], woT[:, h, :], start=True, stop=True)
                ins.then_inc(fold_ps, 1)
                pe.wait_ge(bias_row, 1)
                pe.matmul(ps[:, 7, 0:HID], ones[:], bo_row[:, 1, :], start=True, stop=True).then_inc(bias_ps, 1)

            @block.vector
            def _(dve):
                own = Steps(dve, pre_own)
                dve.memset(ones[:], 1.0).then_inc(onesd, 1)
                dve.wait_ge(mod_ps, 1)
                dve.tensor_copy(mod[:, 0, :].rearrange("p (n c) -> p n c", n=3), ps[0:NBATCH, 0:3, :]).then_inc(mod_sb, 1)
                dve.wait_ge(mod_sb, 2)
                for l in range(2):
                    for k in (CA, CB):
                        v = mod[:, l, k * HID:(k + 1) * HID]
                        own.done(dve.tensor_scalar(v, v, 1.0, None, ALU.add))
                    for k in (GA, GB):
                        v = mod[:, l, k * HID:(k + 1) * HID]
                        dve.tensor_scalar(sign[:], v, 0.0, 2.0, ALU.is_ge, ALU.mult)
                        own.done(dve.scalar_tensor_tensor(v, v, -1.0, v, ALU.mult, ALU.max))
                        own.done(dve.tensor_scalar(v, v, 0.25, None, ALU.max))
                        ins = dve.scalar_tensor_tensor(v, sign[:], -1.0, v, ALU.add, ALU.mult)
                        if (l, k) == (1, GB):
                            ins.then_inc(mod_rows, 1)
                        else:
                            own.done(ins)
                dve.wait_ge(fold_ps, 1)
                dve.tensor_copy(aq[:, 0, :].rearrange("p (b c) -> p b c", b=2), ps[:, 0:2, :])
                dve.tensor_copy(aqb[:], ps[:, 4, 0:NH // 2])
                dve.tensor_copy(aq[0:QC - P, 1, :].rearrange("p (b c) -> p b c", b=2), ps[0:QC - P, 2:4, :]).then_inc(fold_sb, 1)
                dve.wait_ge(onesd, 1)
                dve.wait_ge(rest_loaded, 80)
                dve.wait_ge(fold_ps, 2)
                dve.tensor_tensor(bo_row[:, 1, :], ps[0:1, 5, 0:HID], bo_row[:, 0, :], ALU.add).then_inc(bias_row, 1)
                for k in range(TILES):
                    row_stats(dve, sb, k)
                dve.wait_ge(cols_ps, 1)
                dve.tensor_copy(sb["modT"][:].rearrange("p l j b -> p (l j b)"), ps[:, 6, 0:2 * 4 * NBATCH])
                dve.wait_ge(fold_ps, 3)
                dve.tensor_copy(wvo[:].rearrange("p (b h) c -> p b (h c)", b=4), ps[:, 0:4, :])
                dve.wait_ge(bias_ps, 1)
                dve.tensor_copy(bo[:], ps[:, 7, 0:HID])

        hT = s("hT", [P, HC, SEQ])
        xn = s("xn", [P, TPB, HID])
        cq = s("cq", [P, 2, SEQ])
        ckv = s("ckv", [P, 2, 2, SEQ])
        ckvt = s("ckvt", [P, 2, TPB, KVC])
        qT = s("qT", [P, 2, NH // 2, SEQ])
        mx, sums, rinv = s("mx", [P, 2, 4]), s("sums", [P, 2, 4]), s("rinv", [P, 2, 4])
        prob = s("prob", [P, 2, 4, SEQ])
        probT = s("probT", [P, 4, TPB, P])
        ctxT = s("ctxT", [P, 2, NH // 2 * P])
        ga = s("ga", [P, NBATCH, HID])
        y = s("y", [P, HID])
        zero = s("zero", [P, 4 * HID])
        S = lambda st: ps[:, 2 * (st % 2):2 * (st % 2) + 2, :]
        C, O, U = ps[:, 6, 0:2 * P], ps[:, 6, 2 * P:2 * P + HID], ps[:, 7, :]
        block = ctx.enter_context(nc.Block())

        ACT_UNITS, DVE_UNITS = (0, 1, 5, 6, 7), (2, 3, 4)

        def batches(eng, batch):
            batch(0, 0, True, False)
            with eng.Fori(0, NBATCH // 2 - 1) as k:
                batch(2 * k + 1, 1, False, False)
                batch(2 * k + 2, 0, False, False)
            batch(NBATCH - 1, 1, False, True)

        @block.sync
        def _(sp):
            sp.dma_start(ga[:], modd[0:1, :, GA * HID:(GA + 1) * HID].to_broadcast([P, NBATCH, HID])).then_inc(ga_loaded, 16)
            sp.dma_start(sb["modb"][:], modd[0:1, :, SB * HID:(CB + 1) * HID].to_broadcast([P, NBATCH, 2 * HID])).then_inc(ga_loaded, 16)
            sp.dma_start(sb["gb"][:], modd[0:1, :, GB * HID:(GB + 1) * HID].to_broadcast([P, NBATCH, HID])).then_inc(gb_loaded, 16)
            sp.wait_ge(gb_loaded, 16)
            sp.wait_ge(zero_set, 1)
            for l in range(2):
                lists = xs_dram[l].rearrange("(n p r) c -> n p (r c)", p=P, r=4)
                for n in range((NSPARSE + 1) // 4):
                    sp.dma_start(lists[n], zero[:]).then_inc(cleared, 16)
            sp.wait_ge(cleared, 16 * 2 * ((NSPARSE + 1) // 4))
            sp.wait_ge(ga_loaded, 32)

        @block.gpsimd
        def _(pool):
            pool.memset(zero[:], 0.0).then_inc(zero_set, 1)

        @block.tensor
        def _(pe):
            def unit(i, u, b):
                if u != 3 and not (isinstance(i, int) and STEPS * i + u == 0):
                    pe.wait_ge(unit_sb, STEPS * i + u)
                if u == 0:
                    pe.wait_ge(xn_ready, i + 1)
                    for t in range(TPB):
                        for c in range(HC):
                            ins = pe.transpose(U[:, c * SEQ + t * P:c * SEQ + (t + 1) * P], xn[:, t, c * P:(c + 1) * P], ident[:])
                elif u == 1:
                    for c in range(HC):
                        pe.matmul(U[:, 0:SEQ], wlat[:, c, 0:P], hT[:, c, :], start=(c == 0), stop=(c == HC - 1))
                    for c in range(HC):
                        ins = pe.matmul(U[0:QC - P, SEQ:2 * SEQ], wlat[:, c, P:QC], hT[:, c, :], start=(c == 0), stop=(c == HC - 1))
                elif u == 2:
                    for c in range(HC):
                        ins = pe.matmul(U[:, 0:SEQ], wlat[:, c, QC:QC + P], hT[:, c, :], start=(c == 0), stop=(c == HC - 1))
                elif u == 3:
                    for t in range(TPB):
                        ins = pe.transpose(U[:, t * KVC:(t + 1) * KVC], ckv[0:KVC, b, 0, t * P:(t + 1) * P], ident[0:KVC, 0:KVC])
                else:
                    for n in range(2):
                        p = 2 * (u - 4) + n
                        pe.matmul(U[:, n * SEQ:(n + 1) * SEQ], aq[:, 0, p * P:(p + 1) * P], cq[:, 0, :], start=True, stop=False)
                        ins = pe.matmul(U[:, n * SEQ:(n + 1) * SEQ], aq[0:QC - P, 1, p * P:(p + 1) * P], cq[0:QC - P, 1, :],
                                        start=False, stop=True)
                ins.then_inc(unit_ps, 1)

            def score(st, b):
                for n in range(2):
                    ins = pe.matmul(S(st)[:, n, :], qT[:, b, (st % 4) * 2 + n, (st // 4) * P:(st // 4 + 1) * P],
                                    ckv[:, b, :, :].rearrange("p h k -> p (h k)"), start=True, stop=True)
                ins.then_inc(scores, 1)

            def out(n, half):
                pe.wait_ge(ctx_sb, n + 1)
                for p in range(NH // 2):
                    ins = pe.matmul(O, ctxT[:, half, p * P:(p + 1) * P], wvo[:, p, :], start=(p == 0), stop=(p == NH // 2 - 1))
                ins.then_inc(out_ps, 1)

            def batch(i, b, first, last):
                for st in range(STEPS):
                    n = STEPS * i + st
                    pe.wait_ge(prob_ready, n + 1)
                    for j in range(4):
                        for k in range(TPB):
                            ins = pe.transpose(ps[:, 4 + j // 2, ((j % 2) * TPB + k) * P:((j % 2) * TPB + k + 1) * P],
                                               prob[:, st % 2, j, k * P:(k + 1) * P], ident[:])
                    ins.then_inc(pT_ps, 1)
                    if st % 4 == 0 and not (first and st == 0):
                        out(n - 1, 1 - st // 4)
                    if not (last and st + 2 >= STEPS):
                        ahead = (st + 2) % STEPS
                        if ahead < 4:
                            pe.wait_ge(unit_sb, STEPS * (i + (st + 2) // STEPS) + 4 + ahead + 1)
                        if st == 3 and not last:
                            pe.wait_ge(unit_sb, STEPS * (i + 1) + 3)
                        pe.wait_ge(exp_done, n + 1)
                        score(ahead, (b + (st + 2) // STEPS) % 2)
                    if not last:
                        unit(i + 1, st, 1 - b)
                    pe.wait_ge(pT_act, n + 1)
                    pe.wait_ge(pT_dve, n + 1)
                    if not (first and st == 0):
                        pe.wait_ge(ctx_sb, n)
                    if st % 4 == 0 and not (first and st == 0):
                        pe.wait_ge(out_read, 2 * i + st // 4)
                    for j in range(4):
                        for k in range(TPB):
                            ins = pe.matmul(C[(j % 2) * KVC:(j % 2 + 1) * KVC, j // 2 * P:(j // 2 + 1) * P], ckvt[:, b, k, :],
                                            probT[:, j, k, :], start=(k == 0), stop=(k == TPB - 1))
                    ins.then_inc(ctx_ps, 1)

            pe.wait_ge(zeroed, 1)
            for u in range(STEPS):
                if u == 3:
                    pe.wait_ge(unit_sb, 3)
                unit(0, u, 0)
            pe.wait_ge(unit_sb, STEPS)
            score(0, 0)
            score(1, 0)
            batches(pe, batch)
            out(STEPS * NBATCH - 1, 1)

        @block.scalar
        def _(act):
            def unit(i, u, b):
                act.wait_ge(unit_ps, STEPS * i + u + 1)
                if u == 0:
                    for c in range(HC):
                        ins = act.activation(hT[:, c, :], U[:, c * SEQ:(c + 1) * SEQ], ACT.Identity,
                                             scale=sb["modT"][:, 0, CT_CA + c, bass.ds(i, 1)], bias=sb["modT"][:, 0, CT_SA + c, bass.ds(i, 1)])
                elif u == 1:
                    act.activation(cq[:, 0, :], U[:, 0:SEQ], ACT.Identity, bias=blat[:, 0:1])
                    ins = act.activation(cq[0:QC - P, 1, :], U[0:QC - P, SEQ:2 * SEQ], ACT.Identity, bias=blat[0:QC - P, 1:2])
                else:
                    for n in range(2):
                        p = 2 * (u - 4) + n
                        ins = act.activation(qT[:, b, p, :], U[:, n * SEQ:(n + 1) * SEQ], ACT.Identity, bias=aqb[:, p:p + 1])
                ins.then_inc(unit_sb, 1)

            def exp(n, st):
                act.wait_ge(max_ready, n + 1)
                for j in range(4):
                    ins = act.activation(prob[:, st % 2, j, :], S(st)[:, j // 2, (j % 2) * SEQ:(j % 2 + 1) * SEQ], ACT.Exp,
                                         bias=mx[:, st % 2, j:j + 1], scale=SCALE0, accum_out=sums[:, st % 2, j:j + 1])
                ins.then_inc(exp_done, 1)

            def batch(i, b, first, last):
                for st in range(STEPS):
                    n = STEPS * i + st
                    act.wait_ge(pT_ps, n + 1)
                    act.activation(probT[:, 0:2, :, :].rearrange("p h k q -> p (h k q)"), ps[:, 4, :], ACT.Copy).then_inc(pT_act, 1)
                    if not (last and st + 2 >= STEPS):
                        exp(n + 2, st)
                    if not last and st in ACT_UNITS:
                        unit(i + 1, st, 1 - b)

            row_roots(act, sb, var_ready, root_done)
            for u in ACT_UNITS:
                unit(0, u, 0)
            exp(0, 0)
            exp(1, 1)
            batches(act, batch)

        @block.vector
        def _(dve):
            own = Steps(dve, own_s)

            def rows(i):
                for t in range(TPB):
                    ins = normalise(dve, sb, TPB * i + t, xn[:, t, :])
                ins.then_inc(xn_ready, 1)

            def unit(i, u, b):
                dve.wait_ge(unit_ps, STEPS * i + u + 1)
                if u == 2:
                    for h in range(2):
                        r = slice(h * KVC, (h + 1) * KVC)
                        ins = dve.tensor_scalar(ckv[r, b, h, :], U[r, 0:SEQ], blat[r, 2:3], None, ALU.add)
                elif u == 3:
                    ins = dve.tensor_copy(ckvt[:, b, :, :].rearrange("p t c -> p (t c)"), U[:, 0:TPB * KVC])
                else:
                    for n in range(2):
                        p = 2 * (u - 4) + n
                        ins = dve.tensor_scalar(qT[:, b, p, :], U[:, n * SEQ:(n + 1) * SEQ], aqb[:, p:p + 1], None, ALU.add)
                ins.then_inc(unit_sb, 1)

            def maxima(n, st):
                dve.wait_ge(scores, n + 1)
                own.done(dve.tensor_reduce(mx[:, st % 2, :], S(st).rearrange("p b (h k) -> p (b h) k", h=2), AX, ALU.max))
                dve.tensor_scalar(mx[:, st % 2, :], mx[:, st % 2, :], -SCALE0, None, ALU.mult).then_inc(max_ready, 1)

            def divide(n, st):
                dve.wait_ge(exp_done, n + 1)
                own.done(dve.reciprocal(rinv[:, st % 2, :], sums[:, st % 2, :]))
                for j in range(4):
                    ins = dve.tensor_scalar(prob[:, st % 2, j, :], prob[:, st % 2, j, :], rinv[:, st % 2, j:j + 1], None, ALU.mult)
                ins.then_inc(prob_ready, 1)

            def context(n, st):
                dve.wait_ge(ctx_ps, n + 1)
                dve.tensor_copy(ctxT[:, st // 4 % 2, st % 4 * 2 * P:(st % 4 + 1) * 2 * P], C).then_inc(ctx_sb, 1)

            def add_bias(tile):
                dve.wait_ge(out_ps, tile + 1)
                dve.tensor_tensor(y[:], O, bo[:], ALU.add).then_inc(out_read, 1)

            def residual(tile, i):
                x = row(sb["x"], tile)
                dve.wait_ge(out_read, tile + 1)
                own.done(dve.tensor_tensor(y[:], y[:], row(ga, i), ALU.mult))
                own.done(dve.tensor_tensor(x, x, y[:], ALU.add))
                row_stats(dve, sb, tile)

            def batch(i, b, first, last):
                if not first:
                    own.start(before + per_batch * (i - 1))
                for st in range(STEPS):
                    n = STEPS * i + st
                    if not (first and st == 0):
                        context(n - 1, st - 1)
                    if st == 0 and not last:
                        rows(i + 1)
                    dve.wait_ge(pT_ps, n + 1)
                    dve.tensor_copy(probT[:, 2:4, :, :].rearrange("p h k q -> p (h k q)"), ps[:, 5, :]).then_inc(pT_dve, 1)
                    if not (last and st == STEPS - 1):
                        divide(n + 1, st + 1)
                    finished = st % 4 == 0 and not (first and st == 0)
                    tile = TPB * i + st // 4 - 1
                    if finished:
                        add_bias(tile)
                    if not (last and st + 2 >= STEPS):
                        maxima(n + 2, st)
                    if finished:
                        residual(tile, i if st else i - 1)
                    if not last and st in DVE_UNITS:
                        unit(i + 1, st, 1 - b)
                if not first:
                    assert last or own.n == per_batch, own.n

            dve.memset(ckv[:], 0.0).then_inc(zeroed, 1)
            row_scales(dve, own, sb, var_ready, root_done)
            dve.wait_ge(zeroed, 1)
            rows(0)
            for u in DVE_UNITS:
                unit(0, u, 0)
            maxima(0, 0)
            maxima(1, 1)
            divide(0, 0)
            per_batch = 2 * STEPS + 4
            before = own.n + per_batch - 2
            dve.wait_ge(ga_loaded, 32)
            batches(dve, batch)
            context(STEPS * NBATCH - 1, STEPS - 1)
            add_bias(TILES - 1)
            residual(TILES - 1, NBATCH - 1)


class WayBack:

    def __init__(self, alloc, sem, sb, l):
        self.sb, self.l = sb, l
        self.flight = 4 if l else 8
        self.g = alloc("g", [P, self.flight, 2, HID])
        self.acc = alloc("acc", [P, 2, 2, HID])
        self.got = [sem(f"got{n}") for n in range(self.flight)]
        self.x_new = sem("x_new")

    def gather(self, pool, ys):
        for t in range(TILES):
            if t >= self.flight:
                pool.wait_ge(self.x_new, t - self.flight + 1)
            for n in range(2):
                pool.indirect_dma_start(self.g[:, t % self.flight, n, :], None, ys,
                                        bass.IndirectOffsetOnAxis(ap=self.sb["pos"][:, n, t:t + 1], axis=0),
                                        bounds_check=NSPARSE * P - 1).then_inc(self.got[t % self.flight], 16)

    def add(self, dve, own, t, shared=None):
        slot, prob, pair = t % self.flight, self.sb["prob"], slice(t, t + 2)
        x, acc = self.sb["x"][:, pair, :], self.acc[:, t // 2 % 2, :, :]
        for k in range(2):
            dve.wait_ge(self.got[slot + k], 32 * (t // self.flight + 1))
            ins = dve.tensor_scalar(acc[:, k, :], self.g[:, slot + k, 0, :], prob[:, 0, t + k:t + k + 1], None, ALU.mult)
        own.done(ins)
        for k in range(2):
            ins = dve.scalar_tensor_tensor(acc[:, k, :], self.g[:, slot + k, 1, :], prob[:, 1, t + k:t + k + 1], acc[:, k, :], ALU.mult, ALU.add)
        own.done(ins)
        if shared is not None:
            own.done(dve.tensor_tensor(acc, acc, shared, ALU.add))
        own.done(dve.tensor_tensor(acc, acc, self.sb["gb"][:, t // TPB:t // TPB + 1, :].to_broadcast([P, 2, HID]), ALU.mult))
        dve.tensor_tensor(x, x, acc, ALU.add).then_inc(self.x_new, 2)


def attention1(nc, io, sb, modd, ys):
    with ExitStack() as ctx:
        s = lambda n, shape: ctx.enter_context(nc.sbuf_tensor(f"l1_{n}", shape, F32))
        sems = Sems(nc, ctx)
        q = lambda n: sems(f"l1_{n}")
        wlat = s("wlat", [P, HC, P])
        blat = s("blat", [P, 1])
        wqkv = s("wqkv", [P, 384 + 512])
        wkr = s("wkr", [P, HC, P])
        btok = s("btok", [1, 1024])
        bo = s("bo", [1, HID])
        ones = s("ones", [1, P])
        wo = s("wo", [P, HC, HID])
        rope = s("rope", [P, 2, TPB, DRH])
        ga = s("ga", [P, NBATCH, HID])
        xn = s("xn", [P, HID])
        hT = s("hT", [P, HC, P])
        cT = s("cT", [P, P])
        raw = s("raw", [P, 2, 2 * NH, DRH])
        qk = s("qk", [P, 2, 2, NH, DQK])
        rt = s("rt", [P, 2, 2 * NH, DRH])
        v = s("v", [P, TILES, DH, NH])
        sprod = s("sprod", [P, 2, NH, NH * DQK])
        vprod = s("vprod", [P, NH, DH * NH])
        sc = s("sc", [P, 2, NH, NH])
        red = s("red", [P, 3, NH])
        o = s("o", [P, NH * DH])
        oT = s("oT", [P, HC, P])
        y = s("y", [P, HID])
        ps = ctx.enter_context(nc.psum_tensor("l1_ps", [P, 8, 512], F32))
        var_ready, root_done, loaded, own_s, onesd = q("var_ready"), q("root_done"), q("loaded"), q("own"), q("ones")
        rest_loaded, late_loaded = q("rest_loaded"), q("late_loaded")
        back = WayBack(s, q, sb, 0)
        FIRST, OTHERS = slice(0, 2), slice(2, TILES)
        xn_ready, xT_ps, hT_sb, lat_ps, lat_sb, tok_ps, tok_sb, qk_ready = (
            q("xn_ready"), q("xT_ps"), q("hT_sb"), q("lat_ps"), q("lat_sb"), q("tok_ps"), q("tok_sb"), q("qk_ready"))
        pool_sprod, dve_sprod, sc_ready, exp_done, p_ready, pool_vprod, o_ready, oT_ps, oT_sb, out_ps, out_read = (
            q("pool_sprod"), q("dve_sprod"), q("sc_ready"), q("exp_done"), q("p_ready"), q("pool_vprod"), q("o_ready"), q("oT_ps"),
            q("oT_sb"), q("out_ps"), q("out_read"))
        block = ctx.enter_context(nc.Block())
        ident = sb["ident"]

        def tiles(eng, turn):
            for t in (0, 1):
                turn(t, t, 0, t == 0, TILES)
            with eng.Fori(1, TILES // 2 - 2) as i:
                turn(2 * i, 0, i, False, TILES)
                turn(2 * i + 1, 1, i, False, TILES)
            for t in range(TILES - 4, TILES):
                turn(t, t % 2, t // 2, False, TILES - 1 - t)

        def score_product(eng, u, a, b):
            n = b - a
            return eng.tensor_tensor(sprod[:, u, a:b, :].rearrange("p i (j d) -> p i j d", j=NH),
                                     qk[:, u, 0, a:b, :].rearrange("p i (o d) -> p i o d", o=1).to_broadcast([P, n, NH, DQK]),
                                     qk[:, u, 1, :, :].rearrange("p (o j) d -> p o j d", o=1).to_broadcast([P, n, NH, DQK]), ALU.mult)

        def value_product(eng, t, u, a, b):
            n = b - a
            return eng.tensor_tensor(vprod[:, a:b, :].rearrange("p i (d j) -> p i d j", d=DH),
                                     sc[:, u, a:b, :].rearrange("p i (o j) -> p i o j", o=1).to_broadcast([P, n, DH, NH]),
                                     v[:, bass.ds(t, 1), :, :].to_broadcast([P, n, DH, NH]), ALU.mult)

        @block.sync
        def _(sp):
            for dst, name in ((wlat, "l1_wlat"), (blat, "l1_blat"), (wqkv, "l1_wqkv"), (wkr, "l1_wkr"), (btok, "l1_btok")):
                sp.dma_start(dst[:], io[name]).then_inc(loaded, 16)
            for dst, name in ((rope, "l1_rope"), (wo, "l1_wo"), (bo, "l1_bo")):
                sp.dma_start(dst[:], io[name]).then_inc(rest_loaded, 16)
            sp.wait_ge(back.x_new, 6)
            sp.dma_start(ga[:], modd[1:2, :, GA * HID:(GA + 1) * HID].to_broadcast([P, NBATCH, HID])).then_inc(late_loaded, 16)
            sp.dma_start(sb["modb"][:], modd[1:2, :, SB * HID:(CB + 1) * HID].to_broadcast([P, NBATCH, 2 * HID])).then_inc(late_loaded, 16)

        @block.tensor
        def _(pe):
            def front(t, u):
                bank = 2 + 2 * u
                pe.wait_ge(xn_ready, t + 1)
                for c in range(HC):
                    ins = pe.transpose(ps[:, 0, c * P:(c + 1) * P], xn[:, c * P:(c + 1) * P], ident[:])
                ins.then_inc(xT_ps, 1)
                if not isinstance(t, int) or t > 1:
                    pe.wait_ge(tok_sb, t - 1)
                for n in range(2):
                    pe.matmul(ps[:, bank + n, :], ones[:], btok[:, n * 512:(n + 1) * 512], start=True, stop=False)
                pe.wait_ge(hT_sb, t + 1)
                for c in range(HC):
                    ins = pe.matmul(ps[:, 1, 0:P], wlat[:, c, :], hT[:, c, :], start=(c == 0), stop=(c == HC - 1))
                ins.then_inc(lat_ps, 1)
                for c in range(HC):
                    pe.matmul(ps[:, bank, 384:512], hT[:, c, :], wkr[:, c, :], start=False, stop=False)
                pe.wait_ge(lat_sb, t + 1)
                pe.matmul(ps[:, bank, 0:384], cT[:], wqkv[:, 0:384], start=False, stop=True)
                pe.matmul(ps[:, bank + 1, :], cT[:], wqkv[:, 384:896], start=False, stop=True).then_inc(tok_ps, 1)

            def tail(t, first):
                pe.wait_ge(o_ready, t + 1)
                for c in range(HC):
                    ins = pe.transpose(ps[:, 6, c * P:(c + 1) * P], o[:, c * P:(c + 1) * P], ident[:])
                ins.then_inc(oT_ps, 1)
                if not first:
                    pe.wait_ge(out_read, t)
                pe.matmul(ps[:, 7, 0:HID], ones[:], bo[:], start=True, stop=False)
                pe.wait_ge(oT_sb, t + 1)
                for c in range(HC):
                    ins = pe.matmul(ps[:, 7, 0:HID], oT[:, c, :], wo[:, c, :], start=False, stop=(c == HC - 1))
                ins.then_inc(out_ps, 1)

            def turn(t, u, i, first, left):
                if left >= 3:
                    front(t + 3, 1 - u)
                tail(t, first)

            pe.wait_ge(loaded, 80)
            pe.wait_ge(onesd, 1)
            for t in range(3):
                front(t, t % 2)
            pe.wait_ge(rest_loaded, 48)
            tiles(pe, turn)

        @block.scalar
        def _(act):
            def front(t, u, b):
                act.activation(xn[:], row(sb["x"], t), ACT.Identity, scale=sb["rstd"][:, bass.ds(t, 1)],
                               bias=sb["shift"][:, bass.ds(t, 1)]).then_inc(xn_ready, 1)
                act.wait_ge(xT_ps, t + 1)
                for c in range(HC):
                    ins = act.activation(hT[:, c, :], ps[:, 0, c * P:(c + 1) * P], ACT.Identity,
                                         scale=sb["modT"][:, 1, CT_CA + c, bass.ds(b, 1)], bias=sb["modT"][:, 1, CT_SA + c, bass.ds(b, 1)])
                ins.then_inc(hT_sb, 1)
                act.wait_ge(lat_ps, t + 1)
                act.activation(cT[:], ps[:, 1, 0:P], ACT.Identity, bias=blat[:]).then_inc(lat_sb, 1)
                act.wait_ge(tok_ps, t + 1)
                if not isinstance(t, int) or t > 1:
                    act.wait_ge(pool_sprod, t - 1)
                    act.wait_ge(dve_sprod, t - 1)
                bank = 2 + 2 * u
                heads = lambda a: a.rearrange("p (h d) -> p h d", h=NH)
                act.activation(qk[:, u, 0, :, 0:DH], heads(ps[:, bank, 0:256]), ACT.Copy)
                act.activation(raw[:, u, :, :].rearrange("p h d -> p (h d)"), ps[:, bank, 256:512], ACT.Copy)
                act.activation(qk[:, u, 1, :, 0:DH], heads(ps[:, bank + 1, 0:256]), ACT.Copy)
                act.activation(v[:, bass.ds(t, 1), :, :].rearrange("p o d j -> p j (o d)"), heads(ps[:, bank + 1, 256:512]),
                               ACT.Copy).then_inc(tok_sb, 1)

            def exp(t, u):
                act.wait_ge(sc_ready, t + 1)
                act.activation(sc[:, u, :, :], sc[:, u, :, :], ACT.Exp, scale=SCALE1).then_inc(exp_done, 1)

            def turn(t, u, i, first, left):
                if left >= 3:
                    front(t + 3, 1 - u, i + (u + 3) // 2)
                if left >= 1:
                    exp(t + 1, 1 - u)
                act.wait_ge(oT_ps, t + 1)
                act.activation(oT[:].rearrange("p c q -> p (c q)"), ps[:, 6, 0:HID], ACT.Copy).then_inc(oT_sb, 1)

            row_roots(act, sb, var_ready, root_done, FIRST)
            act.wait_ge(root_done, 2)
            act.wait_ge(loaded, 80)
            front(0, 0, 0)
            front(1, 1, 0)
            row_roots(act, sb, var_ready, root_done, OTHERS, 1)
            act.wait_ge(root_done, 4)
            front(2, 0, 1)
            exp(0, 0)
            tiles(act, turn)

        @block.gpsimd
        def _(pool):
            def scores(t, u):
                pool.wait_ge(qk_ready, t + 1)
                if not isinstance(t, int) or t > 1:
                    pool.wait_ge(sc_ready, t - 1)
                score_product(pool, u, NH - POOL_S, NH).then_inc(pool_sprod, 1)

            def turn(t, u, i, first, left):
                pool.wait_ge(p_ready, t + 1)
                value_product(pool, t, u, NH - POOL_V, NH).then_inc(pool_vprod, 1)
                if left >= 2:
                    scores(t + 2, u)

            back.gather(pool, ys)
            scores(0, 0)
            scores(1, 1)
            tiles(pool, turn)

        @block.vector
        def _(dve):
            own = Steps(dve, own_s)

            def rotate(t, u):
                dve.wait_ge(tok_sb, t + 1)
                r = raw[:, u, :, :]
                table = lambda n, a, b: rope[:, n, u:u + 1, a:b].to_broadcast([P, 2 * NH, b - a])
                hf = DRH // 2
                dve.tensor_tensor(rt[:, 0, :, :], r, table(0, 0, DRH), ALU.mult)
                dve.tensor_tensor(rt[:, 1, :, 0:hf], r[:, :, hf:DRH], table(1, 0, hf), ALU.mult)
                own.done(dve.tensor_tensor(rt[:, 1, :, hf:DRH], r[:, :, 0:hf], table(1, hf, DRH), ALU.mult))
                dve.tensor_tensor(qk[:, u, :, :, DH:DQK].rearrange("p n h d -> p (n h) d"), rt[:, 0, :, :], rt[:, 1, :, :],
                                  ALU.add).then_inc(qk_ready, 1)
                dve.wait_ge(qk_ready, t + 1)
                score_product(dve, u, 0, NH - POOL_S).then_inc(dve_sprod, 1)

            def scores(t, u):
                dve.wait_ge(dve_sprod, t + 1)
                dve.wait_ge(pool_sprod, t + 1)
                own.done(dve.tensor_reduce(sc[:, u, :, :], sprod[:, u, :, :].rearrange("p i (j d) -> p i j d", j=NH), AX, ALU.add))
                own.done(dve.tensor_reduce(red[:, 0, :], sc[:, u, :, :], AX, ALU.max))
                dve.tensor_tensor(sc[:, u, :, :], sc[:, u, :, :], each(0), ALU.subtract).then_inc(sc_ready, 1)

            each = lambda k: red[:, k, :].rearrange("p (i o) -> p i o", o=1).to_broadcast([P, NH, NH])

            def probabilities(t, u):
                dve.wait_ge(exp_done, t + 1)
                own.done(dve.tensor_reduce(red[:, 1, :], sc[:, u, :, :], AX, ALU.add))
                own.done(dve.reciprocal(red[:, 2, :], red[:, 1, :]))
                dve.tensor_tensor(sc[:, u, :, :], sc[:, u, :, :], each(2), ALU.mult).then_inc(p_ready, 1)

            def values(t, u, first):
                dve.wait_ge(p_ready, t + 1)
                own.done(value_product(dve, t, u, 0, NH - POOL_V))
                dve.wait_ge(pool_vprod, t + 1)
                if not first:
                    dve.wait_ge(oT_ps, t)
                dve.tensor_reduce(o[:], vprod[:].rearrange("p i (d j) -> p (i d) j", d=DH), AX, ALU.add).then_inc(o_ready, 1)

            def output(t, b):
                x = row(sb["x"], t)
                dve.wait_ge(out_ps, t + 1)
                dve.tensor_tensor(y[:], ps[:, 7, 0:HID], row(ga, b), ALU.mult).then_inc(out_read, 1)
                dve.wait_ge(out_read, t + 1)
                own.done(dve.tensor_tensor(x, x, y[:], ALU.add))
                row_stats(dve, sb, t)

            def turn(t, u, i, first, left):
                if left > 0:
                    own.start(before if first else before + 7 * t - 1)
                if left >= 2:
                    rotate(t + 2, u)
                if not first:
                    output(t - 1, i - (1 - u))
                if left >= 1:
                    scores(t + 1, 1 - u)
                values(t, u, first)
                if left >= 1:
                    probabilities(t + 1, 1 - u)
                assert left < 2 or own.n == 7 - first, own.n

            dve.memset(ones[:], 1.0).then_inc(onesd, 1)
            for before, part in enumerate((FIRST, OTHERS)):
                for t in range(part.start, part.stop, 2):
                    if t == 8:
                        dve.wait_ge(rest_loaded, 48)
                        rotate(0, 0)
                    if t == 12:
                        rotate(1, 1)
                    back.add(dve, own, t)
                    dve.wait_ge(back.x_new, t + 2)
                    for k in range(2):
                        ins = row_stats(dve, sb, t + k)
                own.done(ins)
                row_scales(dve, own, sb, var_ready, root_done, part, before)
            scores(0, 0)
            probabilities(0, 0)
            before = own.n
            dve.wait_ge(late_loaded, 32)
            tiles(dve, turn)
            output(TILES - 1, NBATCH - 1)


class SharedExpert:

    def __init__(self, nc, alloc, sem, w, ident, ps, keep, start, count):
        self.nc, (self.wg, self.wu, self.wd), self.ident, self.ps, self.keep = nc, w, ident, ps, keep
        self.start, self.count = start, count
        self.xT, self.sg, self.gu, self.aT = (
            alloc("xT", [P, 2, HC, P]), alloc("sg", [P, F1]), alloc("gu", [P, 2, F1]), alloc("aT", [P, F1C, P]))
        self.xT_ready, self.g_ps, self.u_ps, self.silu_done, self.a_ready, self.aT_ps, self.aT_sb, self.y_ps, self.y_sb = (
            sem(n) for n in ("xT_ready", "g_ps", "u_ps", "silu", "a_ready", "aT_ps", "aT_sb", "y_ps", "y_sb"))
        self.G, self.U, self.AT, self.Y = (0, 1), (5, 6), 7, 2

    def loop(self, eng, first, both, last):
        first(0)
        both(0, 0)
        both(1, 1)
        with eng.Fori(1, self.count // 2 - 1) as i:
            both(2 * i, 0)
            both(2 * i + 1, 1)
        both(self.count - 2, 0)
        last(self.count - 1)

    def tensor(self, pe):
        half = F1 // 2

        def gate_up(t, u):
            pe.wait_ge(self.xT_ready, t + 1)
            for n in range(2):
                for w, bank, signal in ((self.wg, self.G[n], self.g_ps), (self.wu, self.U[n], self.u_ps)):
                    for c in range(HC):
                        ins = pe.matmul(self.ps[:, bank, 0:half], self.xT[:, u, c, :], w[:, c, NE, n * half:(n + 1) * half],
                                        start=(c == 0), stop=(c == HC - 1))
                    ins.then_inc(signal, 1)

        def turn(t, u):
            pe.wait_ge(self.a_ready, 2 * t + 2)
            for k in range(F1C):
                ins = pe.transpose(self.ps[:, self.AT, k * P:(k + 1) * P], self.gu[:, u, k * P:(k + 1) * P], self.ident[:])
            ins.then_inc(self.aT_ps, 1)

        def down(t):
            pe.wait_ge(self.aT_sb, t + 1)
            if not isinstance(t, int) or t > 0:
                pe.wait_ge(self.y_sb, t)
            for k in range(F1C):
                ins = pe.matmul(self.ps[:, self.Y, 0:HID], self.aT[:, k, :], self.wd[:, NE * F1C + k, :], start=(k == 0), stop=(k == F1C - 1))
            ins.then_inc(self.y_ps, 1)

        def both(t, u):
            turn(t, u)
            gate_up(t + 1, 1 - u)
            down(t)

        def last(t):
            turn(t, 1)
            down(t)

        self.loop(pe, lambda t: gate_up(t, 0), both, last)

    def scalar(self, act):
        half = F1 // 2

        def xt(t, u):
            if not isinstance(t, int) or t > 1:
                act.wait_ge(self.u_ps, 2 * t - 2)
            act.activation(self.xT[:, u, :, :].rearrange("p c q -> p (c q)"), row(self.keep, self.start + t), ACT.Copy).then_inc(self.xT_ready, 1)

        def silu(t):
            for n in range(2):
                act.wait_ge(self.g_ps, 2 * t + n + 1)
                if not isinstance(t, int) or t > 0:
                    act.wait_ge(self.a_ready, 2 * t + n - 1)
                act.activation(self.sg[:, n * half:(n + 1) * half], self.ps[:, self.G[n], 0:half], ACT.Silu).then_inc(self.silu_done, 1)

        def at(t):
            act.wait_ge(self.aT_ps, t + 1)
            act.activation(self.aT[:].rearrange("p k q -> p (k q)"), self.ps[:, self.AT, :], ACT.Copy).then_inc(self.aT_sb, 1)

        def first(t):
            xt(0, 0)
            silu(0)

        def both(t, u):
            xt(t + 1, 1 - u)
            at(t)
            silu(t + 1)

        self.loop(act, first, both, at)

    def mul(self, dve, t, u):
        half = F1 // 2
        for n in range(2):
            dve.wait_ge(self.silu_done, 2 * t + n + 1)
            dve.wait_ge(self.u_ps, 2 * t + n + 1)
            dve.tensor_tensor(self.gu[:, u, n * half:(n + 1) * half], self.sg[:, n * half:(n + 1) * half], self.ps[:, self.U[n], 0:half],
                              ALU.mult).then_inc(self.a_ready, 1)

    def result(self, dve, t):
        dve.wait_ge(self.y_ps, t + 1)
        dve.tensor_copy(row(self.keep, self.start + t), self.ps[:, self.Y, 0:HID]).then_inc(self.y_sb, 1)

    def vector(self, dve):
        def both(t, u):
            self.mul(dve, t + 1, 1 - u)
            self.result(dve, t)

        self.loop(dve, lambda t: self.mul(dve, t, 0), both, lambda t: self.result(dve, t))


EARLY = 8


def mixture(nc, io, sb, modd, l, xs, ys, out):
    F, FC = ((F0, F0C), (F1, F1C))[l]
    ne = NE + l
    nt = NSPARSE
    FP = FC * P
    half = F // 2
    with ExitStack() as ctx:
        s = lambda n, shape, dt=F32: ctx.enter_context(nc.sbuf_tensor(f"m{l}_{n}", shape, dt))
        sems = Sems(nc, ctx)
        q = lambda n: sems(f"m{l}_{n}")
        wg, wu = s("wg", [P, HC, ne, F]), s("wu", [P, HC, ne, F])
        wd = s("wd", [P, ne * FC, HID])
        pos, prob = sb["pos"], sb["prob"]
        eid = s("eid", [1, nt], U32)
        w_loaded = q("w_loaded")
        keep = s("keep", [P, TILES, HID]) if l else None

        with ExitStack() as rc:
            t_ = lambda n, shape, dt=F32: rc.enter_context(nc.sbuf_tensor(f"r{l}_{n}", shape, dt))
            part_sems = Sems(nc, rc)
            r = lambda n, part_sems=part_sems: part_sems(f"r{l}_{n}")
            h = t_("h", [P, TILES, HID])
            hcur = t_("hcur", [P, TPB, HID])
            xn = t_("xn", [P, TPB, HID])
            wr = t_("wr", [P, HC, NE])
            var_ready, root_done = r("var_ready"), r("root_done")
            hT = t_("hT", [P, 2, HC, P])
            rk = t_("rk", [P, 9, TILES, NE])
            sm = t_("sm", [P, 8, TILES])
            cst = t_("cst", [P, 2 * P + 96])
            tri, ones_m, rev = cst[:, 0:P], cst[:, P:2 * P], cst[:, 2 * P:2 * P + NE]
            thr, tile_no = cst[:, 2 * P + 16:2 * P + 32], cst[0:1, 2 * P + 32:2 * P + 32 + NSPARSE]
            ex = t_("ex", [P, 4, NE])
            ecmp = t_("ecmp", [P, NE * TILES])
            ejc = t_("ejc", [1, NSPARSE, NE])
            ejs = t_("ejs", [1, nt])
            ps = rc.enter_context(nc.psum_tensor(f"r{l}_ps", [P, 8, 512], F32))
            gb_loaded, shared_loaded, xn_ready, scaled, h_kept = r("gb_loaded"), r("shared_loaded"), r("xn_ready"), r("scaled"), r("h_kept")
            own_s, loaded, h_ready, hT_ps, hT_sb, logits, masks, ranks, diff, e2, pos_ready, sent = (
                r("own"), r("loaded"), r("h_ready"), r("hT_ps"), r("hT_sb"), r("logits"), r("masks"),
                r("ranks"), r("diff"), r("e2"), r("pos_ready"), r("sent"))
            if l:
                early = SharedExpert(nc, lambda n, shape: t_("s" + n, shape), lambda n: r("s" + n), (wg, wu, wd), sb["ident"], ps, keep, 0, EARLY)
            block = rc.enter_context(nc.Block())

            @block.sync
            def _(sp):
                sp.dma_start(wr[:], io[f"l{l}_wr"]).then_inc(loaded, 16)
                sp.dma_start(cst[:], io["cst"]).then_inc(loaded, 16)
                if l:
                    sp.dma_start(wg[:, :, NE, :], io["l1_wg"][:, :, NE, :]).then_inc(shared_loaded, 16)
                    sp.dma_start(wu[:, :, NE, :], io["l1_wu"][:, :, NE, :]).then_inc(shared_loaded, 16)
                    sp.dma_start(wd[:, NE * FC:, :], io["l1_wd"][:, NE * FC:, :]).then_inc(shared_loaded, 16)
                    sp.dma_start(sb["gb"][:], modd[1:2, :, GB * HID:(GB + 1) * HID].to_broadcast([P, NBATCH, HID])).then_inc(gb_loaded, 16)
                    sp.wait_ge(gb_loaded, 16)
                sp.dma_start(wd[:, 0:NE * FC, :], io[f"l{l}_wd"][:, 0:NE * FC, :]).then_inc(w_loaded, 16)
                for c in range(HC):
                    sp.dma_start(wg[:, c, 0:NE, :], io[f"l{l}_wg"][:, c, 0:NE, :]).then_inc(w_loaded, 16)
                    sp.dma_start(wu[:, c, 0:NE, :], io[f"l{l}_wu"][:, c, 0:NE, :]).then_inc(w_loaded, 16)

            @block.scalar
            def _(act):
                row_roots(act, sb, var_ready, root_done)
                act.wait_ge(root_done, 2)

                def rows(tile, t):
                    act.activation(xn[:, t, :], row(sb["x"], tile), ACT.Identity, scale=sb["rstd"][:, bass.ds(tile, 1)],
                                   bias=sb["shift"][:, bass.ds(tile, 1)]).then_inc(xn_ready, 1)

                def channels(tile, t):
                    act.wait_ge(hT_ps, tile + 1)
                    if l:
                        act.activation(row(keep, tile), ps[:, t, 0:HID], ACT.Copy)
                    act.activation(hT[:, t, :, :].rearrange("p c q -> p (c q)"), ps[:, t, 0:HID], ACT.Copy).then_inc(hT_sb, 1)

                for t in range(TPB):
                    rows(t, t)
                with act.Fori(0, NBATCH - 1) as i:
                    for t in range(TPB):
                        channels(TPB * i + t, t)
                        act.wait_ge(h_kept, TPB * i + t + 1)
                        rows(TPB * (i + 1) + t, t)
                for t in range(TPB):
                    channels(TILES - TPB + t, t)
                act.wait_ge(diff, 1)
                act.activation(sm[:, 3, :], sm[:, 2, :], ACT.Exp).then_inc(e2, 1)
                if l:
                    early.scalar(act)

            @block.tensor
            def _(pe):
                pe.wait_ge(loaded, 32)
                def channels(tile, t):
                    pe.wait_ge(h_ready, tile + 1)
                    pe.wait_ge(hT_sb, tile + 1)
                    for c in range(HC):
                        ins = pe.transpose(ps[:, t, c * P:(c + 1) * P], hcur[:, t, c * P:(c + 1) * P], sb["ident"][:])
                    ins.then_inc(hT_ps, 1)

                def score(tile, t):
                    pe.wait_ge(hT_sb, tile + 3)
                    for c in range(HC):
                        ins = pe.matmul(ps[:, 2, bass.ds(tile * NE, NE)], hT[:, t, c, :], wr[:, c, :], start=(c == 0), stop=(c == HC - 1))
                    ins.then_inc(logits, 1)

                channels(0, 0)
                with pe.Fori(0, NBATCH - 1) as i:
                    for t in range(TPB):
                        channels(TPB * i + t + 1, 1 - t)
                        score(TPB * i + t, t)
                channels(TILES - 1, 1)
                score(TILES - 2, 0)
                score(TILES - 1, 1)
                pe.wait_ge(masks, 1)
                m = rk[:, 4, :, :].rearrange("p t e -> p (t e)")
                pe.matmul(ps[:, 3, 0:P], tri, m, start=True, stop=True)
                pe.matmul(ps[:, 4, 0:P], ones_m, m, start=True, stop=True).then_inc(ranks, 1)
                if l:
                    pe.wait_ge(shared_loaded, 48)
                    early.tensor(pe)

            @block.vector
            def _(dve):
                own = Steps(dve, own_s)
                dve.memset(rk[:, 0, 0, 0:1], 0.0).then_inc(hT_sb, 2)
                row_scales(dve, own, sb, var_ready, root_done)
                with dve.Fori(0, NBATCH) as i:
                    for t in range(TPB):
                        tile = TPB * i + t
                        dve.wait_ge(xn_ready, tile + 1)
                        dve.tensor_tensor(xn[:, t, :], xn[:, t, :], row(sb["modb"], i)[:, HID:2 * HID], ALU.mult).then_inc(scaled, 1)
                        dve.wait_ge(scaled, tile + 1)
                        dve.wait_ge(hT_sb, tile + 1)
                        dve.tensor_tensor(hcur[:, t, :], xn[:, t, :], row(sb["modb"], i)[:, 0:HID], ALU.add).then_inc(h_ready, 1)
                dve.wait_ge(loaded, 32)
                dve.wait_ge(logits, TILES)
                v = lambda k: rk[:, k, :, :]
                bc = lambda k: sm[:, k, :].rearrange("p (t o) -> p t o", o=1).to_broadcast([P, TILES, NE])
                rev_b = rev.rearrange("p (o e) -> p o e", o=1).to_broadcast([P, TILES, NE])
                own.done(dve.tensor_copy(v(0).rearrange("p t e -> p (t e)"), ps[:, 2, 0:P]))
                for n in range(2):
                    own.done(dve.tensor_reduce(sm[:, n, :], v(0), AX, ALU.max))
                    own.done(dve.tensor_tensor(v(1), v(0), bc(n), ALU.is_equal))
                    own.done(dve.tensor_tensor(v(1), v(1), rev_b, ALU.mult))
                    own.done(dve.tensor_reduce(sm[:, 4, :], v(1), AX, ALU.max))
                    own.done(dve.tensor_tensor(v(2 + n), bc(4), rev_b, ALU.is_equal))
                    if n == 0:
                        own.done(dve.scalar_tensor_tensor(v(0), v(2), -3.0e38, v(0), ALU.mult, ALU.add))
                dve.tensor_tensor(v(4), v(2), v(3), ALU.add).then_inc(masks, 1)
                dve.tensor_tensor(sm[:, 2, :], sm[:, 1, :], sm[:, 0, :], ALU.subtract).then_inc(diff, 1)
                dve.wait_ge(e2, 1)
                own.done(dve.tensor_scalar(sm[:, 5, :], sm[:, 3, :], 1.0, None, ALU.add))
                own.done(dve.reciprocal(prob[:, 0, :], sm[:, 5, :]))
                own.done(dve.tensor_tensor(prob[:, 1, :], prob[:, 0, :], sm[:, 3, :], ALU.mult))
                dve.wait_ge(ranks, 1)
                own.done(dve.tensor_copy(v(5).rearrange("p t e -> p (t e)"), ps[:, 4, 0:P]))
                a, b = 5, 6
                for d in (1, 2, 4, 8):
                    dve.tensor_copy(rk[:, b, 0:d, :], rk[:, a, 0:d, :])
                    own.done(dve.tensor_tensor(rk[:, b, d:, :], rk[:, a, d:, :], rk[:, a, 0:TILES - d, :], ALU.add))
                    a, b = b, a
                cnt = rk[:, a, TILES - 1, :]
                ec = ecmp[:].rearrange("p (e k) -> p e k", e=NE)
                own.done(dve.tensor_tensor(ec, cnt.rearrange("p (e o) -> p e o", o=1).to_broadcast([P, NE, TILES]),
                                           thr.rearrange("p (o k) -> p o k", o=1).to_broadcast([P, NE, TILES]), ALU.is_gt))
                own.done(dve.tensor_reduce(ex[:, 0, :], ec, AX, ALU.add))
                for d, ea, eb in ((1, 0, 1), (2, 1, 2), (4, 2, 1)):
                    dve.tensor_copy(ex[:, eb, 0:d], ex[:, ea, 0:d])
                    own.done(dve.tensor_tensor(ex[:, eb, d:], ex[:, ea, d:], ex[:, ea, 0:NE - d], ALU.add))
                incl = ex[:, 1, :]
                own.done(dve.memset(ex[:, 3, 0:1], 0.0))
                own.done(dve.tensor_scalar(ex[:, 3, 1:NE], incl[:, 0:NE - 1], float(P), None, ALU.mult))
                own.done(dve.tensor_tensor(v(7), ex[:, 3, :].rearrange("p (o e) -> p o e", o=1).to_broadcast([P, TILES, NE]),
                                           ps[:, 3, 0:P].rearrange("p (t e) -> p t e", e=NE), ALU.add))
                own.done(dve.tensor_tensor(rk[:, 7, 1:, :], rk[:, 7, 1:, :], rk[:, a, 0:TILES - 1, :], ALU.add))
                for n in range(2):
                    own.done(dve.tensor_tensor(v(8), v(7), v(2 + n), ALU.mult))
                    own.done(dve.tensor_reduce(sm[:, 6 + n, :], v(8), AX, ALU.add))
                    own.done(dve.tensor_copy(pos[:, n, :], sm[:, 6 + n, :]))
                dve.memset(ecmp[:, 0:1], 0.0).then_inc(pos_ready, 1)
                own.done(dve.tensor_tensor(ejc[:, :, 0:NE - 1],
                                           tile_no.rearrange("p (j o) -> p j o", o=1).to_broadcast([1, NSPARSE, NE - 1]),
                                           incl[0:1, 0:NE - 1].rearrange("p (o e) -> p o e", o=1).to_broadcast([1, NSPARSE, NE - 1]), ALU.is_ge))
                own.done(dve.tensor_reduce(ejs[:, 0:NSPARSE], ejc[:, :, 0:NE - 1], AX, ALU.add))
                own.done(dve.tensor_copy(eid[:], ejs[:]))
                if l:
                    early.vector(dve)

            @block.gpsimd
            def _(pool):
                with pool.Fori(0, NBATCH) as i:
                    for t in range(TPB):
                        pool.wait_ge(scaled, TPB * i + t + 1)
                        pool.tensor_tensor(row(h, TPB * i + t), xn[:, t, :], row(sb["modb"], i)[:, 0:HID], ALU.add).then_inc(h_kept, 1)
                pool.wait_ge(h_kept, TILES)
                pool.wait_ge(pos_ready, 1)
                for t in range(TILES):
                    for n in range(2):
                        pool.indirect_dma_start(xs[0:NSPARSE * P, :], bass.IndirectOffsetOnAxis(ap=pos[:, n, t:t + 1], axis=0),
                                                h[:, t, :], None, bounds_check=NSPARSE * P - 1).then_inc(sent, 16)
                pool.wait_ge(sent, 16 * 2 * TILES)

        with ExitStack() as ec:
            t_ = lambda n, shape, dt=F32: ec.enter_context(nc.sbuf_tensor(f"e{l}_{n}", shape, dt))
            part_sems = Sems(nc, ec)
            r = lambda n, part_sems=part_sems: part_sems(f"e{l}_{n}")
            xin = t_("xin", [P, 2, HID])
            xT = t_("xT", [P, 2, HC, P])
            sg = t_("sg", [P, F])
            a = t_("a", [P, 2, FP])
            aT = t_("aT", [P, FC, P])
            yo = t_("yo", [P, 2, HID])
            ps = ec.enter_context(nc.psum_tensor(f"e{l}_ps", [P, 8, 512], F32))
            pad_zero, x_loaded, xT_ps, xT_sb, g_ps, u_ps, silu_done, a_ready, aT_ps, aT_act, aT_dve, y_ps, y_sb, y_st = (
                r("pad_zero"), [r("x_loaded0"), r("x_loaded1")], r("xT_ps"), r("xT_sb"), r("g_ps"), r("u_ps"), r("silu"), r("a_ready"), r("aT_ps"),
                r("aT_act"), r("aT_dve"), r("y_ps"), r("y_sb"), [r("y_st0"), r("y_st1")])
            block = ec.enter_context(nc.Block())
            NA = min(FC, 4)

            assert nt % 2 == 1

            @block.sync
            def _(sp):
                def load(j, u):
                    sp.dma_start(xin[:, u, :], xs[bass.ds(j * P, P), :]).then_inc(x_loaded[u], 16)
                load(0, 0)
                load(1, 1)
                with sp.Fori(0, (nt - 1) // 2) as i:
                    for u in (0, 1):
                        sp.wait_ge(xT_ps, 2 * i + u + 1)
                        load(2 * i + u + 2, u)
                        sp.wait_ge(y_sb, 2 * i + u + 2)
                        sp.dma_start(ys[bass.ds((2 * i + u) * P, P), :], yo[:, u, :]).then_inc(y_st[u], 16)
                sp.wait_ge(y_sb, nt + 1)
                sp.dma_start(ys[(nt - 1) * P:nt * P, :], yo[:, 0, :]).then_inc(y_st[0], 16)
                sp.wait_ge(y_st[0], 16 * ((nt + 1) // 2))
                sp.wait_ge(y_st[1], 16 * ((nt - 1) // 2))
                sp.wait_ge(x_loaded[1], 16 * ((nt + 1) // 2))

            @block.tensor
            def _(pe):
                def rows(j, u, loads):
                    pe.wait_ge(x_loaded[u], loads)
                    pe.wait_ge(xT_sb, j + 1)
                    for c in range(HC):
                        ins = pe.transpose(ps[:, 6, c * P:(c + 1) * P], xin[:, u, c * P:(c + 1) * P], sb["ident"][:])
                    ins.then_inc(xT_ps, 1)

                def expert(j):
                    return pe.value_load(eid[0:1, bass.ds(j, 1)], min_val=0, max_val=NE - 1)

                def gate_up(j, u, ej):
                    pe.wait_ge(xT_sb, j + 2)
                    for n in range(2):
                        for w, bank, signal in ((wg, n, g_ps), (wu, 2 + n, u_ps)):
                            for c in range(HC):
                                ins = pe.matmul(ps[:, bank, 0:half], xT[:, u, c, :],
                                                w[:, c, bass.ds(ej, 1), n * half:(n + 1) * half].rearrange("p o f -> p (o f)"),
                                                start=(c == 0), stop=(c == HC - 1))
                            ins.then_inc(signal, 1)

                def turn(j, u):
                    pe.wait_ge(a_ready, 2 * j + 4)
                    for k in range(FC):
                        ins = pe.transpose(ps[:, 4 + k // 4, (k % 4) * P:(k % 4 + 1) * P], a[:, u, k * P:(k + 1) * P], sb["ident"][:])
                    ins.then_inc(aT_ps, 1)

                def down(j, ej):
                    pe.wait_ge(aT_act, j + 1)
                    if FC > 4:
                        pe.wait_ge(aT_dve, j + 1)
                    pe.wait_ge(y_sb, j + 1)
                    for k in range(FC):
                        ins = pe.matmul(ps[:, 7, 0:HID], aT[:, k, :], wd[:, bass.ds(ej * FC + k, 1), :].rearrange("p o c -> p (o c)"),
                                        start=(k == 0), stop=(k == FC - 1))
                    ins.then_inc(y_ps, 1)

                pe.wait_ge(w_loaded, 16 * (1 + 2 * HC))
                pe.wait_ge(pad_zero, 1)
                rows(0, 0, 16)
                gate_up(0, 0, expert(0))
                rows(1, 1, 16)
                with pe.Fori(0, (nt - 1) // 2) as i:
                    turn(2 * i, 0)
                    _, (here, middle, ahead) = nc.values_load_multi_w_load_instructions(
                        eid[0:1, bass.ds(2 * i, 3)], engines=[mybir.EngineType.PE], min_val=0, max_val=NE - 1)
                    gate_up(2 * i + 1, 1, middle)
                    rows(2 * i + 2, 0, 16 * i + 32)
                    down(2 * i, here)
                    turn(2 * i + 1, 1)
                    gate_up(2 * i + 2, 0, ahead)
                    rows(2 * i + 3, 1, 16 * i + 32)
                    down(2 * i + 1, middle)
                turn(nt - 1, 0)
                down(nt - 1, expert(nt - 1))

            @block.scalar
            def _(act):
                def xt(j, u):
                    act.wait_ge(xT_ps, j + 1)
                    act.activation(xT[:, u, :, :].rearrange("p c q -> p (c q)"), ps[:, 6, 0:HID], ACT.Copy).then_inc(xT_sb, 1)

                def silu(j, u):
                    for n in range(2):
                        act.wait_ge(g_ps, 2 * j + n + 1)
                        act.wait_ge(a_ready, 2 * j + n + 1)
                        act.activation(sg[:, n * half:(n + 1) * half], ps[:, n, 0:half], ACT.Silu).then_inc(silu_done, 1)

                def at(j):
                    act.wait_ge(aT_ps, j + 1)
                    act.activation(aT[:, 0:NA, :].rearrange("p k q -> p (k q)"), ps[:, 4, 0:NA * P], ACT.Copy).then_inc(aT_act, 1)

                xt(0, 0)
                silu(0, 0)
                xt(1, 1)
                with act.Fori(0, (nt - 1) // 2) as i:
                    at(2 * i)
                    silu(2 * i + 1, 1)
                    xt(2 * i + 2, 0)
                    at(2 * i + 1)
                    silu(2 * i + 2, 0)
                    xt(2 * i + 3, 1)
                at(nt - 1)

            @block.vector
            def _(dve):
                dve.memset(yo[:, 0, 0:1], 0.0).then_inc(a_ready, 2)
                dve.memset(yo[:, 0, 1:2], 0.0).then_inc(xT_sb, 1)
                dve.memset(yo[:, 0, 2:3], 0.0).then_inc(y_sb, 1)
                dve.memset(a[:], 0.0).then_inc(pad_zero, 1)
                dve.wait_ge(pad_zero, 1)

                def mul(j, u):
                    for n in range(2):
                        dve.wait_ge(silu_done, 2 * j + n + 1)
                        dve.wait_ge(u_ps, 2 * j + n + 1)
                        dve.tensor_tensor(a[:, u, n * half:(n + 1) * half], sg[:, n * half:(n + 1) * half], ps[:, 2 + n, 0:half],
                                          ALU.mult).then_inc(a_ready, 1)

                def at(j):
                    if FC > 4:
                        dve.wait_ge(aT_ps, j + 1)
                        dve.tensor_copy(aT[:, 4:FC, :].rearrange("p k q -> p (k q)"), ps[:, 5, 0:(FC - 4) * P]).then_inc(aT_dve, 1)

                def y(j, u, stores=None):
                    dve.wait_ge(y_ps, j + 1)
                    if stores is not None:
                        dve.wait_ge(y_st[u], stores)
                    dve.tensor_copy(yo[:, u, :], ps[:, 7, 0:HID]).then_inc(y_sb, 1)

                mul(0, 0)
                at(0)
                mul(1, 1)
                y(0, 0)
                at(1)
                mul(2, 0)
                y(1, 1)
                with dve.Fori(1, (nt - 1) // 2) as i:
                    at(2 * i)
                    mul(2 * i + 1, 1)
                    y(2 * i, 0, 16 * i)
                    at(2 * i + 1)
                    mul(2 * i + 2, 0)
                    y(2 * i + 1, 1, 16 * i)
                at(nt - 1)
                y(nt - 1, 0, 16 * ((nt - 1) // 2))

        if l == 0:
            return
        with ExitStack() as fc:
            t_ = lambda n, shape: fc.enter_context(nc.sbuf_tensor(f"c1_{n}", shape, F32))
            part_sems = Sems(nc, fc)
            r = lambda n: part_sems(f"c1_{n}")
            back = WayBack(t_, r, sb, 1)
            own_s, out_st = r("own"), r("out_st")
            ps = fc.enter_context(nc.psum_tensor("c1_ps", [P, 8, 512], F32))
            late = SharedExpert(nc, lambda n, shape: t_("s" + n, shape), lambda n: r("s" + n), (wg, wu, wd), sb["ident"], ps, keep,
                                EARLY, TILES - EARLY)
            block = fc.enter_context(nc.Block())

            @block.tensor
            def _(pe):
                late.tensor(pe)

            @block.scalar
            def _(act):
                late.scalar(act)

            @block.sync
            def _(sp):
                for t in range(0, TILES, 2):
                    sp.wait_ge(back.x_new, t + 2)
                    sp.dma_start(out[t * P:(t + 2) * P, :].rearrange("(t p) c -> p t c", p=P), sb["x"][:, t:t + 2, :]).then_inc(out_st, 16)
                sp.wait_ge(out_st, 16 * TILES // 2)

            @block.gpsimd
            def _(pool):
                back.gather(pool, ys)

            @block.vector
            def _(dve):
                own = Steps(dve, own_s)
                count = TILES - EARLY
                done = 0
                for k in range(count + 1):
                    if k < count:
                        late.mul(dve, k, k % 2)
                    if k > 0:
                        late.result(dve, k - 1)
                    until = min(2 * k + 2, (EARLY + k) // 2 * 2) if k < count else TILES
                    for t in range(done, until, 2):
                        if t >= EARLY:
                            dve.wait_ge(late.y_sb, t - EARLY + 2)
                        back.add(dve, own, t, keep[:, t:t + 2, :])
                    done = until


def program(nc, io, out):
    with ExitStack() as ctx:
        sb = {
            "x": ctx.enter_context(nc.sbuf_tensor("x_tok", [P, TILES, HID], F32)),
            "ident": ctx.enter_context(nc.sbuf_tensor("ident_sb", [P, P], F32)),
            "stats": ctx.enter_context(nc.sbuf_tensor("row_stats", [P, TILES, 6], F32)),
            "mv": ctx.enter_context(nc.sbuf_tensor("row_mv", [P, TILES, 2], F32)),
            "var": ctx.enter_context(nc.sbuf_tensor("row_var", [P, TILES], F32)),
            "root": ctx.enter_context(nc.sbuf_tensor("row_root", [P, TILES], F32)),
            "rstd": ctx.enter_context(nc.sbuf_tensor("row_rstd", [P, TILES], F32)),
            "pos": ctx.enter_context(nc.sbuf_tensor("list_rows", [P, 2, TILES], U32)),
            "prob": ctx.enter_context(nc.sbuf_tensor("list_weights", [P, 2, TILES], F32)),
            "shift": ctx.enter_context(nc.sbuf_tensor("row_shift", [P, TILES], F32)),
            "modb": ctx.enter_context(nc.sbuf_tensor("mixture_mod", [P, NBATCH, 2 * HID], F32)),
            "gb": ctx.enter_context(nc.sbuf_tensor("mixture_gate", [P, NBATCH, HID], F32)),
            "modT": ctx.enter_context(nc.sbuf_tensor("modT", [P, 2, 4, NBATCH], F32)),
        }
        modd = nc.dram_tensor("mod_rows", [2, NBATCH, 6 * HID], F32, kind="Internal").ap()
        xs = [nc.dram_tensor(f"xs{l}", [(NSPARSE + 1) * P, HID], F32, kind="Internal").ap() for l in range(2)]
        ys = [nc.dram_tensor(f"ys{l}", [NSPARSE * P, HID], F32, kind="Internal").ap() for l in range(2)]
        attention0(nc, io, sb, modd, xs)
        mixture(nc, io, sb, modd, 0, xs[0], ys[0], None)
        attention1(nc, io, sb, modd, ys[0])
        mixture(nc, io, sb, modd, 1, xs[1], ys[1], out)


def layout(i):
    f = np.float32
    a = {k: np.asarray(v) for k, v in i.items()}
    o = {}
    o["x"] = a["L0_attn_hidden_states"].reshape(TOK, HID)
    chunks = lambda w: np.ascontiguousarray(w.reshape(-1, P, w.shape[1]).transpose(1, 0, 2))
    o["cT"] = np.ascontiguousarray(np.stack([chunks(a[f"L{l}_c"].T) for l in range(2)], 1))
    o["wmod"] = np.ascontiguousarray(np.stack([chunks(a[f"L{l}_wmod"]) for l in range(2)], 1))
    o["ident"] = np.eye(P, dtype=f)
    cst = np.zeros((P, 2 * P + 96), f)
    cst[:, 0:P] = np.triu(np.ones((P, P), f), 1)
    cst[:, P:2 * P] = 1.0
    cst[:, 2 * P:2 * P + NE] = np.arange(NE, 0, -1)
    cst[:, 2 * P + 16:2 * P + 32] = np.arange(TILES) * P
    cst[:, 2 * P + 32:2 * P + 32 + NSPARSE] = np.arange(NSPARSE)
    o["cst"] = cst
    heads = lambda w: np.ascontiguousarray(w.reshape(NH, D0, -1).transpose(1, 0, 2))
    o["l0_wuq"], o["l0_wuk"], o["l0_wuv"] = (heads(a[f"L0_attn_W_{k}_w"]) for k in ("UQ", "UK", "UV"))
    o["l0_woT"] = heads(a["L0_attn_W_O_w"].T)
    o["l0_bup"] = np.ascontiguousarray(np.stack([a[f"L0_attn_W_{k}_b"].reshape(NH, D0).T for k in ("UQ", "UV")], 1))
    dq, dkv = a["L0_attn_W_DQ_w"].T, a["L0_attn_W_DKV_w"].T
    o["l0_wlat"] = chunks(np.concatenate([dq, dkv, dkv], 1))
    bl = np.zeros((P, 3), f)
    bl[:, 0] = a["L0_attn_W_DQ_b"][:P]
    bl[0:QC - P, 1] = a["L0_attn_W_DQ_b"][P:]
    bl[0:KVC, 2] = a["L0_attn_W_DKV_b"]
    bl[KVC:, 2] = a["L0_attn_W_DKV_b"]
    o["l0_blat"] = bl
    o["l0_bo"] = a["L0_attn_W_O_b"].reshape(1, HID)
    o["l0_wr"] = chunks(a["L0_ffn_router_w"].T)
    ffn = lambda w: np.ascontiguousarray(w.reshape(w.shape[0], HC, P, -1).transpose(2, 1, 0, 3))
    o["l0_wg"], o["l0_wu"] = (ffn(a[f"L0_ffn_{k}_w"].transpose(0, 2, 1)) for k in ("gate", "up"))
    wd = np.zeros((NE, F0C * P, HID), f)
    wd[:, 0:F0, :] = a["L0_ffn_down_w"].transpose(0, 2, 1)
    o["l0_wd"] = np.ascontiguousarray(wd.reshape(NE * F0C, P, HID).transpose(1, 0, 2))
    o["l1_wlat"] = chunks(np.concatenate([a["L1_attn_Wc"], a["L1_attn_Wckv"]], 1))
    o["l1_blat"] = np.concatenate([a["L1_attn_bc"], a["L1_attn_bckv"]]).reshape(P, 1)
    wqkv = np.zeros((P, 896), f)
    wqkv[0:64, 0:256], wqkv[0:64, 256:384] = a["L1_attn_Wcq"], a["L1_attn_Wqr"]
    wqkv[64:128, 384:640], wqkv[64:128, 640:896] = a["L1_attn_Wck"], a["L1_attn_Wv"]
    o["l1_wqkv"] = wqkv
    o["l1_wkr"] = chunks(a["L1_attn_Wkr"])
    o["l1_btok"] = np.concatenate([a[f"L1_attn_{k}"] for k in ("bcq", "bqr", "bkr", "bck", "bv")]).reshape(1, 1024)
    o["l1_wo"] = chunks(a["L1_attn_Wo"])
    o["l1_bo"] = a["L1_attn_bo"].reshape(1, HID)
    inv = (1.0 / 10000.0 ** (np.arange(0, DRH, 2, dtype=f) / DRH)).astype(f)
    fr = np.arange(SEQ, dtype=f)[:, None] * inv[None, :]
    cos, sin = np.cos(fr).astype(f), np.sin(fr).astype(f)
    tab = np.stack([np.concatenate([cos, cos], 1), np.concatenate([-sin, sin], 1)])
    o["l1_rope"] = np.ascontiguousarray(tab.reshape(2, TPB, P, DRH).transpose(2, 0, 1, 3))
    o["l1_wr"] = chunks(a["L1_ffn_gate_w"])
    gu = np.concatenate([a["L1_ffn_w_gate_up"], a["L1_ffn_shared_gate_up"][None]], 0)
    o["l1_wg"], o["l1_wu"] = ffn(gu[:, :, 0:F1]), ffn(gu[:, :, F1:])
    dn = np.concatenate([a["L1_ffn_w_down"], a["L1_ffn_shared_down"][None]], 0)
    o["l1_wd"] = np.ascontiguousarray(dn.reshape((NE + 1) * F1C, P, HID).transpose(1, 0, 2))
    return {k: np.ascontiguousarray(v, dtype=f) for k, v in o.items()}


def kernel(**inputs):
    import concourse.bacc as bacc
    from concourse.bass_utils import run_bass_kernel_spmd

    nc = bacc.Bacc("TRN2", target_bir_lowering=False, num_devices=1)
    arrays = layout(inputs)
    io = {k: nc.dram_tensor(f"in_{k}", v.shape, F32, kind="ExternalInput").ap() for k, v in arrays.items()}
    out = nc.dram_tensor("out_x", (TOK, HID), F32, kind="ExternalOutput").ap()
    program(nc, io, out)
    r = run_bass_kernel_spmd(nc, [{f"in_{k}": v for k, v in arrays.items()}], core_ids=[0])
    return r.results[0]["out_x"].reshape(NBATCH, SEQ, HID)
```
